# Optimizing a Trainium2 kernel written in Bass

```python
import numpy as np
import jax
import jax.numpy as jnp

def _softmax(x, axis=-1):
    return jax.nn.softmax(x, axis=axis)

def _gelu(x):
    return jax.nn.gelu(x, approximate=True)

def _silu(x):
    return jax.nn.silu(x)

def _sigmoid(x):
    return jax.nn.sigmoid(x)

def _layernorm(x, axis=-1, eps=1e-05):
    m = jnp.mean(x, axis=axis, keepdims=True)
    v = jnp.var(x, axis=axis, keepdims=True)
    return (x - m) / jnp.sqrt(v + eps)

def _scatter_add(tgt, idx, src, axis=0):
    return tgt.at[idx].add(src)

def _segment_sum(src, seg, n):
    return jax.ops.segment_sum(src, seg, n)
kernel_name = 'mk_adaln_d1_jaxref_r4_4073f2'

def setup_inputs(seed: int=0):
    np.random.seed(seed)
    _w = jnp.asarray

    def _L0_attn_setup():
        import jax, jax.numpy as jnp
        import numpy as np
        B, T, DM, H, D = (2, 1024, 256, 16, 64)
        HD = H * D
        PHASE_SCALE = 10.0

        def _multiscale_phasors(num_heads, head_dim):
            d = np.arange(head_dim, dtype=np.float32) / head_dim
            base = 10000.0 ** (-d)
            head_scale = 2.0 ** (-np.arange(num_heads, dtype=np.float32))
            return jnp.asarray(2.0 * np.pi * head_scale[:, None] * base[None, :], dtype=jnp.float32)

        def _holo_fused_step(v, binder, probe):
            mem = jnp.cumsum(v * binder, axis=1)
            t = v.shape[1]
            scale = jnp.sqrt(jnp.arange(1, t + 1, dtype=jnp.float32))[None, :, None, None]
            return jnp.real(mem * probe) / scale
        key = jax.random.key(seed)
        k0, k1, k2, k3 = jax.random.split(key, 4)
        x = jax.random.normal(k0, (B, T, DM), jnp.float32)
        Wk = jax.random.normal(k1, (DM, HD), jnp.float32) / np.float32(np.sqrt(DM))
        Wv = jax.random.normal(k2, (DM, HD), jnp.float32) / np.float32(np.sqrt(DM))
        Wo = jax.random.normal(k3, (HD, DM), jnp.float32) / np.float32(np.sqrt(HD))
        gate = jnp.full((H, 2), 0.5, jnp.float32)
        freqs = _multiscale_phasors(H, D)
        return {'x': x, 'Wk': Wk, 'Wv': Wv, 'Wo': Wo, 'gate': gate, 'freqs': freqs}
    _L0_attn_in = _L0_attn_setup()

    def _L0_ffn_setup():
        import math
        import jax, jax.numpy as jnp
        from jax import lax
        import numpy as np
        E = 16
        K = 2
        CF = 1.25
        key = jax.random.key(seed)
        k0, k1, k2, k3, k4 = jax.random.split(key, 5)
        B, S, D, H = (2, 512, 256, 256)
        scale = 0.02
        return {'x': jax.random.normal(k0, (B, S, D), dtype=jnp.float32), 'router_w': jax.random.normal(k1, (D, E), dtype=jnp.float32) * scale, 'gate_w': jax.random.normal(k2, (E, D, H), dtype=jnp.float32) * scale, 'up_w': jax.random.normal(k3, (E, D, H), dtype=jnp.float32) * scale, 'down_w': jax.random.normal(k4, (E, H, D), dtype=jnp.float32) * scale}
    _L0_ffn_in = _L0_ffn_setup()
    _L0_c = _w((lambda *s: np.random.randn(*s).astype(np.float32) * 0.05)(4, 256))
    _L0_wmod = _w((lambda *s: np.random.randn(*s).astype(np.float32) * 0.05)(256, 6 * 256) * 256 ** (-0.5))
    _d = {'L0_attn_x': _L0_attn_in['x'], 'L0_attn_Wk': _L0_attn_in['Wk'], 'L0_attn_Wv': _L0_attn_in['Wv'], 'L0_attn_Wo': _L0_attn_in['Wo'], 'L0_attn_gate': _L0_attn_in['gate'], 'L0_attn_freqs': _L0_attn_in['freqs'], 'L0_ffn_router_w': _L0_ffn_in['router_w'], 'L0_ffn_gate_w': _L0_ffn_in['gate_w'], 'L0_ffn_up_w': _L0_ffn_in['up_w'], 'L0_ffn_down_w': _L0_ffn_in['down_w'], 'L0_c': _L0_c, 'L0_wmod': _L0_wmod}
    _x0 = _d['L0_attn_x']
    _d['L0_attn_x'] = jax.random.normal(jax.random.fold_in(jax.random.key(seed), 1), (4, 1024, 256), dtype=_x0.dtype)
    del _x0
    return _d

def reference(L0_attn_x, L0_attn_Wk, L0_attn_Wv, L0_attn_Wo, L0_attn_gate, L0_attn_freqs, L0_ffn_router_w, L0_ffn_gate_w, L0_ffn_up_w, L0_ffn_down_w, L0_c, L0_wmod):

    def _L0_attn_ref(x, Wk, Wv, Wo, gate, freqs):
        import jax, jax.numpy as jnp
        import numpy as np
        B, T, DM, H, D = (2, 1024, 256, 16, 64)
        HD = H * D
        PHASE_SCALE = 10.0

        def _multiscale_phasors(num_heads, head_dim):
            d = np.arange(head_dim, dtype=np.float32) / head_dim
            base = 10000.0 ** (-d)
            head_scale = 2.0 ** (-np.arange(num_heads, dtype=np.float32))
            return jnp.asarray(2.0 * np.pi * head_scale[:, None] * base[None, :], dtype=jnp.float32)

        def _holo_fused_step(v, binder, probe):
            mem = jnp.cumsum(v * binder, axis=1)
            t = v.shape[1]
            scale = jnp.sqrt(jnp.arange(1, t + 1, dtype=jnp.float32))[None, :, None, None]
            return jnp.real(mem * probe) / scale
        Bb, Tt, _ = x.shape
        k_real = (x @ Wk).reshape(Bb, Tt, H, D)
        v = (x @ Wv).reshape(Bb, Tt, H, D).astype(jnp.complex64)
        k = jnp.exp(1j * (k_real * PHASE_SCALE))
        t = jnp.arange(Tt, dtype=jnp.float32)
        rotors = jnp.exp(1j * (t[:, None, None] * freqs))[None]
        out_pos = _holo_fused_step(v, rotors, jnp.conj(rotors))
        k_shifted = jnp.roll(k, 1, axis=1).at[:, 0].set(0.0)
        out_assoc = _holo_fused_step(v, jnp.conj(k_shifted), k)
        g_pos = gate[:, 0][None, None, :, None]
        g_assoc = gate[:, 1][None, None, :, None]
        out = out_pos * g_pos + out_assoc * g_assoc
        return out.reshape(Bb, Tt, HD) @ Wo

    def _L0_ffn_ref(x, router_w, gate_w, up_w, down_w):
        import math
        import jax, jax.numpy as jnp
        from jax import lax
        import numpy as np
        E = 16
        K = 2
        CF = 1.25
        B, S, D = x.shape
        xf = x.reshape(-1, D)
        T = B * S
        capacity = max(1, math.ceil(T * K / E * CF))
        Cbuf = K * capacity
        logits = xf @ router_w
        probs = jax.nn.softmax(logits, axis=-1)
        w, idx = lax.top_k(probs, K)
        oh = jax.nn.one_hot(idx, E, dtype=w.dtype)
        rank = jnp.cumsum(oh, axis=0) - oh
        myrank = jnp.sum(rank * oh, axis=-1)
        keep = myrank < capacity
        w = jnp.where(keep, w, 0.0)
        flat_e = idx.reshape(-1)
        flat_w = w.reshape(-1)
        keep_f = keep.reshape(-1)
        tok = jnp.repeat(jnp.arange(T, dtype=jnp.int32), K)
        ohk = jax.nn.one_hot(flat_e, E, dtype=jnp.int32) * keep_f[:, None].astype(jnp.int32)
        pos = jnp.cumsum(ohk, axis=0) - ohk
        slot = jnp.sum(pos * ohk, axis=-1)
        e_idx = jnp.where(keep_f, flat_e, E)
        dispatch = jnp.full((E + 1, Cbuf), T, dtype=jnp.int32).at[e_idx, slot].set(tok)
        wbuf = jnp.zeros((E + 1, Cbuf), dtype=w.dtype).at[e_idx, slot].set(flat_w)
        dispatch = dispatch[:E]
        wbuf = wbuf[:E]
        x_pad = jnp.concatenate([xf, jnp.zeros((1, D), xf.dtype)], axis=0)
        xe = x_pad[dispatch]
        gate = jnp.einsum('ecd,edh->ech', xe, gate_w)
        up = jnp.einsum('ecd,edh->ech', xe, up_w)
        hidden = jax.nn.silu(gate) * up
        out = jnp.einsum('ech,ehd->ecd', hidden, down_w)
        out = out * wbuf[:, :, None]
        combined = jnp.zeros((T + 1, D), dtype=xf.dtype).at[dispatch.reshape(-1)].add(out.reshape(-1, D))
        return combined[:T].reshape(B, S, D)
    x = L0_attn_x
    mod = (_silu(L0_c) @ L0_wmod).reshape(L0_c.shape[0], 6, 1, -1)
    sa, ca, ga, sb, cb, gb = (mod[:, 0], mod[:, 1], mod[:, 2], mod[:, 3], mod[:, 4], mod[:, 5])
    ga = (2 * (ga >= 0) - 1) * jnp.maximum(jnp.abs(ga), 0.25)
    gb = (2 * (gb >= 0) - 1) * jnp.maximum(jnp.abs(gb), 0.25)
    h = _layernorm(x, axis=-1) * (1 + ca) + sa
    x = x + ga * _L0_attn_ref(h, L0_attn_Wk, L0_attn_Wv, L0_attn_Wo, L0_attn_gate, L0_attn_freqs)
    h = _layernorm(x, axis=-1) * (1 + cb) + sb
    x = x + gb * _L0_ffn_ref(h, L0_ffn_router_w, L0_ffn_gate_w, L0_ffn_up_w, L0_ffn_down_w)
    return x

_drawn_inputs = setup_inputs


def setup_inputs(seed=0):
    import zlib

    import numpy as np

    out = dict(_drawn_inputs(seed))
    spreads = {'L0_attn_gate': (0.5, 0.592)}
    factors = {'L0_ffn_router_w': 8.0, 'L0_ffn_gate_w': 8.0, 'L0_ffn_up_w': 8.0, 'L0_ffn_down_w': 8.0}
    for name, (base, spread) in spreads.items():
        noise = np.random.default_rng([zlib.crc32(name.encode()), seed]).standard_normal(out[name].shape)
        drawn = base * np.exp(spread * noise) if base else spread * noise
        out[name] = jnp.asarray(drawn.astype(out[name].dtype))
    for name, factor in factors.items():
        out[name] = (out[name] * factor).astype(out[name].dtype)
    return out
```

```python
import concourse.bass as bass
from concourse import mybir
from contextlib import ExitStack
import math
import numpy as np


def adaln_block(nc, x, wk_d, wv_d, wo_d, gate_d, freqs_d, router_d, egate_d, eup_d, edown_d, c_d, wmod_d, out):
    fp32, i32, bf16 = mybir.dt.float32, mybir.dt.int32, mybir.dt.bfloat16
    ALU, ACT, AX = mybir.AluOpType, mybir.ActivationFunctionType, mybir.AxisListType
    ds = bass.ds

    B, T, D = x.shape
    P = 128
    H, HD = freqs_d.shape
    CH = H * HD
    CB = CH // P
    WIN = 512
    NW = T // WIN
    Q = WIN // P
    KT = D // P
    NG = NW * B
    NU = NG * CB
    N = B * T
    NT = N // P
    TB = T // P
    E = router_d.shape[1]
    EH = egate_d.shape[2]
    TOPK = 2
    CAP = max(1, math.ceil(N * TOPK / E * 1.25))
    NBLK = -(-(N * TOPK // P + E) // 4) * 4
    assert KT == 2 and EH == 2 * P and NBLK <= P and NG == 8 and CB % 2 == 0
    PHASE = 10.0
    TWO_PI = 2.0 * math.pi
    TURN = float(np.nextafter(np.float32(TWO_PI), np.float32(0)))
    HALF_PI = float(np.float32(math.pi / 2))
    PI = float(np.nextafter(np.float32(math.pi), np.float32(0)))
    MAGIC = 12582912.0
    C1 = 6.28125
    C2 = float(np.float32(TWO_PI - C1))
    EPS = 1e-5
    NEG = -3.0e38

    x_v = x.rearrange("b (n p) d -> p (b n) d", p=P)
    out_v = out.rearrange("b (n p) d -> p (b n) d", p=P)
    x2_d = nc.dram_tensor("x2_scratch", (N, D), fp32, kind="Internal").ap()
    h2_d = nc.dram_tensor("h2_scratch", (N, D), fp32, kind="Internal").ap()
    y_d = nc.dram_tensor("y_scratch", (NBLK * P, D), fp32, kind="Internal").ap()
    x2_v = x2_d.rearrange("(n p) d -> p n d", p=P)
    h2_v = h2_d.rearrange("(n p) d -> p n d", p=P)
    y_v = y_d.rearrange("(n p) d -> p n d", p=P)

    ctx = ExitStack()
    with ctx:
        def sb(name, shape, dt=fp32):
            return ctx.enter_context(nc.sbuf_tensor(name, shape, dt))

        def sem(name):
            return ctx.enter_context(nc.semaphore(name))

        egu = sb("egu", [P, E * KT * 2 * EH])
        egu_v = egu[:, :].rearrange("p (e k n) -> p e k n", e=E, k=KT)
        LATE = 4
        pr_flat = egu[:, (E - LATE) * KT * 2 * EH:]
        prod = pr_flat.rearrange("p (s r t) -> p s r t", s=2, r=4)
        wmod = pr_flat[:, 0:KT * 6 * D].rearrange("p (k n) -> p k n", k=KT)
        csb = pr_flat[:, KT * 6 * D:KT * 6 * D + KT * B * P].rearrange("p (k b m) -> p k b m", k=KT, b=B)
        tab_flat = sb("rotor_tables", [P, CB * 2 * WIN])
        tab = tab_flat[:, :].rearrange("p (c r t) -> p c r t", c=CB, r=2)
        edn_v = tab_flat[:, :].rearrange("p (e k n) -> p e k n", e=E, k=KT)
        wk = sb("wk", [P, KT, CH])
        wv = sb("wv", [P, KT, CH])
        wo = sb("wo", [P, CB, D])
        modr = sb("mod_rows", [P, B, 4, D])
        GA, SB_, CB1, GB = range(4)
        modc = sb("mod_cols", [P, 2 * KT, B])
        trow = sb("t_row", [P, T])
        trig = sb("trig", [P, 2, 2, WIN + 1])
        vg = sb("v_gated", [P, 2, 2, WIN])
        ssum = sb("pair_sums", [P, 2, WIN])
        o_t = sb("mixed", [P, 2, WIN])
        t_t = sb("rounded_turns", [P, WIN])
        r_t = sb("turns", [P, WIN])
        a_t = sb("abs_turns", [P, WIN])
        phi = sb("phi", [P, WIN])
        nphi = sb("nphi", [P, WIN])
        xa = sb("xa", [P, Q, D])
        xr = sb("xr", [P, Q, D])
        h2 = sb("h2", [P, Q, D])
        hT = sb("hT", [P, KT, WIN])
        h2T = sb("h2T", [P, KT, WIN])
        rw = sb("router_w", [P, KT, E])
        gcol = sb("gate_cols", [P, CB, 2])
        fcol = sb("freq_cols", [P, CB])
        cT = sb("cT", [P, KT, B])
        csT = sb("csT", [P, KT, B])
        ident = sb("ident", [P, P])
        tcarry = sb("trig_carry", [P, B, CB, 2])
        scarry = sb("scan_carry", [P, B, CB, 4])
        one = sb("one", [P, 1])
        spare = sb("spare", [P, 8])
        mhalf = sb("minus_half", [P, TB])
        bnst = sb("bn_stats", [P, Q, 6])
        mv1 = sb("mean_var1", [P, Q, 2])
        mv2 = sb("mean_var2", [P, Q, 2])
        ve1 = sb("var_eps1", [P, Q])
        ve2 = sb("var_eps2", [P, Q])
        rs1 = sb("rstd1", [P, Q])
        rs2 = sb("rstd2", [P, Q])
        isq = sb("inv_sqrt_t", [P, TB])
        tcol = sb("t_col", [P, TB])
        logits = sb("logits", [P, NT, E])
        NE = NT * E
        vf = vg[:, :, :, :].rearrange("p a b t -> p (a b t)")
        oh = vf[:, 0:2 * NE].rearrange("p (k n e) -> p k n e", k=2, n=NT)
        eqt = vf[:, 2 * NE:3 * NE].rearrange("p (n e) -> p n e", n=NT)
        lmask = vf[:, 3 * NE:4 * NE].rearrange("p (n e) -> p n e", n=NT)
        tf = trig[:, :, :, :].rearrange("p a b t -> p (a b t)")
        tot = tf[:, 0:2 * NE].rearrange("p (k e n) -> p k e n", k=2, e=E)
        incl = tf[:, 2 * NE:4 * NE].rearrange("p (k e n) -> p k e n", k=2, e=E)
        rank = ssum[:, :, :].rearrange("p k (n e) -> p k n e", n=NT)
        segm = o_t[:, :, :].rearrange("p k (e n) -> p k e n", e=E)
        ohb = t_t[:, :].bitcast(bf16).rearrange("p (k m) -> p k m", k=2)
        expo = r_t[:, :].rearrange("p (n e) -> p n e", n=NT)
        iota_p = a_t[:, 0:P]
        triu = a_t[:, P:P + P // 2].bitcast(bf16)
        onesb = a_t[:, P + P // 2:2 * P].bitcast(bf16)
        e16 = a_t[:, 2 * P:2 * P + E]
        blk_hot = phi[:, :].rearrange("p (s m) -> p s m", s=4)
        pos_hot = nphi[:, :].rearrange("p (s m) -> p s m", s=4)
        hx = h2[:, :, :].rearrange("p q d -> p (q d)")
        m1 = sb("top_logit", [P, 2, NT])
        first = sb("first_index", [P, NT])
        zsum = sb("z_sum", [P, NT])
        wgt = sb("weights", [P, 2, NT])
        rsel = sb("ranks", [P, 2, NT])
        keep = sb("keep", [P, 2, NT])
        slot = sb("slots", [P, 2, NT])
        smap = sb("slots_mapped", [P, 2, NT])
        sloti = sb("slots_int", [P, 2, NT], i32)
        gsi = sb("gather_slots", [P, NT, 2], i32)
        posi = sb("pos_int", [P, 2, NT], i32)
        posf = sb("pos_f", [P, 2, NT])
        blkf = sb("blk_f", [P, 2, NT])
        tokf = sb("token_ids", [P, NT])
        kept = sb("kept", [P, 2, E])
        nexp = sb("n_expert", [P, E])
        nexpi = sb("n_expert_int", [P, E], i32)
        nblkf = sb("n_blocks", [P, E])
        bend = sb("block_end", [P, E])
        aoff = sb("slot_offsets", [P, 2, E])
        eblk = sb("expert_of_block", [P, P])
        eblki = sb("expert_of_block_int", [P, P], i32)
        mapi = sb("slot_tokens", [P, P], i32)
        idxc = sb("gather_index", [P, 4, 2], i32)
        xg = xa
        xgT = hT[:, :, :].rearrange("p k (s m) -> p k s m", s=4)
        hidT = h2T[:, :, :].rearrange("p k (s m) -> p k s m", s=4)
        sg = ssum[:, :, 0:EH]
        hid = o_t[:, :, 0:EH]
        ysb = xr
        y0 = vf[:, 0:4 * D].rearrange("p (s d) -> p s d", s=4)
        y1 = vf[:, 4 * D:8 * D].rearrange("p (s d) -> p s d", s=4)
        xf = tf[:, 0:4 * D].rearrange("p (s d) -> p s d", s=4)

        ps = ctx.enter_context(nc.psum_tensor("ps", [P, 8, 512], fp32))
        U, V, WO, TP, MISC = 0, 2, 4, 6, 7

        def S(names):
            return [sem(n) for n in names.split()]

        (c_in, wmod_in, wk_in, wv_in, wo_in, small_in, xa_in, xr_in, egu_in, elate_in, x2_out, h2_out) = S(
            "c_in wmod_in wk_in wv_in wo_in small_in xa_in xr_in egu_in elate_in x2_out h2_out")
        (ident_done, iota_done, pc_chain, silu_done, csb_done, modc_mm, modr_mm, modc_done, modr_copied, modr_done,
         wk_scaled, isq_done) = S(
            "ident_done iota_done pc_chain silu_done csb_done modc_mm modr_mm modc_done modr_copied modr_done wk_scaled isq_done")
        (var1_done, rstd1_done, xn_done, tp1_done, hT_done, k_done, v_done, t_done, r_done, abs_done, sin_done, trig_done,
         vcopy_done) = S(
            "var1_done rstd1_done xn_done tp1_done hT_done k_done v_done t_done r_done abs_done sin_done trig_done vcopy_done")
        (phi_done, nphi_mid, nphi_done, phir_mid, phir_done, phia_done, tab_done) = S(
            "phi_done nphi_mid nphi_done phir_mid phir_done phia_done tab_done")
        (dassoc_done, sassoc_done, dpos_done, spos_done, carry_done, fassoc_done, fpos_done, pair_done, mixed_done, wo_done) = S(
            "dassoc_done sassoc_done dpos_done spos_done carry_done fassoc_done fpos_done pair_done mixed_done wo_done")
        (wo_read, x2_done, var2_done, rstd2_done, h2n_done, h2c_done, h2_done, tp2_done, h2T_done, lg_done, lg_copied, ln1_chain, ln2_chain) = S(
            "wo_read x2_done var2_done rstd2_done h2n_done h2c_done h2_done tp2_done h2T_done lg_done lg_copied ln1_chain ln2_chain")
        (rt, rt_iota, rt_onehot, rt_rank, rt_exp_in, rt_exp, hot_done, map_mm, map_done, exps_done) = S(
            "rt rt_iota rt_onehot rt_rank rt_exp_in rt_exp hot_done map_mm map_done exps_done")
        gath = [sem(f"rows_gathered{s}") for s in range(4)]
        ystor = [sem(f"y_stored{s}") for s in range(4)]
        yg = [sem(f"y_gathered{s}") for s in range(4)]
        xf_in = [sem(f"x2_back{s}") for s in range(4)]
        ostor = [sem(f"out_stored{s}") for s in range(4)]
        (idx_done, bt_done, bxT_done, bgu_done, bsilu_done, bhid_done, bht_done, bhT_done, by_done, by_copied) = S(
            "idx_done bt_done bxT_done bgu_done bsilu_done bhid_done bht_done bhT_done by_done by_copied")
        carried = sem("carried")
        (cidx_done, cw0_done, cw1_done, cgb_done, csum_done) = S("cidx_done cw0_done cw1_done cgb_done csum_done")

        block = ctx.enter_context(nc.Block())

        def wait(eng, s, n):
            if not (isinstance(n, int) and n <= 0):
                eng.wait_ge(s, n)

        def apart(eng, n):
            if not isinstance(n, int):
                if eng is nc.vector:
                    nc.vector.memset(spare[:, 0:1], 0.0)
                else:
                    nc.scalar.activation(spare[:, 2:3], one[:, 0:1], ACT.Copy)

        def bodies(eng, body):
            for w in range(NW):
                body(w, 0, w - 1 if w else None, B - 1)
                with eng.Fori(1, B) as b:
                    body(w, b, w, b - 1)

        @block.sync
        def _(sp):
            sp.dma_start(cT[:, 0, :], c_d[:, 0:P].rearrange("b p -> p b"), allow_slow_non_contiguous=True).then_inc(c_in, 16)
            sp.dma_start(cT[:, 1, :], c_d[:, P:2 * P].rearrange("b p -> p b"), allow_slow_non_contiguous=True).then_inc(c_in, 16)
            sp.dma_start(wmod, wmod_d.rearrange("(k p) n -> p k n", p=P)).then_inc(wmod_in, 16)

            def body(w, b, wp, bp):
                g = w * B + b
                wait(sp, tp1_done, KT * g)
                sp.dma_start(xa[:, :, :], x_v[:, ds(b * TB + w * Q, Q), :]).then_inc(xa_in, 16)
                if isinstance(b, int) and w == 0:
                    sp.dma_start(wk[:, :, :], wk_d.rearrange("(k p) n -> p k n", p=P)).then_inc(wk_in, 16)
                    sp.dma_start(wv[:, :, :], wv_d.rearrange("(k p) n -> p k n", p=P)).then_inc(wv_in, 16)
                    for hh in range(P // HD):
                        sp.dma_start(gcol[hh * HD:(hh + 1) * HD, :, :],
                                     gate_d.rearrange("(c h) g -> h c g", h=P // HD)[hh, :, :].partition_broadcast(HD)
                                     ).then_inc(small_in, 16)
                        sp.dma_start(fcol[hh * HD:(hh + 1) * HD, :],
                                     freqs_d.rearrange("(c h) d -> h d c", h=P // HD)[hh, :, :],
                                     allow_slow_non_contiguous=True).then_inc(small_in, 16)
                    sp.dma_start(rw[:, :, :], router_d.rearrange("(k p) n -> p k n", p=P)).then_inc(small_in, 16)
                    sp.dma_start(wo[:, :, :], wo_d.rearrange("(c p) n -> p c n", p=P)).then_inc(wo_in, 16)
                    for e in range(E - LATE):
                        for half, src in enumerate((egate_d, eup_d)):
                            sp.dma_start(egu_v[:, e, :, half * EH:(half + 1) * EH],
                                         src[e, :, :].rearrange("(k p) n -> p k n", p=P)).then_inc(egu_in, 16)
                if wp is not None:
                    wait(sp, x2_done, g)
                    sp.dma_start(x2_v[:, ds(bp * TB + wp * Q, Q), :], xr[:, :, :]).then_inc(x2_out, 16)
                    wait(sp, h2_done, g)
                    sp.dma_start(h2_v[:, ds(bp * TB + wp * Q, Q), :], h2[:, :, :]).then_inc(h2_out, 16)
                    wait(sp, x2_out, 16 * g)
                    wait(sp, h2_out, 16 * g)
                sp.dma_start(xr[:, :, :], x_v[:, ds(b * TB + w * Q, Q), :]).then_inc(xr_in, 16)

            bodies(sp, body)
            sp.wait_ge(x2_done, NG)
            sp.dma_start(x2_v[:, ds((B - 1) * TB + (NW - 1) * Q, Q), :], xr[:, :, :]).then_inc(x2_out, 16)
            sp.wait_ge(h2_done, NG)
            sp.dma_start(h2_v[:, ds((B - 1) * TB + (NW - 1) * Q, Q), :], h2[:, :, :]).then_inc(h2_out, 16)
            sp.wait_ge(pair_done, NU)
            sp.wait_ge(fpos_done, NU)
            for e in range(E - LATE, E):
                for half, src in enumerate((egate_d, eup_d)):
                    sp.dma_start(egu_v[:, e, :, half * EH:(half + 1) * EH],
                                 src[e, :, :].rearrange("(k p) n -> p k n", p=P)).then_inc(elate_in, 16)
            for e in range(0, E, 4):
                sp.dma_start(edn_v[:, e:e + 4, :, :],
                             edown_d[e:e + 4, :, :].rearrange("e (k p) n -> p e k n", p=P)).then_inc(elate_in, 16)
            with sp.Fori(0, NBLK // 4) as i:
                for s in range(4):
                    sp.wait_ge(by_copied, i * 4 + s + 1)
                    sp.dma_start(y_v[:, ds(i * 4 + s, 1), :], ysb[:, s:s + 1, :]).then_inc(ystor[s], 16)
            sp.wait_ge(x2_out, 16 * NG)
            def last_sums(i, first):
                for s in range(4):
                    if not first:
                        sp.wait_ge(ostor[s], i * 16)
                    sp.dma_start(xf[:, s:s + 1, :], x2_v[:, ds(i * 4 + s, 1), :]).then_inc(xf_in[s], 16)
                for s in range(4):
                    sp.wait_ge(csum_done, i * 4 + s + 1)
                    sp.dma_start(out_v[:, ds(i * 4 + s, 1), :], xf[:, s:s + 1, :]).then_inc(ostor[s], 16)

            last_sums(0, True)
            with sp.Fori(1, NT // 4) as i:
                last_sums(i, False)
            for s in range(4):
                sp.wait_ge(ostor[s], 16 * (NT // 4))

        @block.tensor
        def _(pe):
            pe.wait_ge(silu_done, 1)
            pe.wait_ge(wmod_in, 16)
            for j in range(2 * KT):
                for k in range(KT):
                    last = nc.tensor.matmul(ps[:, MISC, j * B:(j + 1) * B], wmod[:, k, j * P:(j + 1) * P], csT[:, k, :],
                                            start=(k == 0), stop=(k == KT - 1))
            last.then_inc(modc_mm, 1)
            pe.wait_ge(csb_done, 1)
            for b in range(B):
                pair = U if b % 2 == 0 else V
                if b >= 2:
                    pe.wait_ge(modr_copied, b - 1)
                for n in range(2):
                    for k in range(KT):
                        last = nc.tensor.matmul(ps[:, pair + n, :], csb[:, k, b, :],
                                                wmod[:, k, 2 * D + n * 512:2 * D + (n + 1) * 512],
                                                start=(k == 0), stop=(k == KT - 1))
                last.then_inc(modr_mm, 1)
            pe.wait_ge(ident_done, 2)
            pe.wait_ge(small_in, 80)

            def project_out(u, cb):
                wait(pe, mixed_done, u + 1)
                for q in range(Q):
                    last = nc.tensor.matmul(ps[:, WO + q // 2, (q % 2) * D:(q % 2 + 1) * D],
                                            o_t[:, cb % 2, q * P:(q + 1) * P], wo[:, cb, :],
                                            start=(cb == 0 and q % 2 == 0), stop=(cb == CB - 1), skip_group_check=True)
                last.then_inc(wo_done, 1)

            def transposes(src, k, done):
                for q in range(Q):
                    last = nc.tensor.transpose(ps[:, TP, q * P:(q + 1) * P], src[:, q, k * P:(k + 1) * P], ident[:, :])
                last.then_inc(done, 1)

            def router(g):
                wait(pe, h2_done, g + 1)
                for k in range(KT):
                    if k == 0:
                        wait(pe, hT_done, KT * (g + 2) if not isinstance(g, int) or g < NG - 1 else KT * NG)
                    else:
                        wait(pe, h2T_done, KT * g + 1)
                    transposes(h2, k, tp2_done)
                wait(pe, h2T_done, KT * (g + 1))
                for q in range(Q):
                    for k in range(KT):
                        last = nc.tensor.matmul(ps[:, MISC, q * E:(q + 1) * E], h2T[:, k, q * P:(q + 1) * P], rw[:, k, :],
                                                start=(k == 0), stop=(k == KT - 1))
                last.then_inc(lg_done, 1)

            def body(w, b, wp, bp):
                g = w * B + b
                u0 = g * CB
                wait(pe, xn_done, g + 1)
                for k in range(KT):
                    if k:
                        wait(pe, hT_done, KT * g + k)
                    transposes(xa, k, tp1_done)
                wait(pe, hT_done, KT * (g + 1))
                if isinstance(b, int) and w == 0:
                    pe.wait_ge(wk_scaled, 1)
                    pe.wait_ge(wv_in, 16)
                    pe.wait_ge(wo_in, 16)
                    pe.wait_ge(modr_copied, B)
                for cb in range(CB):
                    u = u0 + cb
                    wait(pe, r_done, u - 1)
                    for k in range(KT):
                        last = nc.tensor.matmul(ps[:, U + cb % 2, :], wk[:, k, cb * P:(cb + 1) * P], hT[:, k, :],
                                                start=(k == 0), stop=(k == KT - 1))
                    last.then_inc(k_done, 1)
                    wait(pe, vcopy_done, u - 1)
                    for k in range(KT):
                        last = nc.tensor.matmul(ps[:, V + cb % 2, :], wv[:, k, cb * P:(cb + 1) * P], hT[:, k, :],
                                                start=(k == 0), stop=(k == KT - 1))
                    last.then_inc(v_done, 1)
                    lag = 3
                    if wp is not None or cb >= lag:
                        if cb == lag:
                            wait(pe, wo_read, g)
                        project_out(u - lag, (cb - lag) % CB)
                    if cb == 5 and wp is not None:
                        router(g - 1)

            bodies(pe, body)
            for cb in range(CB - 3, CB):
                project_out(NU - CB + cb, cb)
            router(NG - 1)

            pe.wait_ge(rt_iota, 4)
            pe.wait_ge(rt_onehot, 1)
            for k in range(2):
                nc.tensor.matmul(ps[:, 2 * k, :], triu, ohb[:, k, :], start=True, stop=True)
                last = nc.tensor.matmul(ps[:, 2 * k + 1, :], onesb, ohb[:, k, :], start=True, stop=True)
            last.then_inc(rt_rank, 1)
            def map_four(i, first):
                for s in range(4):
                    pe.wait_ge(hot_done, i * 4 + s + 1)
                    nc.tensor.matmul(ps[:, MISC, 0:P], pos_hot[:, s, :], blk_hot[:, s, :], start=(first and s == 0),
                                     stop=True, skip_group_check=True).then_inc(map_mm, 1)

            map_four(0, True)
            with pe.Fori(1, NT // 2) as i:
                map_four(i, False)

            pe.wait_ge(map_done, 1)
            pe.wait_ge(exps_done, 1)
            pe.wait_ge(egu_in, 16 * 2 * (E - LATE))
            pe.wait_ge(elate_in, 16 * (2 * LATE + 4))

            def step(j, s, lo=0, hi=3):
                if lo <= 0 <= hi:
                    pe.wait_ge(gath[s % 4], 16 * (j // 4 + 1) if isinstance(j, int) else 16 * ((j - s % 4) // 4) + 16)
                    wait(pe, bxT_done, j - 1)
                    for k in range(KT):
                        last = nc.tensor.transpose(ps[:, 0 + s % 2, k * P:(k + 1) * P], xg[:, s % 4, k * P:(k + 1) * P], ident[:, :])
                    last.then_inc(bt_done, 1)
                if lo <= 1 <= hi:
                    e = pe.value_load(eblki[0:1, ds(j - 1, 1)], min_val=0, max_val=E - 1)
                    wait(pe, bxT_done, j)
                    wait(pe, bhid_done, j - 2)
                    for k in range(KT):
                        last = nc.tensor.matmul(ps[:, 2 + (s - 1) % 2, :], xgT[:, k, (s - 1) % 4, :], egu_v[:, ds(e, 1), k, :],
                                                start=(k == 0), stop=(k == KT - 1))
                    last.then_inc(bgu_done, 1)
                if lo <= 2 <= hi:
                    wait(pe, bhid_done, j - 1)
                    wait(pe, bhT_done, j - 3)
                    for k in range(KT):
                        last = nc.tensor.transpose(ps[:, 4 + s % 2, k * P:(k + 1) * P], hid[:, s % 2, k * P:(k + 1) * P], ident[:, :])
                    last.then_inc(bht_done, 1)
                if lo <= 3 <= hi:
                    e = pe.value_load(eblki[0:1, ds(j - 3, 1)], min_val=0, max_val=E - 1)
                    wait(pe, bhT_done, j - 2)
                    wait(pe, by_copied, j - 4)
                    for k in range(KT):
                        last = nc.tensor.matmul(ps[:, 6 + (s - 3) % 2, 0:D], hidT[:, k, (s - 3) % 4, :], edn_v[:, ds(e, 1), k, :],
                                                start=(k == 0), stop=(k == KT - 1))
                    last.then_inc(by_done, 1)

            for j in range(8):
                step(j, j % 4, 0, j)
            with pe.Fori(2, NBLK // 4) as i:
                for s in range(4):
                    step(i * 4 + s, s)
            for j in range(3):
                step(NBLK + j, j, j + 1, 3)

        @block.scalar
        def _(act):
            act.wait_ge(c_in, 32)
            act.activation(csT[:, :, :], cT[:, :, :], ACT.Silu).then_inc(silu_done, 1)
            for b in range(B):
                act.wait_ge(modr_mm, b + 1)
                pair = U if b % 2 == 0 else V
                act.activation(modr[:, b, :, :].rearrange("p s d -> p (s d)"),
                               ps[:, pair:pair + 2, :].rearrange("p a n -> p (a n)"), ACT.Copy).then_inc(modr_copied, 1)
            act.wait_ge(small_in, 80)
            act.wait_ge(modc_done, 1)
            act.wait_ge(iota_done, 1)

            def copy_h2T(g):
                for k in range(KT):
                    wait(act, tp2_done, KT * g + k + 1)
                    act.activation(h2T[:, k, :], ps[:, TP, :], ACT.Copy).then_inc(h2T_done, 1)

            def body(w, b, wp, bp):
                g = w * B + b
                u0 = g * CB
                tables = isinstance(b, int)
                for k in range(KT):
                    wait(act, tp1_done, KT * g + k + 1)
                    wait(act, v_done, u0)
                    apart(act, b)
                    act.activation(hT[:, k, :], ps[:, TP, :], ACT.Identity, scale=modc[:, KT + k, ds(b, 1)],
                                   bias=modc[:, k, ds(b, 1)]).then_inc(hT_done, 1)
                for cb in range(CB):
                    u = u0 + cb
                    s = cb % 2
                    if tables:
                        m = w * CB + cb
                        wait(act, tab_done, m)
                        act.activation(phi[:, :], trow[:, w * WIN:(w + 1) * WIN], ACT.Copy,
                                       scale=fcol[:, cb:cb + 1]).then_inc(phi_done, 1)
                        act.wait_ge(phi_done, m + 1)
                        act.activation(nphi[:, :], phi[:, :], ACT.Copy, scale=1.0 / TWO_PI, bias=MAGIC).then_inc(nphi_mid, 1)
                        act.wait_ge(nphi_mid, m + 1)
                        act.activation(nphi[:, :], nphi[:, :], ACT.Copy, bias=-MAGIC).then_inc(nphi_done, 1)
                    wait(act, k_done, u + 1)
                    wait(act, r_done, u)
                    act.activation(t_t[:, :], ps[:, U + s, :], ACT.Copy, bias=MAGIC).then_inc(t_done, 1)
                    wait(act, v_done, u + 1)
                    wait(act, dpos_done, u - 1)
                    wait(act, dassoc_done, u - 1)
                    wait(act, trig_done, u)
                    act.activation(vg[:, s, 0, :], ps[:, V + s, :], ACT.Copy, scale=gcol[:, cb, 0:1])
                    lb, lc = (b, cb - 1) if cb else (bp, CB - 1)
                    if w == 0 and (cb or wp is not None):
                        act.activation(tcarry[:, ds(lb, 1), lc, :].rearrange("p a r -> p r a"),
                                       trig[:, 1 - s, :, WIN:WIN + 1], ACT.Copy)
                    if w == 1 and tables and cb == 0:
                        act.activation(tcarry[:, B - 1:B, CB - 1, :].rearrange("p a r -> p r a"),
                                       trig[:, 1 - s, :, WIN:WIN + 1], ACT.Copy)
                    act.activation(vg[:, s, 1, :], ps[:, V + s, :], ACT.Copy, scale=gcol[:, cb, 1:2]).then_inc(vcopy_done, 1)
                    if tables:
                        wait(act, phir_done, m + 1)
                        act.activation(nphi[:, :], phi[:, :], ACT.Abs).then_inc(phia_done, 1)
                        wait(act, fpos_done, u - CB + 1 if w else 0)
                        act.activation(tab[:, cb, 1, :], phi[:, :], ACT.Sin)
                        act.wait_ge(phia_done, m + 1)
                        act.activation(tab[:, cb, 0, :], nphi[:, :], ACT.Sin, scale=-1.0, bias=HALF_PI).then_inc(tab_done, 1)
                    wait(act, r_done, u + 1)
                    wait(act, fassoc_done, u - 1)
                    act.activation(a_t[:, :], r_t[:, :], ACT.Abs).then_inc(abs_done, 1)
                    act.activation(trig[:, s, 1, 1:WIN + 1], r_t[:, :], ACT.Sin, scale=-TURN)
                    act.activation(trig[:, s, :, 0:1], tcarry[:, ds(b, 1), cb, :].rearrange("p a r -> p r a"),
                                   ACT.Copy)
                    act.wait_ge(abs_done, u + 1)
                    act.activation(trig[:, s, 0, 1:WIN + 1], a_t[:, :], ACT.Sin, scale=-TURN, bias=HALF_PI).then_inc(trig_done, 1)
                    if cb == 5 and wp is not None:
                        copy_h2T(g - 1)

            bodies(act, body)
            copy_h2T(NG - 1)
            act.wait_ge(rt_exp_in, 1)
            act.activation(expo, expo, ACT.Exp).then_inc(rt_exp, 1)
            act.activation(wgt[:, 1, :], m1[:, 1, :], ACT.Exp).then_inc(rt_exp, 1)

            def step(j, s, lo=0, hi=3):
                if lo <= 1 <= hi:
                    wait(act, bgu_done, j)
                    wait(act, bhid_done, j - 2)
                    act.activation(sg[:, (s - 1) % 2, :], ps[:, 2 + (s - 1) % 2, 0:EH], ACT.Silu).then_inc(bsilu_done, 1)
                if lo <= 2 <= hi:
                    wait(act, bht_done, j - 1)
                    wait(act, by_done, j - 4)
                    act.activation(hidT[:, :, (s - 2) % 4, :], ps[:, 4 + s % 2, 0:2 * P].rearrange("p (k m) -> p k m", k=KT),
                                   ACT.Copy).then_inc(bhT_done, 1)
                if lo <= 3 <= hi:
                    wait(act, by_done, j - 2)
                    if isinstance(j, int):
                        wait(act, ystor[(s - 3) % 4], 16 * ((j - 3) // 4))
                    else:
                        act.wait_ge(ystor[(s - 3) % 4], 4 * (j - 3 - (s - 3) % 4))
                    act.activation(ysb[:, (s - 3) % 4, :], ps[:, 6 + (s - 3) % 2, 0:D], ACT.Copy).then_inc(by_copied, 1)

            act.wait_ge(x2_out, 16 * NG)
            for j in range(8):
                step(j, j % 4, 0, j)
            with act.Fori(2, NBLK // 4) as i:
                for s in range(4):
                    step(i * 4 + s, s)
            for j in range(3):
                step(NBLK + j, j, j + 1, 3)

        @block.vector
        def _(dve):
            v = nc.vector
            chain = [0]

            def link(ins, s=pc_chain):
                chain[0] += 1
                ins.then_inc(s, 1)
                dve.wait_ge(s, chain[0])

            v.memset(one[:, :], 1.0)
            v.memset(mhalf[:, :], -0.5)
            link(v.memset(tcarry[:, :, :, :], 0.0))
            dve.wait_ge(silu_done, 1)
            v.tensor_copy(csb, csT[:, :, :].unsqueeze(3).to_broadcast([P, KT, B, P])).then_inc(csb_done, 1)
            dve.wait_ge(modc_mm, 1)
            link(v.tensor_copy(modc[:, :, :], ps[:, MISC, 0:2 * KT * B].rearrange("p (j b) -> p j b", b=B)))
            v.tensor_scalar(modc[:, KT:2 * KT, :], modc[:, KT:2 * KT, :], 1.0, None, ALU.add).then_inc(modc_done, 1)

            def ln_stats(src, mv, ve, g, chain_, done):
                for q in range(Q):
                    last = v.bn_stats(bnst[:, q, :], src[:, q, :])
                last.then_inc(chain_, 1)
                wait(dve, chain_, 2 * g + 1)
                apart(dve, g)
                for q in range(Q):
                    last = v.bn_aggr(mv[:, q, :], bnst[:, q, :])
                last.then_inc(chain_, 1)
                wait(dve, chain_, 2 * g + 2)
                v.tensor_scalar(ve[:, :], mv[:, :, 1], EPS, None, ALU.add).then_inc(done, 1)

            def ln_apply(dst, src, mv, rs, done):
                for q in range(Q):
                    last = v.tensor_scalar(dst[:, q, :], src[:, q, :], mv[:, q, 0:1], rs[:, q:q + 1], ALU.subtract, ALU.mult)
                last.then_inc(done, 1)

            def add_heads(g, b, w):
                wait(dve, wo_done, CB * (g + 1))
                if isinstance(g, int):
                    wait(dve, h2_out, 16 * g)
                for q in range(Q):
                    last = v.scalar_tensor_tensor(h2[:, q, :], ps[:, WO + q // 2, (q % 2) * D:(q % 2 + 1) * D],
                                                  isq[:, w * Q + q:w * Q + q + 1], modr[:, ds(b, 1), GA, :], ALU.mult, ALU.mult)
                last.then_inc(wo_read, 1)
                wait(dve, wo_read, g + 1)
                wait(dve, xr_in, 16 * (g + 1))
                v.tensor_tensor(xr[:, :, :], xr[:, :, :], h2[:, :, :], ALU.add).then_inc(x2_done, 1)
                wait(dve, x2_done, g + 1)
                ln_stats(xr, mv2, ve2, g, ln2_chain, var2_done)

            def normalise2(g, b):
                wait(dve, rstd2_done, g + 1)
                ln_apply(h2, xr, mv2, rs2, h2n_done)
                wait(dve, h2n_done, g + 1)
                v.tensor_tensor(h2[:, :, :], h2[:, :, :], modr[:, ds(b, 1), CB1, :].to_broadcast([P, Q, D]), ALU.mult).then_inc(h2c_done, 1)
                wait(dve, h2c_done, g + 1)
                v.tensor_tensor(h2[:, :, :], h2[:, :, :], modr[:, ds(b, 1), SB_, :].to_broadcast([P, Q, D]), ALU.add).then_inc(h2_done, 1)

            def copy_logits(g, b, w):
                wait(dve, lg_done, g + 1)
                v.tensor_scalar(logits[:, ds(b * TB + w * Q, Q), :],
                                ps[:, MISC, 0:Q * E].rearrange("p (q e) -> p q e", q=Q), 1.0, None, ALU.mult).then_inc(lg_copied, 1)

            def turns(u, s):
                wait(dve, t_done, u + 1)
                wait(dve, trig_done, u)
                v.scalar_tensor_tensor(r_t[:, :], t_t[:, :], MAGIC, ps[:, U + s, :], ALU.subtract, ALU.subtract).then_inc(r_done, 1)

            def assoc_sums(u, s, w, b, cb):
                wait(dve, trig_done, u + 1)
                wait(dve, vcopy_done, u + 1)
                wait(dve, pair_done, u - 1)
                v.tensor_tensor(prod[:, s, 2:4, :], vg[:, s, 1:2, :].to_broadcast([P, 2, WIN]), trig[:, s, :, 0:WIN],
                                ALU.mult).then_inc(dassoc_done, 1)
                wait(dve, dassoc_done, u + 1)
                for r in (2, 3):
                    last = v.tensor_tensor_scan(prod[:, s, r, :], one[:, 0:1].to_broadcast([P, WIN]), prod[:, s, r, :],
                                                scarry[:, ds(b, 1), cb, r] if w else 0.0, ALU.mult, ALU.add)
                last.then_inc(sassoc_done, 1)

            def pos_sums(u, s, w, b, cb):
                wait(dve, dpos_done, u + 1)
                for r in (0, 1):
                    last = v.tensor_tensor_scan(prod[:, s, r, :], one[:, 0:1].to_broadcast([P, WIN]), prod[:, s, r, :],
                                                scarry[:, ds(b, 1), cb, r] if w else 0.0, ALU.mult, ALU.add)
                last.then_inc(spos_done, 1)
                wait(dve, spos_done, u + 1)
                wait(dve, sassoc_done, u + 1)
                v.tensor_scalar(scarry[:, ds(b, 1), cb, :].rearrange("p a r -> p r a"),
                                prod[:, s, :, WIN - 1:WIN], 1.0, None, ALU.mult).then_inc(carry_done, 1)

            def assoc_probe(u, s):
                wait(dve, carry_done, u + 1)
                v.tensor_tensor(prod[:, s, 2:4, :], prod[:, s, 2:4, :], trig[:, s, :, 1:WIN + 1], ALU.mult).then_inc(fassoc_done, 1)

            def pairs(u, s):
                wait(dve, fpos_done, u + 1)
                wait(dve, fassoc_done, u + 1)
                wait(dve, mixed_done, u)
                pv = prod[:, s, :, :].rearrange("p (a c) t -> p a c t", c=2)
                v.tensor_tensor(ssum[:, :, :], pv[:, :, 0, :], pv[:, :, 1, :], ALU.add).then_inc(pair_done, 1)

            def table_angles(w, cb):
                m = w * CB + cb
                wait(dve, nphi_done, m + 1)
                v.scalar_tensor_tensor(phi[:, :], nphi[:, :], -C1, phi[:, :], ALU.mult, ALU.add).then_inc(phir_mid, 1)
                wait(dve, phir_mid, 2 * m + 1)
                v.scalar_tensor_tensor(phi[:, :], nphi[:, :], -C2, phi[:, :], ALU.mult, ALU.add).then_inc(phir_mid, 1)
                wait(dve, phir_mid, 2 * m + 2)
                v.tensor_scalar(phi[:, :], phi[:, :], PI, -PI, ALU.min, ALU.max).then_inc(phir_done, 1)

            def body(w, b, wp, bp):
                g = w * B + b
                u0 = g * CB
                tables = isinstance(b, int)
                wait(dve, xa_in, 16 * (g + 1))
                ln_stats(xa, mv1, ve1, g, ln1_chain, var1_done)
                if tables and w == 0:
                    dve.wait_ge(modr_copied, B)
                    v.tensor_scalar(modr[:, :, CB1, :], modr[:, :, CB1, :], 1.0, None, ALU.add)
                    sgn = ssum[:, :, :].rearrange("p a (c d) -> p (a c) d", d=D)
                    for which in (GA, GB):
                        link(v.tensor_scalar(sgn, modr[:, :, which, :], 0.0, 2.0, ALU.is_ge, ALU.mult))
                        link(v.scalar_tensor_tensor(modr[:, :, which, :], modr[:, :, which, :], -1.0,
                                                    modr[:, :, which, :], ALU.mult, ALU.max))
                        link(v.tensor_scalar(modr[:, :, which, :], modr[:, :, which, :], 0.25, None, ALU.max))
                        link(v.scalar_tensor_tensor(modr[:, :, which, :], sgn, 1.0, modr[:, :, which, :],
                                                    ALU.subtract, ALU.mult))
                    dve.wait_ge(wk_in, 16)
                    v.tensor_scalar(wk[:, :, :], wk[:, :, :], PHASE / TWO_PI, None, ALU.mult).then_inc(wk_scaled, 1)
                if wp is None:
                    wait(dve, rstd1_done, g + 1)
                    ln_apply(xa, xa, mv1, rs1, xn_done)
                for cb in range(CB):
                    u = u0 + cb
                    s = cb % 2
                    lw, lb, lc = (w, b, cb - 1) if cb else (wp, bp, CB - 1)
                    if lw is None:
                        table_angles(w, cb)
                        turns(u, s)
                        continue
                    assoc_sums(u - 1, 1 - s, lw, lb, lc)
                    if cb == 0:
                        wait(dve, rstd1_done, g + 1)
                        ln_apply(xa, xa, mv1, rs1, xn_done)
                    if tables:
                        table_angles(w, cb)
                    if cb:
                        turns(u, s)
                    pos_sums(u - 1, 1 - s, lw, lb, lc)
                    assoc_probe(u - 1, 1 - s)
                    if wp is not None or cb >= 2:
                        pairs(u - 2, s)
                    if cb == 0:
                        turns(u, s)
                    if cb == 3 and wp is not None:
                        add_heads(g - 1, bp, wp)
                    if cb == 4 and wp is not None:
                        normalise2(g - 1, bp)
                    if cb == 7 and wp is not None:
                        copy_logits(g - 1, bp, wp)

            bodies(dve, body)
            s = (CB - 1) % 2
            assoc_sums(NU - 1, s, NW - 1, B - 1, CB - 1)
            pos_sums(NU - 1, s, NW - 1, B - 1, CB - 1)
            assoc_probe(NU - 1, s)
            pairs(NU - 2, 1 - s)
            pairs(NU - 1, s)
            add_heads(NG - 1, B - 1, NW - 1)
            normalise2(NG - 1, B - 1)
            copy_logits(NG - 1, B - 1, NW - 1)

            chain[0] = 0

            def step_(ins):
                link(ins, rt)

            def over_e(ap):
                return ap.unsqueeze(2).to_broadcast([P, NT, E])

            dve.wait_ge(rt_iota, 4)
            dve.wait_ge(lg_copied, NG)
            dve.wait_ge(mixed_done, NU)
            dve.wait_ge(wo_done, NU)
            dve.wait_ge(trig_done, NU)
            e_row = e16.unsqueeze(1).to_broadcast([P, NT, E])
            src = logits[:, :, :]
            for k in range(2):
                step_(v.tensor_reduce(m1[:, k, :], src, AX.X, ALU.max))
                step_(v.tensor_tensor(eqt, src, over_e(m1[:, k, :]), ALU.is_equal))
                step_(v.tensor_scalar(eqt, eqt, -1.0, -float(E), ALU.add, ALU.mult))
                step_(v.tensor_tensor(eqt, eqt, e_row, ALU.add))
                step_(v.tensor_reduce(first[:, :], eqt, AX.X, ALU.min))
                step_(v.tensor_tensor(oh[:, k, :, :], e_row, over_e(first[:, :]), ALU.is_equal))
                if k == 0:
                    step_(v.scalar_tensor_tensor(lmask, oh[:, k, :, :], NEG, src, ALU.mult, ALU.add))
                    src = lmask
            v.tensor_copy(ohb.rearrange("p k (n e) -> p k n e", n=NT), oh).then_inc(rt_onehot, 1)
            step_(v.tensor_tensor(expo, logits[:, :, :], over_e(m1[:, 0, :]), ALU.subtract))
            step_(v.tensor_tensor(m1[:, 1, :], m1[:, 1, :], m1[:, 0, :], ALU.subtract))
            v.memset(segm, 1.0).then_inc(rt_exp_in, 1)
            dve.wait_ge(rt_exp_in, 1)
            step_(v.memset(segm[:, :, :, 0:1], 0.0))
            dve.wait_ge(rt_rank, 1)
            for k in range(2):
                step_(v.tensor_copy(tot[:, k, :, :], ps[:, 2 * k + 1, :].rearrange("p (n e) -> p e n", n=NT)))
            step_(v.tensor_tensor_scan(incl.rearrange("p k e n -> p (k e n)"), segm.rearrange("p k e n -> p (k e n)"),
                                       tot.rearrange("p k e n -> p (k e n)"), 0.0, ALU.mult, ALU.add))
            step_(v.tensor_tensor(tot, incl, tot, ALU.subtract))
            for k in range(2):
                step_(v.tensor_tensor(rank[:, k, :, :], ps[:, 2 * k, :].rearrange("p (n e) -> p n e", n=NT),
                                      tot[:, k, :, :].rearrange("p e n -> p n e"), ALU.add))
            step_(v.tensor_scalar(kept[:, :, :], incl[:, :, :, NT - 1], float(CAP), None, ALU.min))
            step_(v.tensor_tensor(nexp[:, :], kept[:, 0, :], kept[:, 1, :], ALU.add))
            step_(v.tensor_scalar(nexpi[:, :], nexp[:, :], float(P - 1), None, ALU.add))
            step_(v.tensor_scalar(nexpi[:, :], nexpi[:, :], 7, None, ALU.logical_shift_right))
            step_(v.tensor_copy(nblkf[:, :], nexpi[:, :]))
            step_(v.tensor_tensor_scan(bend[:, :], one[:, 0:1].to_broadcast([P, E]), nblkf[:, :], 0.0, ALU.mult, ALU.add))
            step_(v.tensor_tensor(nexp[:, :], bend[:, :], nblkf[:, :], ALU.subtract))
            step_(v.tensor_scalar(aoff[:, 0, :], nexp[:, :], float(P), None, ALU.mult))
            step_(v.tensor_tensor(aoff[:, 1, :], aoff[:, 0, :], kept[:, 0, :], ALU.add))
            for k in range(2):
                step_(v.tensor_tensor(eqt, oh[:, k, :, :], rank[:, k, :, :], ALU.mult))
                step_(v.tensor_reduce(rsel[:, k, :], eqt, AX.X, ALU.add))
                step_(v.tensor_tensor(eqt, oh[:, k, :, :], aoff[:, k:k + 1, :].to_broadcast([P, NT, E]), ALU.mult))
                step_(v.tensor_reduce(slot[:, k, :], eqt, AX.X, ALU.add))
            step_(v.tensor_scalar(keep[:, :, :], rsel[:, :, :], float(CAP), None, ALU.is_lt))
            step_(v.tensor_tensor(slot[:, :, :], slot[:, :, :], rsel[:, :, :], ALU.add))
            step_(v.tensor_tensor(slot[:, :, :], slot[:, :, :], keep[:, :, :], ALU.mult))
            step_(v.tensor_copy(gsi[:, :, :].rearrange("p n k -> p k n"), slot[:, :, :]))
            step_(v.tensor_scalar(smap[:, :, :], keep[:, :, :], -float(P * (P - 1)), float(P * (P - 1)), ALU.mult, ALU.add))
            step_(v.tensor_tensor(sloti[:, :, :], smap[:, :, :], slot[:, :, :], ALU.add))
            step_(v.tensor_scalar(posi[:, :, :], sloti[:, :, :], P - 1, None, ALU.bitwise_and))
            step_(v.tensor_copy(posf[:, :, :], posi[:, :, :]))
            step_(v.tensor_scalar(posi[:, :, :], sloti[:, :, :], 7, None, ALU.logical_shift_right))
            step_(v.tensor_copy(blkf[:, :, :], posi[:, :, :]))
            def hot_four(i, first):
                for s in range(4):
                    n, k = i * 2 + s // 2, s % 2
                    if not first:
                        dve.wait_ge(map_mm, i * 4 + s - 3)
                    v.tensor_scalar(pos_hot[:, s, :], iota_p, posf[:, k, ds(n, 1)], None, ALU.is_equal)
                    v.tensor_scalar(blk_hot[:, s, :], iota_p, blkf[:, k, ds(n, 1)], tokf[:, ds(n, 1)],
                                    ALU.is_equal, ALU.mult).then_inc(hot_done, 1)

            hot_four(0, True)
            with dve.Fori(1, NT // 2) as i:
                hot_four(i, False)
            step_(v.memset(eblk[:, :], 0.0))
            for e in range(E - 1):
                step_(v.scalar_tensor_tensor(eblk[:, :], iota_p, bend[:, e:e + 1], eblk[:, :], ALU.is_ge, ALU.add))
            v.tensor_copy(eblki[:, :], eblk[:, :]).then_inc(exps_done, 1)
            dve.wait_ge(map_mm, 2 * NT)
            v.tensor_copy(mapi[:, :], ps[:, MISC, 0:P]).then_inc(map_done, 1)
            dve.wait_ge(rt_exp, 2)
            step_(v.tensor_reduce(zsum[:, :], expo, AX.X, ALU.add))
            step_(v.reciprocal(wgt[:, 0, :], zsum[:, :]))
            step_(v.tensor_tensor(wgt[:, 1, :], wgt[:, 1, :], wgt[:, 0, :], ALU.mult))
            step_(v.tensor_tensor(wgt[:, :, :], wgt[:, :, :], keep[:, :, :], ALU.mult))

            def step(j, s, lo=0, hi=3):
                if lo <= 0 <= hi:
                    wait(dve, bt_done, j + 1)
                    wait(dve, bgu_done, j - 3)
                    v.tensor_copy(xgT[:, :, s % 4, :], ps[:, 0 + s % 2, 0:2 * P].rearrange("p (k m) -> p k m", k=KT)).then_inc(bxT_done, 1)
                if lo <= 1 <= hi:
                    wait(dve, bsilu_done, j)
                    wait(dve, bht_done, j - 2)
                    v.tensor_tensor(hid[:, (s - 1) % 2, :], sg[:, (s - 1) % 2, :], ps[:, 2 + (s - 1) % 2, EH:2 * EH],
                                    ALU.mult).then_inc(bhid_done, 1)

            for j in range(8):
                step(j, j % 4, 0, j)
            with dve.Fori(2, NBLK // 4) as i:
                for s in range(4):
                    step(i * 4 + s, s)
            step(NBLK, 0, 1, 3)

            with dve.Fori(0, B) as b:
                for nn in range(TB):
                    n = b * TB + nn
                    s = nn % 4
                    dve.wait_ge(yg[s], (b * (TB // 4) + nn // 4) * 32 + 32)
                    v.tensor_scalar(y0[:, s, :], y0[:, s, :], wgt[:, 0, ds(n, 1)], None, ALU.mult).then_inc(cw0_done, 1)
                    dve.wait_ge(cw0_done, n + 1)
                    v.scalar_tensor_tensor(y0[:, s, :], y1[:, s, :], wgt[:, 1, ds(n, 1)], y0[:, s, :], ALU.mult,
                                           ALU.add).then_inc(cw1_done, 1)
                    dve.wait_ge(cw1_done, n + 1)
                    v.tensor_tensor(y0[:, s, :], y0[:, s, :], modr[:, ds(b, 1), GB, :], ALU.mult).then_inc(cgb_done, 1)
                    dve.wait_ge(cgb_done, n + 1)
                    dve.wait_ge(xf_in[s], (b * (TB // 4) + nn // 4) * 16 + 16)
                    v.tensor_tensor(xf[:, s, :], xf[:, s, :], y0[:, s, :], ALU.add).then_inc(csum_done, 1)

        @block.gpsimd
        def _(pool):
            gp = nc.gpsimd
            gp.memset(ident[:, :], 0.0).then_inc(ident_done, 1)
            gp.iota(trow[:, :], [[1, T]], base=0, channel_multiplier=0, allow_small_or_imprecise_dtypes=True).then_inc(iota_done, 1)
            gp.iota(tcol[:, :], [[P, TB]], base=1, channel_multiplier=1, allow_small_or_imprecise_dtypes=True).then_inc(isq_done, 1)
            gp.iota(tokf[:, :], [[P, NT]], base=0, channel_multiplier=1, allow_small_or_imprecise_dtypes=True)
            pool.wait_ge(ident_done, 1)
            gp.affine_select(out=ident[:, :], in_=ident[:, :], compare_op=ALU.not_equal, fill=1.0, base=0,
                             pattern=[[-1, P]], channel_multiplier=1).then_inc(ident_done, 1)
            pool.wait_ge(pc_chain, 1)
            pool.wait_ge(isq_done, 1)
            gp.tensor_tensor(isq[:, :], tcol[:, :], mhalf[:, :], ALU.pow).then_inc(isq_done, 1)

            def rstd(var, dst, ve, n, done):
                wait(pool, var, n)
                gp.tensor_tensor(dst[:, :], ve[:, :], mhalf[:, 0:Q], ALU.pow).then_inc(done, 1)

            def pos_products(u, s, cb, w):
                wait(pool, vcopy_done, u + 1)
                wait(pool, tab_done, w * CB + cb + 1)
                wait(pool, pair_done, u - 1)
                gp.tensor_tensor(prod[:, s, 0:2, :], vg[:, s, 0:1, :].to_broadcast([P, 2, WIN]), tab[:, cb, :, :],
                                 ALU.mult).then_inc(dpos_done, 1)

            def mix(u, s):
                wait(pool, pair_done, u + 1)
                wait(pool, wo_done, u - 1)
                gp.tensor_tensor(o_t[:, s, :], ssum[:, 0, :], ssum[:, 1, :], ALU.add).then_inc(mixed_done, 1)

            def pos_probe(u, s, cb):
                wait(pool, carry_done, u + 1)
                gp.tensor_tensor(prod[:, s, 0:2, :], prod[:, s, 0:2, :], tab[:, cb, :, :], ALU.mult).then_inc(fpos_done, 1)

            def body(w, b, wp, bp):
                g = w * B + b
                u0 = g * CB
                rstd(var1_done, rs1, ve1, g + 1, rstd1_done)
                for cb in range(CB):
                    u = u0 + cb
                    s = cb % 2
                    lw, lc = (w, cb - 1) if cb else (wp, CB - 1)
                    if lw is None:
                        continue
                    pos_products(u - 1, 1 - s, lc, lw)
                    if wp is not None or cb >= 3:
                        mix(u - 3, 1 - s)
                    pos_probe(u - 1, 1 - s, lc)
                    if cb == 3 and wp is not None:
                        rstd(var2_done, rs2, ve2, g, rstd2_done)

            bodies(pool, body)
            s = (CB - 1) % 2
            pos_products(NU - 1, s, CB - 1, NW - 1)
            mix(NU - 3, s)
            pos_probe(NU - 1, s, CB - 1)
            mix(NU - 2, 1 - s)
            mix(NU - 1, s)
            rstd(var2_done, rs2, ve2, NG, rstd2_done)

            pool.wait_ge(trig_done, NU)
            gp.iota(iota_p, [[1, P]], base=0, channel_multiplier=0, allow_small_or_imprecise_dtypes=True).then_inc(rt_iota, 1)
            gp.iota(e16, [[1, E]], base=-E, channel_multiplier=0, allow_small_or_imprecise_dtypes=True).then_inc(rt_iota, 1)
            gp.memset(onesb, 1.0).then_inc(rt_iota, 1)
            pool.wait_ge(rt_iota, 3)
            gp.affine_select(out=triu, in_=onesb, compare_op=ALU.is_gt, fill=0.0, base=0,
                             pattern=[[1, P]], channel_multiplier=-1).then_inc(rt_iota, 1)

            pool.wait_ge(map_done, 1)
            pool.wait_ge(h2_out, 16 * NG)

            def gather(j, s, first_round):
                if not first_round:
                    pool.wait_ge(gath[s], 4 * (j - s))
                    pool.wait_ge(bt_done, j - 3)
                wait(pool, carried, j)
                gp.tensor_copy(idxc[:, s, 0:1], mapi[:, ds(j, 1)]).then_inc(idx_done, 1)
                pool.wait_ge(idx_done, j + 1)
                gp.tensor_tensor(spare[:, 4:5], one[:, 0:1], one[:, 0:1], ALU.mult).then_inc(carried, 1)
                gp.indirect_dma_start(out=xg[:, s, :], out_offset=None, in_=h2_d,
                                      in_offset=bass.IndirectOffsetOnAxis(ap=idxc[:, s, 0:1], axis=0)).then_inc(gath[s], 16)

            for j in range(4):
                gather(j, j, True)
            with pool.Fori(1, NBLK // 4) as i:
                for s in range(4):
                    gather(i * 4 + s, s, False)

            for s in range(4):
                pool.wait_ge(ystor[s], 16 * (NBLK // 4))
            pool.wait_ge(gath[3], 16 * (NBLK // 4))

            def gather_y(n, s, first_round):
                if not first_round:
                    pool.wait_ge(csum_done, n - 3)
                wait(pool, carried, NBLK + n)
                gp.tensor_copy(idxc[:, s, :], gsi[:, ds(n, 1), :].rearrange("p a k -> p (a k)")).then_inc(cidx_done, 1)
                pool.wait_ge(cidx_done, n + 1)
                gp.tensor_tensor(spare[:, 4:5], one[:, 0:1], one[:, 0:1], ALU.mult).then_inc(carried, 1)
                gp.indirect_dma_start(out=y0[:, s, :], out_offset=None, in_=y_d,
                                      in_offset=bass.IndirectOffsetOnAxis(ap=idxc[:, s, 0:1], axis=0)).then_inc(yg[s], 16)
                gp.indirect_dma_start(out=y1[:, s, :], out_offset=None, in_=y_d,
                                      in_offset=bass.IndirectOffsetOnAxis(ap=idxc[:, s, 1:2], axis=0)).then_inc(yg[s], 16)

            for n in range(4):
                gather_y(n, n, True)
            with pool.Fori(1, NT // 4) as i:
                for s in range(4):
                    gather_y(i * 4 + s, s, False)


_INS = ['L0_attn_x', 'L0_attn_Wk', 'L0_attn_Wv', 'L0_attn_Wo', 'L0_attn_gate', 'L0_attn_freqs', 'L0_ffn_router_w',
        'L0_ffn_gate_w', 'L0_ffn_up_w', 'L0_ffn_down_w', 'L0_c', 'L0_wmod']
_OUTS = [((4, 1024, 256), 'float32')]


def kernel(**inputs):
    import numpy as _np
    import concourse.bacc as _bacc
    from concourse import mybir as _mybir
    from concourse.bass_utils import run_bass_kernel_spmd as _run

    nc = _bacc.Bacc("TRN2", target_bir_lowering=False, num_devices=1)
    arrays, args = {}, []
    for name in _INS:
        a = _np.ascontiguousarray(inputs[name])
        arrays[f"in_{name}_dram"] = a
        args.append(nc.dram_tensor(f"in_{name}_dram", a.shape, _mybir.dt.from_np(a.dtype), kind="ExternalInput").ap())
    for i, (shape, dtype) in enumerate(_OUTS):
        dt = _mybir.dt.from_np(_np.dtype(dtype))
        args.append(nc.dram_tensor(f"out_{i}_dram", shape, dt, kind="ExternalOutput").ap())
    adaln_block(nc, *args)
    r = _run(nc, [arrays], core_ids=[0])
    return r.results[0]["out_0_dram"]
```

```python
import concourse.bass as bass
from concourse import mybir
from contextlib import ExitStack
import math
import numpy as np


def adaln_block(nc, x, wk_d, wv_d, wo_d, gate_d, freqs_d, router_d, egate_d, eup_d, edown_d, c_d, wmod_d, out):
    fp32, i32, bf16 = mybir.dt.float32, mybir.dt.int32, mybir.dt.bfloat16
    ALU, ACT, AX = mybir.AluOpType, mybir.ActivationFunctionType, mybir.AxisListType
    ds = bass.ds

    B, T, D = x.shape
    P = 128
    H, HD = freqs_d.shape
    CH = H * HD
    CB = CH // P
    WIN = 512
    NW = T // WIN
    Q = WIN // P
    KT = D // P
    NG = NW * B
    NU = NG * CB
    N = B * T
    NT = N // P
    TB = T // P
    E = router_d.shape[1]
    EH = egate_d.shape[2]
    TOPK = 2
    CAP = max(1, math.ceil(N * TOPK / E * 1.25))
    NBLK = -(-(N * TOPK // P + E) // 4) * 4
    assert KT == 2 and EH == 2 * P and NBLK <= P and NG == 8 and CB % 2 == 0
    PHASE = 10.0
    TWO_PI = 2.0 * math.pi
    TURN = float(np.nextafter(np.float32(TWO_PI), np.float32(0)))
    HALF_PI = float(np.float32(math.pi / 2))
    PI = float(np.nextafter(np.float32(math.pi), np.float32(0)))
    MAGIC = 12582912.0
    C1 = 6.28125
    C2 = float(np.float32(TWO_PI - C1))
    EPS = 1e-5
    NEG = -3.0e38

    x_v = x.rearrange("b (n p) d -> p (b n) d", p=P)
    out_v = out.rearrange("b (n p) d -> p (b n) d", p=P)
    x2_d = nc.dram_tensor("x2_scratch", (N, D), fp32, kind="Internal").ap()
    h2_d = nc.dram_tensor("h2_scratch", (N, D), fp32, kind="Internal").ap()
    y_d = nc.dram_tensor("y_scratch", (NBLK * P, D), fp32, kind="Internal").ap()
    x2_v = x2_d.rearrange("(n p) d -> p n d", p=P)
    h2_v = h2_d.rearrange("(n p) d -> p n d", p=P)
    y_v = y_d.rearrange("(n p) d -> p n d", p=P)

    ctx = ExitStack()
    with ctx:
        def sb(name, shape, dt=fp32):
            return ctx.enter_context(nc.sbuf_tensor(name, shape, dt))

        def sem(name):
            return ctx.enter_context(nc.semaphore(name))

        egu = sb("egu", [P, E * KT * 2 * EH])
        egu_v = egu[:, :].rearrange("p (e k n) -> p e k n", e=E, k=KT)
        LATE = 4
        pr_flat = egu[:, (E - LATE) * KT * 2 * EH:]
        prod = pr_flat[:, 0:4 * WIN].rearrange("p (s r t) -> p s r t", s=2, r=2)
        hT = pr_flat[:, 4 * WIN:(4 + 2 * KT) * WIN].rearrange("p (s k t) -> p s k t", s=2, k=KT)
        MODE = E - 2 * LATE
        assert 6 * D + B * P <= LATE * 2 * EH
        mo_flat = egu[:, MODE * KT * 2 * EH:(E - LATE) * KT * 2 * EH]
        wmod = mo_flat[:, 0:KT * 6 * D].rearrange("p (k n) -> p k n", k=KT)
        csb = mo_flat[:, KT * 6 * D:KT * 6 * D + KT * B * P].rearrange("p (k b m) -> p k b m", k=KT, b=B)
        tab_flat = sb("rotor_tables", [P, CB * 2 * WIN])
        tab = tab_flat[:, :].rearrange("p (c r t) -> p c r t", c=CB, r=2)
        edn_v = tab_flat[:, :].rearrange("p (e k n) -> p e k n", e=E, k=KT)
        wk = sb("wk", [P, KT, CH])
        wv = sb("wv", [P, KT, CH])
        wo = sb("wo", [P, CB, D])
        modr = sb("mod_rows", [P, B, 4, D])
        GA, SB_, CB1, GB = range(4)
        modc = sb("mod_cols", [P, 2 * KT, B])
        trow = sb("t_row", [P, T])
        trig = sb("trig", [P, 2, 2, WIN + 1])
        v_flat = sb("v_gated", [P, 4 * WIN])
        vg = v_flat[:, 0:2 * WIN].rearrange("p (s t) -> p s t", s=2)
        parts = sb("head_parts", [P, 2, 2, WIN])
        t_t = sb("rounded_turns", [P, WIN])
        r_t = sb("turns", [P, WIN])
        a_t = sb("abs_turns", [P, WIN])
        phi = sb("phi", [P, WIN])
        nphi = sb("nphi", [P, WIN])
        xa = sb("xa", [P, Q, D])
        xr = sb("xr", [P, Q, D])
        h2 = sb("h2", [P, Q, D])
        xgT_flat = sb("xgT", [P, KT * WIN])
        h2T = sb("h2T", [P, KT, WIN])
        rw = sb("router_w", [P, KT, E])
        gcol = sb("gate_cols", [P, CB, 2])
        fcol = sb("freq_cols", [P, CB])
        cT = sb("cT", [P, KT, B])
        csT = sb("csT", [P, KT, B])
        ident = sb("ident", [P, P])
        tcarry = sb("trig_carry", [P, B, CB, 2])
        scarry = sb("scan_carry", [P, B, CB, 4])
        one = sb("one", [P, 1])
        spare = sb("spare", [P, 8])
        mhalf = sb("minus_half", [P, TB])
        bnst = sb("bn_stats", [P, Q, 6])
        mv1 = sb("mean_var1", [P, Q, 2])
        mv2 = sb("mean_var2", [P, Q, 2])
        ve1 = sb("var_eps1", [P, Q])
        ve2 = sb("var_eps2", [P, Q])
        nm1 = sb("neg_mean1", [P, Q])
        nm2 = sb("neg_mean2", [P, Q])
        sh1 = sb("shift1", [P, Q])
        sh2 = sb("shift2", [P, Q])
        rs1 = sb("rstd1", [P, Q])
        rs2 = sb("rstd2", [P, Q])
        isq = sb("inv_sqrt_t", [P, TB])
        tcol = sb("t_col", [P, TB])
        logits = sb("logits", [P, NT, E])
        NE = NT * E
        vf = v_flat
        oh = vf[:, 0:2 * NE].rearrange("p (k n e) -> p k n e", k=2, n=NT)
        eqt = vf[:, 2 * NE:3 * NE].rearrange("p (n e) -> p n e", n=NT)
        lmask = vf[:, 3 * NE:4 * NE].rearrange("p (n e) -> p n e", n=NT)
        tf = trig[:, :, :, :].rearrange("p a b t -> p (a b t)")
        tot = tf[:, 0:2 * NE].rearrange("p (k e n) -> p k e n", k=2, e=E)
        incl = tf[:, 2 * NE:4 * NE].rearrange("p (k e n) -> p k e n", k=2, e=E)
        rank = parts[:, 0, :, :].rearrange("p k (n e) -> p k n e", n=NT)
        segm = parts[:, 1, :, :].rearrange("p k (e n) -> p k e n", e=E)
        ohb = t_t[:, :].bitcast(bf16).rearrange("p (k m) -> p k m", k=2)
        expo = r_t[:, :].rearrange("p (n e) -> p n e", n=NT)
        iota_p = a_t[:, 0:P]
        triu = a_t[:, P:P + P // 2].bitcast(bf16)
        onesb = a_t[:, P + P // 2:2 * P].bitcast(bf16)
        e16 = a_t[:, 2 * P:2 * P + E]
        blk_hot = phi[:, :].rearrange("p (s m) -> p s m", s=4)
        pos_hot = nphi[:, :].rearrange("p (s m) -> p s m", s=4)
        hx = h2[:, :, :].rearrange("p q d -> p (q d)")
        m1 = sb("top_logit", [P, 2, NT])
        first = sb("first_index", [P, NT])
        zsum = sb("z_sum", [P, NT])
        wgt = sb("weights", [P, 2, NT])
        rsel = sb("ranks", [P, 2, NT])
        keep = sb("keep", [P, 2, NT])
        slot = sb("slots", [P, 2, NT])
        smap = sb("slots_mapped", [P, 2, NT])
        sloti = sb("slots_int", [P, 2, NT], i32)
        gsi = sb("gather_slots", [P, NT, 2], i32)
        posi = sb("pos_int", [P, 2, NT], i32)
        posf = sb("pos_f", [P, 2, NT])
        blkf = sb("blk_f", [P, 2, NT])
        tokf = sb("token_ids", [P, NT])
        kept = sb("kept", [P, 2, E])
        nexp = sb("n_expert", [P, E])
        nexpi = sb("n_expert_int", [P, E], i32)
        nblkf = sb("n_blocks", [P, E])
        bend = sb("block_end", [P, E])
        aoff = sb("slot_offsets", [P, 2, E])
        eblk = sb("expert_of_block", [P, P])
        eblki = sb("expert_of_block_int", [P, P], i32)
        mapi = sb("slot_tokens", [P, P], i32)
        idxc = sb("gather_index", [P, 4, 2], i32)
        xg = xa
        xgT = xgT_flat[:, :].rearrange("p (k s m) -> p k s m", k=KT, s=4)
        hidT = h2T[:, :, :].rearrange("p k (s m) -> p k s m", s=4)
        sg = parts[:, 0, :, 0:EH]
        hid = parts[:, 1, :, 0:EH]
        ysb = xr
        y0 = vf[:, 0:4 * D].rearrange("p (s d) -> p s d", s=4)
        y1 = vf[:, 4 * D:8 * D].rearrange("p (s d) -> p s d", s=4)
        xf = tf[:, 0:4 * D].rearrange("p (s d) -> p s d", s=4)

        ps = ctx.enter_context(nc.psum_tensor("ps", [P, 8, 512], fp32))
        U, V, A, WO, TP = 0, 1, 3, 5, 7
        MISC = TP
        MOD_STEP = {0: (0, 1), 1: (2, 3, 4), 2: (5,), 3: (6,), 4: (7,)}
        MOD_BANK = (WO, WO + 1, WO, WO + 1, TP, TP, TP, TP)
        LAG = 2

        def S(names):
            return [sem(n) for n in names.split()]

        (c_in, wmod_in, wmodr_in, wk_in, wv_in, wo_in, small_in, xa_in, xr_in, egu_in, elate_in, x2_out, h2_out) = S(
            "c_in wmod_in wmodr_in wk_in wv_in wo_in small_in xa_in xr_in egu_in elate_in x2_out h2_out")
        (ident_done, iota_done, pc_chain, silu_done, csb_done, modc_mm, modr_mm, modc_done, modr_copied, modr_done,
         wk_scaled, isq_done) = S(
            "ident_done iota_done pc_chain silu_done csb_done modc_mm modr_mm modc_done modr_copied modr_done wk_scaled isq_done")
        (var1_done, rstd1_done, xn_done, tp1_done, hT_done, k_done, v_done, t_done, r_done, abs_done, sin_done, trig_done,
         vcopy_done) = S(
            "var1_done rstd1_done xn_done tp1_done hT_done k_done v_done t_done r_done abs_done sin_done trig_done vcopy_done")
        (phi_done, nphi_mid, nphi_done, phir_mid, phir_done, phia_done, tab_done) = S(
            "phi_done nphi_mid nphi_done phir_mid phir_done phia_done tab_done")
        (dassoc_done, sassoc_done, dpos_done, spos_done, carry_done, kept_done, fassoc_done, fpos_done, parts_done, wo_done) = S(
            "dassoc_done sassoc_done dpos_done spos_done carry_done kept_done fassoc_done fpos_done parts_done wo_done")
        (wo_read, x2_done, var2_done, rstd2_done, h2n_done, h2c_done, h2_done, tp2_done, h2T_done, lg_done, lg_copied, ln1_chain, ln2_chain) = S(
            "wo_read x2_done var2_done rstd2_done h2n_done h2c_done h2_done tp2_done h2T_done lg_done lg_copied ln1_chain ln2_chain")
        (rt, rt_iota, rt_onehot, rt_rank, rt_exp_in, rt_exp, hot_done, map_mm, map_done, exps_done) = S(
            "rt rt_iota rt_onehot rt_rank rt_exp_in rt_exp hot_done map_mm map_done exps_done")
        gath = [sem(f"rows_gathered{s}") for s in range(4)]
        ystor = [sem(f"y_stored{s}") for s in range(4)]
        yg = [sem(f"y_gathered{s}") for s in range(4)]
        xf_in = [sem(f"x2_back{s}") for s in range(4)]
        ostor = [sem(f"out_stored{s}") for s in range(4)]
        (idx_done, bt_done, bxT_done, bgu_done, bsilu_done, bhid_done, bht_done, bhT_done, by_done, by_copied) = S(
            "idx_done bt_done bxT_done bgu_done bsilu_done bhid_done bht_done bhT_done by_done by_copied")
        carried = sem("carried")
        (cidx_done, cw0_done, cw1_done, cgb_done, csum_done) = S("cidx_done cw0_done cw1_done cgb_done csum_done")

        block = ctx.enter_context(nc.Block())

        def wait(eng, s, n):
            if not (isinstance(n, int) and n <= 0):
                eng.wait_ge(s, n)

        def apart(eng, n):
            if not isinstance(n, int):
                if eng is nc.vector:
                    nc.vector.memset(spare[:, 0:1], 0.0)
                elif eng is nc.gpsimd:
                    nc.gpsimd.tensor_tensor(spare[:, 6:7], one[:, 0:1], one[:, 0:1], ALU.mult)
                else:
                    nc.scalar.activation(spare[:, 2:3], one[:, 0:1], ACT.Copy)

        def table_of(w, b, cb):
            if isinstance(b, int):
                if w == 0 and b == 0:
                    return cb + 1 if cb < CB - 1 else None
                if b == B - 1 and w == 0 and cb >= 2:
                    return CB + cb - 2
                if b == 0 and w == 1 and cb < 2:
                    return 2 * CB - 2 + cb
            return None

        def bodies(eng, body):
            for w in range(NW):
                body(w, 0, w - 1 if w else None, B - 1, w, 1)
                with eng.Fori(1, B - 1) as b:
                    body(w, b, w, b - 1, w, b + 1)
                body(w, B - 1, w, B - 2, w + 1 if w + 1 < NW else None, 0)

        @block.sync
        def _(sp):
            sp.dma_start(cT[:, 0, :], c_d[:, 0:P].rearrange("b p -> p b"), allow_slow_non_contiguous=True).then_inc(c_in, 16)
            sp.dma_start(cT[:, 1, :], c_d[:, P:2 * P].rearrange("b p -> p b"), allow_slow_non_contiguous=True).then_inc(c_in, 16)
            sp.dma_start(xa[:, :, :], x_v[:, 0:Q, :]).then_inc(xa_in, 16)
            wmod_dv = wmod_d.rearrange("(k p) n -> p k n", p=P)
            sp.dma_start(wmod[:, :, 0:2 * D], wmod_dv[:, :, 0:2 * D]).then_inc(wmod_in, 16)
            for hh in range(P // HD):
                sp.dma_start(fcol[hh * HD:(hh + 1) * HD, :],
                             freqs_d.rearrange("(c h) d -> h d c", h=P // HD)[hh, :, :],
                             allow_slow_non_contiguous=True).then_inc(small_in, 16)
                sp.dma_start(gcol[hh * HD:(hh + 1) * HD, :, :],
                             gate_d.rearrange("(c h) g -> h c g", h=P // HD)[hh, :, :].partition_broadcast(HD)
                             ).then_inc(small_in, 16)
            sp.dma_start(wk[:, :, :], wk_d.rearrange("(k p) n -> p k n", p=P)).then_inc(wk_in, 16)
            sp.dma_start(wv[:, :, :], wv_d.rearrange("(k p) n -> p k n", p=P)).then_inc(wv_in, 16)
            sp.dma_start(wmod[:, :, 2 * D:6 * D], wmod_dv[:, :, 2 * D:6 * D]).then_inc(wmodr_in, 16)
            sp.dma_start(rw[:, :, :], router_d.rearrange("(k p) n -> p k n", p=P)).then_inc(wo_in, 16)
            sp.dma_start(wo[:, :, :], wo_d.rearrange("(c p) n -> p c n", p=P)).then_inc(wo_in, 16)

            def body(w, b, wp, bp, wn, bn):
                g = w * B + b
                if wn is not None:
                    wait(sp, tp1_done, KT * (g + 1))
                    sp.dma_start(xa[:, :, :], x_v[:, ds(bn * TB + wn * Q, Q), :]).then_inc(xa_in, 16)
                if wp is not None:
                    wait(sp, x2_done, g)
                    sp.dma_start(x2_v[:, ds(bp * TB + wp * Q, Q), :], xr[:, :, :]).then_inc(x2_out, 16)
                    wait(sp, x2_out, 16 * g)
                    wait(sp, h2n_done, g)
                sp.dma_start(xr[:, :, :], x_v[:, ds(b * TB + w * Q, Q), :]).then_inc(xr_in, 16)
                if wp is not None:
                    wait(sp, h2_done, g)
                    sp.dma_start(h2_v[:, ds(bp * TB + wp * Q, Q), :], h2[:, :, :]).then_inc(h2_out, 16)
                else:
                    for e in range(E - LATE):
                        if e == MODE:
                            sp.wait_ge(modr_mm, 2 * B)
                        for half, src in enumerate((egate_d, eup_d)):
                            sp.dma_start(egu_v[:, e, :, half * EH:(half + 1) * EH],
                                         src[e, :, :].rearrange("(k p) n -> p k n", p=P)).then_inc(egu_in, 16)

            bodies(sp, body)
            sp.wait_ge(x2_done, NG)
            sp.dma_start(x2_v[:, ds((B - 1) * TB + (NW - 1) * Q, Q), :], xr[:, :, :]).then_inc(x2_out, 16)
            sp.wait_ge(h2_done, NG)
            sp.dma_start(h2_v[:, ds((B - 1) * TB + (NW - 1) * Q, Q), :], h2[:, :, :]).then_inc(h2_out, 16)
            sp.wait_ge(parts_done, NU)
            sp.wait_ge(v_done, NU)
            for e in range(E - LATE, E):
                for half, src in enumerate((egate_d, eup_d)):
                    sp.dma_start(egu_v[:, e, :, half * EH:(half + 1) * EH],
                                 src[e, :, :].rearrange("(k p) n -> p k n", p=P)).then_inc(elate_in, 16)
            for e in range(0, E, 4):
                sp.dma_start(edn_v[:, e:e + 4, :, :],
                             edown_d[e:e + 4, :, :].rearrange("e (k p) n -> p e k n", p=P)).then_inc(elate_in, 16)
            with sp.Fori(0, NBLK // 4) as i:
                for s in range(4):
                    sp.wait_ge(by_copied, i * 4 + s + 1)
                    sp.dma_start(y_v[:, ds(i * 4 + s, 1), :], ysb[:, s:s + 1, :]).then_inc(ystor[s], 16)
            sp.wait_ge(x2_out, 16 * NG)
            def last_sums(i, first):
                for s in range(4):
                    if not first:
                        sp.wait_ge(ostor[s], i * 16)
                    sp.dma_start(xf[:, s:s + 1, :], x2_v[:, ds(i * 4 + s, 1), :]).then_inc(xf_in[s], 16)
                for s in range(4):
                    sp.wait_ge(csum_done, i * 4 + s + 1)
                    sp.dma_start(out_v[:, ds(i * 4 + s, 1), :], xf[:, s:s + 1, :]).then_inc(ostor[s], 16)

            last_sums(0, True)
            with sp.Fori(1, NT // 4) as i:
                last_sums(i, False)
            for s in range(4):
                sp.wait_ge(ostor[s], 16 * (NT // 4))

        @block.tensor
        def _(pe):
            pe.wait_ge(silu_done, 1)
            pe.wait_ge(wmod_in, 16)
            for j in range(2 * KT):
                for k in range(KT):
                    last = nc.tensor.matmul(ps[:, MISC, j * B:(j + 1) * B], wmod[:, k, j * P:(j + 1) * P], csT[:, k, :],
                                            start=(k == 0), stop=(k == KT - 1))
            last.then_inc(modc_mm, 1)
            pe.wait_ge(ident_done, 2)

            def modulation_rows(i):
                b, n = i % B, i // B
                wait(pe, modr_copied, {2: 1, 3: 2, 5: 5, 6: 6, 7: 7}.get(i, 0))
                for k in range(KT):
                    last = nc.tensor.matmul(ps[:, MOD_BANK[i], :], csb[:, k, b, :],
                                            wmod[:, k, 2 * D + n * 512:2 * D + (n + 1) * 512],
                                            start=(k == 0), stop=(k == KT - 1))
                last.then_inc(modr_mm, 1)

            def project_out(u, cb):
                wait(pe, parts_done, u + 1)
                for q in range(Q):
                    for r in range(2):
                        last = nc.tensor.matmul(ps[:, WO + q // 2, (q % 2) * D:(q % 2 + 1) * D],
                                                parts[:, cb % 2, r, q * P:(q + 1) * P], wo[:, cb, :],
                                                start=(cb == 0 and q % 2 == 0 and r == 0),
                                                stop=(cb == CB - 1 and r == 1), skip_group_check=True)
                last.then_inc(wo_done, 1)

            def transposes(src, k, done):
                for q in range(Q):
                    last = nc.tensor.transpose(ps[:, TP, q * P:(q + 1) * P], src[:, q, k * P:(k + 1) * P], ident[:, :])
                last.then_inc(done, 1)

            def router_transposes(g, k):
                if k == 0:
                    wait(pe, h2_done, g + 1)
                    wait(pe, hT_done, KT * (g + 3) if not isinstance(g, int) or g < NG - 2 else KT * NG)
                    if isinstance(g, int) and g == NG - 1:
                        wait(pe, lg_copied, g)
                else:
                    wait(pe, h2T_done, KT * g + 1)
                transposes(h2, k, tp2_done)

            def router(g):
                wait(pe, h2T_done, KT * (g + 1))
                for q in range(Q):
                    for k in range(KT):
                        last = nc.tensor.matmul(ps[:, MISC, q * E:(q + 1) * E], h2T[:, k, q * P:(q + 1) * P], rw[:, k, :],
                                                start=(k == 0), stop=(k == KT - 1))
                last.then_inc(lg_done, 1)

            def ln1_transposes(g, k, first_loop=False):
                if k == 0:
                    wait(pe, xn_done, g + 1)
                    if isinstance(g, int):
                        wait(pe, lg_copied, g - 2)
                    elif not first_loop:
                        wait(pe, lg_copied, g - 2)
                else:
                    wait(pe, hT_done, KT * g + k)
                transposes(xa, k, tp1_done)

            pe.wait_ge(modc_done, 1)
            for k in range(KT):
                ln1_transposes(0, k)
            pe.wait_ge(wk_scaled, 1)
            pe.wait_ge(wv_in, 16)
            pe.wait_ge(wmodr_in, 16)
            pe.wait_ge(wo_in, 32)
            pe.wait_ge(csb_done, 1)

            def body(w, b, wp, bp, wn, bn):
                g = w * B + b
                u0 = g * CB
                wait(pe, hT_done, KT * (g + 1))
                hTg = hT[:, ds(b % 2, 1), :, :].rearrange("p s k t -> p (s k) t")
                for cb in range(CB):
                    u = u0 + cb
                    wait(pe, vcopy_done, u - 1)
                    wait(pe, dassoc_done, u - 1)
                    for k in range(KT):
                        last = nc.tensor.matmul(ps[:, V + cb % 2, :], wv[:, k, cb * P:(cb + 1) * P], hTg[:, k, :],
                                                start=(k == 0), stop=(k == KT - 1))
                    last.then_inc(v_done, 1)
                    wait(pe, r_done, u)
                    for k in range(KT):
                        last = nc.tensor.matmul(ps[:, U, :], wk[:, k, cb * P:(cb + 1) * P], hTg[:, k, :],
                                                start=(k == 0), stop=(k == KT - 1))
                    last.then_inc(k_done, 1)
                    if wp is None and cb in MOD_STEP:
                        for i in MOD_STEP[cb]:
                            modulation_rows(i)
                        if cb == LAG:
                            pe.wait_ge(modr_copied, 4)
                        if cb == 4:
                            pe.wait_ge(modr_copied, 8)
                    if cb in (6, 7) and wp is not None:
                        router_transposes(g - 1, cb - 6)
                    if cb in (4, 5) and wn is not None:
                        ln1_transposes(g + 1, cb - 4, w == 0)
                    if wp is not None or cb >= LAG:
                        if cb == LAG:
                            wait(pe, wo_read, g)
                        project_out(u - LAG, (cb - LAG) % CB)
                    if cb == 7 and wp is not None:
                        router(g - 1)

            bodies(pe, body)
            for cb in range(CB - LAG, CB):
                project_out(NU - CB + cb, cb)
            for k in range(KT):
                router_transposes(NG - 1, k)
            router(NG - 1)

            pe.wait_ge(rt_iota, 4)
            pe.wait_ge(rt_onehot, 1)
            for k in range(2):
                nc.tensor.matmul(ps[:, 2 * k, :], triu, ohb[:, k, :], start=True, stop=True)
                last = nc.tensor.matmul(ps[:, 2 * k + 1, :], onesb, ohb[:, k, :], start=True, stop=True)
            last.then_inc(rt_rank, 1)
            def map_four(i, first):
                for s in range(4):
                    pe.wait_ge(hot_done, i * 4 + s + 1)
                    nc.tensor.matmul(ps[:, MISC, 0:P], pos_hot[:, s, :], blk_hot[:, s, :], start=(first and s == 0),
                                     stop=True, skip_group_check=True).then_inc(map_mm, 1)

            map_four(0, True)
            with pe.Fori(1, NT // 2) as i:
                map_four(i, False)

            pe.wait_ge(map_done, 1)
            pe.wait_ge(exps_done, 1)
            pe.wait_ge(egu_in, 16 * 2 * (E - LATE))
            pe.wait_ge(elate_in, 16 * (2 * LATE + 4))

            def step(j, s, lo=0, hi=3):
                if lo <= 0 <= hi:
                    pe.wait_ge(gath[s % 4], 16 * (j // 4 + 1) if isinstance(j, int) else 16 * ((j - s % 4) // 4) + 16)
                    wait(pe, bxT_done, j - 1)
                    for k in range(KT):
                        last = nc.tensor.transpose(ps[:, 0 + s % 2, k * P:(k + 1) * P], xg[:, s % 4, k * P:(k + 1) * P], ident[:, :])
                    last.then_inc(bt_done, 1)
                if lo <= 1 <= hi:
                    e = pe.value_load(eblki[0:1, ds(j - 1, 1)], min_val=0, max_val=E - 1)
                    wait(pe, bxT_done, j)
                    wait(pe, bhid_done, j - 2)
                    for k in range(KT):
                        last = nc.tensor.matmul(ps[:, 2 + (s - 1) % 2, :], xgT[:, k, (s - 1) % 4, :], egu_v[:, ds(e, 1), k, :],
                                                start=(k == 0), stop=(k == KT - 1))
                    last.then_inc(bgu_done, 1)
                if lo <= 2 <= hi:
                    wait(pe, bhid_done, j - 1)
                    wait(pe, bhT_done, j - 3)
                    for k in range(KT):
                        last = nc.tensor.transpose(ps[:, 4 + s % 2, k * P:(k + 1) * P], hid[:, s % 2, k * P:(k + 1) * P], ident[:, :])
                    last.then_inc(bht_done, 1)
                if lo <= 3 <= hi:
                    e = pe.value_load(eblki[0:1, ds(j - 3, 1)], min_val=0, max_val=E - 1)
                    wait(pe, bhT_done, j - 2)
                    wait(pe, by_copied, j - 4)
                    for k in range(KT):
                        last = nc.tensor.matmul(ps[:, 6 + (s - 3) % 2, 0:D], hidT[:, k, (s - 3) % 4, :], edn_v[:, ds(e, 1), k, :],
                                                start=(k == 0), stop=(k == KT - 1))
                    last.then_inc(by_done, 1)

            for j in range(8):
                step(j, j % 4, 0, j)
            with pe.Fori(2, NBLK // 4) as i:
                for s in range(4):
                    step(i * 4 + s, s)
            for j in range(3):
                step(NBLK + j, j, j + 1, 3)

        @block.scalar
        def _(act):
            act.wait_ge(c_in, 32)
            act.activation(csT[:, :, :], cT[:, :, :], ACT.Silu).then_inc(silu_done, 1)
            act.wait_ge(small_in, 64)
            act.wait_ge(iota_done, 1)

            def copy_modulation(i):
                b, n = i % B, i // B
                act.wait_ge(modr_mm, i + 1)
                act.activation(modr[:, b, 2 * n:2 * n + 2, :].rearrange("p s d -> p (s d)"), ps[:, MOD_BANK[i], :],
                               ACT.Copy).then_inc(modr_copied, 1)

            def copy_h2T(g, k):
                wait(act, tp2_done, KT * g + k + 1)
                act.activation(h2T[:, k, :], ps[:, TP, :], ACT.Copy).then_inc(h2T_done, 1)

            def table_phases(m):
                w, cb = m // CB, m % CB
                wait(act, tab_done, m)
                act.activation(phi[:, :], trow[:, w * WIN:(w + 1) * WIN], ACT.Copy,
                               scale=fcol[:, cb:cb + 1]).then_inc(phi_done, 1)
                act.wait_ge(phi_done, m + 1)
                act.activation(nphi[:, :], phi[:, :], ACT.Copy, scale=1.0 / TWO_PI, bias=MAGIC).then_inc(nphi_mid, 1)
                act.wait_ge(nphi_mid, m + 1)
                act.activation(nphi[:, :], nphi[:, :], ACT.Copy, bias=-MAGIC).then_inc(nphi_done, 1)

            def table(m):
                wait(act, phir_done, m + 1)
                act.activation(nphi[:, :], phi[:, :], ACT.Abs).then_inc(phia_done, 1)
                if m >= CB:
                    wait(act, fpos_done, (B - 1) * CB + m % CB + 1)
                act.activation(tab[:, m % CB, 1, :], phi[:, :], ACT.Sin)
                act.wait_ge(phia_done, m + 1)
                act.activation(tab[:, m % CB, 0, :], nphi[:, :], ACT.Sin, scale=-1.0, bias=HALF_PI).then_inc(tab_done, 1)
                if m + 1 < NW * CB:
                    table_phases(m + 1)

            def copy_hT(g, b, k):
                wait(act, tp1_done, KT * g + k + 1)
                apart(act, b)
                act.activation(hT[:, ds(b % 2, 1), k, :].rearrange("p s t -> p (s t)"), ps[:, TP, :], ACT.Identity,
                               scale=modc[:, KT + k, ds(b, 1)], bias=modc[:, k, ds(b, 1)]).then_inc(hT_done, 1)

            def ln_apply(dst, src, rs, sh, shifted, n, done):
                wait(act, shifted, n)
                for q in range(Q):
                    last = act.activation(dst[:, q, :], src[:, q, :], ACT.Identity, scale=rs[:, q:q + 1], bias=sh[:, q:q + 1])
                last.then_inc(done, 1)

            def copy_logits(g, b, w):
                wait(act, lg_done, g + 1)
                apart(act, g)
                act.activation(logits[:, ds(b * TB + w * Q, Q), :],
                               ps[:, MISC, 0:Q * E].rearrange("p (q e) -> p q e", q=Q), ACT.Copy).then_inc(lg_copied, 1)

            table_phases(0)
            ln_apply(xa, xa, rs1, sh1, rstd1_done, 2, xn_done)
            act.wait_ge(modc_done, 1)
            for k in range(KT):
                copy_hT(0, 0, k)
            table(0)

            def body(w, b, wp, bp, wn, bn):
                g = w * B + b
                u0 = g * CB
                for cb in range(CB):
                    u = u0 + cb
                    s = cb % 2
                    wait(act, v_done, u + 1)
                    wait(act, dpos_done, u - 1)
                    act.activation(vg[:, s, :], ps[:, V + s, :], ACT.Copy, scale=gcol[:, cb, 0:1]).then_inc(vcopy_done, 1)
                    wait(act, k_done, u + 1)
                    wait(act, r_done, u)
                    wait(act, trig_done, u)
                    act.activation(t_t[:, :], ps[:, U, :], ACT.Copy, bias=MAGIC).then_inc(t_done, 1)
                    lb, lc = (b, cb - 1) if cb else (bp, CB - 1)
                    if w == 0 and (cb or wp is not None):
                        act.activation(tcarry[:, ds(lb, 1), lc, :].rearrange("p a r -> p r a"),
                                       trig[:, 1 - s, :, WIN:WIN + 1], ACT.Copy)
                    if w == 1 and isinstance(b, int) and b == 0 and cb == 0:
                        act.activation(tcarry[:, B - 1:B, CB - 1, :].rearrange("p a r -> p r a"),
                                       trig[:, 1 - s, :, WIN:WIN + 1], ACT.Copy)
                    m = table_of(w, b, cb)
                    if wp is None and cb in MOD_STEP:
                        for i in MOD_STEP[cb]:
                            copy_modulation(i)
                    if cb == 1 and wn is not None:
                        ln_apply(xa, xa, rs1, sh1, rstd1_done, 2 * (g + 2), xn_done)
                    if cb in (4, 5) and wn is not None:
                        copy_hT(g + 1, bn, cb - 4)
                    if cb == 3 and wp is not None:
                        ln_apply(h2, xr, rs2, sh2, rstd2_done, 2 * g, h2n_done)
                    if cb in (6, 7) and wp is not None:
                        copy_h2T(g - 1, cb - 6)
                    wait(act, r_done, u + 1)
                    wait(act, fassoc_done, u - 1)
                    act.activation(a_t[:, :], r_t[:, :], ACT.Abs).then_inc(abs_done, 1)
                    act.activation(trig[:, s, 1, 1:WIN + 1], r_t[:, :], ACT.Sin, scale=-TURN)
                    act.activation(trig[:, s, :, 0:1], tcarry[:, ds(b, 1), cb, :].rearrange("p a r -> p r a"),
                                   ACT.Copy)
                    act.wait_ge(abs_done, u + 1)
                    act.activation(trig[:, s, 0, 1:WIN + 1], a_t[:, :], ACT.Sin, scale=-TURN, bias=HALF_PI).then_inc(trig_done, 1)
                    if m is not None:
                        table(m)
                    if cb == 7 and wp is not None:
                        copy_logits(g - 1, bp, wp)

            bodies(act, body)
            for k in range(KT):
                copy_h2T(NG - 1, k)
            copy_logits(NG - 1, B - 1, NW - 1)
            act.wait_ge(rt_exp_in, 1)
            act.activation(expo, expo, ACT.Exp).then_inc(rt_exp, 1)
            act.activation(wgt[:, 1, :], m1[:, 1, :], ACT.Exp).then_inc(rt_exp, 1)

            def step(j, s, lo=0, hi=3):
                if lo <= 1 <= hi:
                    wait(act, bgu_done, j)
                    wait(act, bhid_done, j - 2)
                    act.activation(sg[:, (s - 1) % 2, :], ps[:, 2 + (s - 1) % 2, 0:EH], ACT.Silu).then_inc(bsilu_done, 1)
                if lo <= 2 <= hi:
                    wait(act, bht_done, j - 1)
                    wait(act, by_done, j - 4)
                    act.activation(hidT[:, :, (s - 2) % 4, :], ps[:, 4 + s % 2, 0:2 * P].rearrange("p (k m) -> p k m", k=KT),
                                   ACT.Copy).then_inc(bhT_done, 1)
                if lo <= 3 <= hi:
                    wait(act, by_done, j - 2)
                    if isinstance(j, int):
                        wait(act, ystor[(s - 3) % 4], 16 * ((j - 3) // 4))
                    else:
                        act.wait_ge(ystor[(s - 3) % 4], 4 * (j - 3 - (s - 3) % 4))
                    act.activation(ysb[:, (s - 3) % 4, :], ps[:, 6 + (s - 3) % 2, 0:D], ACT.Copy).then_inc(by_copied, 1)

            act.wait_ge(x2_out, 16 * NG)
            for j in range(8):
                step(j, j % 4, 0, j)
            with act.Fori(2, NBLK // 4) as i:
                for s in range(4):
                    step(i * 4 + s, s)
            for j in range(3):
                step(NBLK + j, j, j + 1, 3)

        @block.vector
        def _(dve):
            v = nc.vector
            chain = [0]

            def link(ins, s=pc_chain):
                chain[0] += 1
                ins.then_inc(s, 1)
                dve.wait_ge(s, chain[0])

            v.memset(one[:, :], 1.0)
            v.memset(mhalf[:, :], -0.5)
            link(v.memset(tcarry[:, :, :, :], 0.0))
            def ln_sums(src, g, chain_):
                for q in range(Q):
                    last = v.bn_stats(bnst[:, q, :], src[:, q, :])
                last.then_inc(chain_, 1)

            def ln_mean_var(mv, g, chain_):
                wait(dve, chain_, 2 * g + 1)
                apart(dve, g)
                for q in range(Q):
                    last = v.bn_aggr(mv[:, q, :], bnst[:, q, :])
                last.then_inc(chain_, 1)

            def ln_var_eps(mv, ve, nm, g, chain_, done):
                wait(dve, chain_, 2 * g + 2)
                v.tensor_scalar(ve[:, :], mv[:, :, 1], EPS, None, ALU.add)
                v.tensor_scalar(nm[:, :], mv[:, :, 0], -1.0, None, ALU.mult).then_inc(done, 1)

            def read_heads(g, b, w):
                wait(dve, wo_done, CB * (g + 1))
                wait(dve, h2_out, 16 * g)
                for q in range(Q):
                    last = v.scalar_tensor_tensor(h2[:, q, :], ps[:, WO + q // 2, (q % 2) * D:(q % 2 + 1) * D],
                                                  isq[:, w * Q + q:w * Q + q + 1], modr[:, ds(b, 1), GA, :], ALU.mult, ALU.mult)
                last.then_inc(wo_read, 1)

            def add_heads(g):
                wait(dve, wo_read, g + 1)
                wait(dve, xr_in, 16 * (g + 1))
                v.tensor_tensor(xr[:, :, :], xr[:, :, :], h2[:, :, :], ALU.add).then_inc(x2_done, 1)

            def turns(u):
                wait(dve, t_done, u + 1)
                wait(dve, trig_done, u)
                v.scalar_tensor_tensor(r_t[:, :], t_t[:, :], MAGIC, ps[:, U, :], ALU.subtract, ALU.subtract).then_inc(r_done, 1)

            def assoc_products(u, s):
                wait(dve, trig_done, u + 1)
                wait(dve, vcopy_done, u + 1)
                wait(dve, parts_done, u)
                v.tensor_tensor(ps[:, A:A + 2, :], ps[:, V + s:V + s + 1, :].to_broadcast([P, 2, WIN]), trig[:, s, :, 0:WIN],
                                ALU.mult).then_inc(dassoc_done, 1)

            def sums(rows, w, b, cb, r0):
                for r in range(2):
                    last = v.tensor_tensor_scan(rows[:, r, :], one[:, 0:1].to_broadcast([P, WIN]), rows[:, r, :],
                                                scarry[:, ds(b, 1), cb, r0 + r] if w else 0.0, ALU.mult, ALU.add)
                return last

            def keep_sums(rows, b, cb, r0):
                return v.tensor_scalar(scarry[:, ds(b, 1), cb, r0:r0 + 2].rearrange("p a r -> p r a"),
                                       rows[:, :, WIN - 1:WIN], 1.0, None, ALU.mult)

            def pos_sums(u, s, w, b, cb):
                wait(dve, dpos_done, u + 1)
                sums(prod[:, s, :, :], w, b, cb, 0).then_inc(carry_done if w == NW - 1 else spos_done, 1)

            def keep_pos(u, s, w, b, cb):
                if w < NW - 1:
                    wait(dve, spos_done, u + 1)
                    keep_sums(prod[:, s, :, :], b, cb, 0).then_inc(carry_done, 1)

            def assoc_sums(u, w, b, cb):
                wait(dve, dassoc_done, u + 1)
                sums(ps[:, A:A + 2, :], w, b, cb, 2).then_inc(sassoc_done, 1)

            def keep_assoc(u, w, b, cb):
                if w < NW - 1:
                    wait(dve, sassoc_done, u + 1)
                    keep_sums(ps[:, A:A + 2, :], b, cb, 2).then_inc(kept_done, 1)

            def assoc_probe(u, s, w, cb):
                if w < NW - 1:
                    wait(dve, kept_done, u + 1)
                else:
                    wait(dve, sassoc_done, u + 1)
                v.scalar_tensor_tensor(ps[:, A:A + 2, :], ps[:, A:A + 2, :], gcol[:, cb, 1:2], trig[:, s, :, 1:WIN + 1],
                                       ALU.mult, ALU.mult).then_inc(fassoc_done, 1)

            def add_positions(u, s):
                wait(dve, fpos_done, u + 1)
                wait(dve, fassoc_done, u + 1)
                wait(dve, wo_done, u - 1)
                v.tensor_tensor(parts[:, s, :, :], ps[:, A:A + 2, :], prod[:, s, :, :], ALU.add).then_inc(parts_done, 1)

            def table_angles(m, part):
                if part == 0:
                    wait(dve, nphi_done, m + 1)
                    v.scalar_tensor_tensor(phi[:, :], nphi[:, :], -C1, phi[:, :], ALU.mult, ALU.add).then_inc(phir_mid, 1)
                elif part == 1:
                    wait(dve, phir_mid, 2 * m + 1)
                    v.scalar_tensor_tensor(phi[:, :], nphi[:, :], -C2, phi[:, :], ALU.mult, ALU.add).then_inc(phir_mid, 1)
                else:
                    wait(dve, phir_mid, 2 * m + 2)
                    v.tensor_scalar(phi[:, :], phi[:, :], PI, -PI, ALU.min, ALU.max).then_inc(phir_done, 1)

            dve.wait_ge(xa_in, 16)
            ln_sums(xa, 0, ln1_chain)
            ln_mean_var(mv1, 0, ln1_chain)
            ln_var_eps(mv1, ve1, nm1, 0, ln1_chain, var1_done)
            for part in range(3):
                table_angles(0, part)
            dve.wait_ge(modc_mm, 1)
            link(v.tensor_copy(modc[:, :, :], ps[:, MISC, 0:2 * KT * B].rearrange("p (j b) -> p j b", b=B)))
            v.tensor_scalar(modc[:, KT:2 * KT, :], modc[:, KT:2 * KT, :], 1.0, None, ALU.add).then_inc(modc_done, 1)
            dve.wait_ge(wk_in, 16)
            v.tensor_scalar(wk[:, :, :], wk[:, :, :], PHASE / TWO_PI, None, ALU.mult).then_inc(wk_scaled, 1)
            dve.wait_ge(silu_done, 1)
            v.tensor_copy(csb, csT[:, :, :].unsqueeze(3).to_broadcast([P, KT, B, P])).then_inc(csb_done, 1)

            sgn = xgT_flat[:, :].rearrange("p (b d) -> p b d", b=B)
            mod_chain = [0]

            def finish_modulation(which, part):
                m = modr[:, :, which, :]
                dve.wait_ge(modr_copied, 4 if which == GA else 8)
                wait(dve, modr_done, mod_chain[0])
                if which == CB1:
                    ins = v.tensor_scalar(m, m, 1.0, None, ALU.add)
                elif part == 0:
                    ins = v.tensor_scalar(sgn, m, 0.0, 2.0, ALU.is_ge, ALU.mult)
                elif part == 1:
                    ins = v.scalar_tensor_tensor(m, m, -1.0, m, ALU.mult, ALU.max)
                elif part == 2:
                    ins = v.tensor_scalar(m, m, 0.25, None, ALU.max)
                else:
                    ins = v.scalar_tensor_tensor(m, sgn, 1.0, m, ALU.subtract, ALU.mult)
                ins.then_inc(modr_done, 1)
                mod_chain[0] += 1

            MOD_WORK = {(2, 1): (GA, 0), (3, 1): (GA, 1), (4, 1): (GA, 2), (5, 0): (GA, 3), (5, 1): (CB1, 0),
                        (6, 0): (GB, 0), (6, 1): (GB, 1), (7, 0): (GB, 2), (7, 1): (GB, 3)}

            def body(w, b, wp, bp, wn, bn):
                g = w * B + b
                u0 = g * CB
                for cb in range(CB):
                    u = u0 + cb
                    s = cb % 2
                    lw, lb, lc = (w, b, cb - 1) if cb else (wp, bp, CB - 1)
                    if lw is None:
                        turns(u)
                        for part in range(3):
                            table_angles(1, part)
                        wait(dve, xa_in, 16 * (g + 2))
                        ln_sums(xa, g + 1, ln1_chain)
                        ln_mean_var(mv1, g + 1, ln1_chain)
                        ln_var_eps(mv1, ve1, nm1, g + 1, ln1_chain, var1_done)
                        continue
                    m = table_of(w, b, cb)
                    pos_sums(u - 1, 1 - s, lw, lb, lc)
                    assoc_products(u - 1, 1 - s)
                    if m is not None:
                        table_angles(m, 0)
                    keep_pos(u - 1, 1 - s, lw, lb, lc)
                    if cb == 2 and wp is not None:
                        wait(dve, x2_done, g)
                        ln_sums(xr, g - 1, ln2_chain)
                    if cb == 0 and wn is not None:
                        wait(dve, xa_in, 16 * (g + 2))
                        ln_sums(xa, g + 1, ln1_chain)
                    assoc_sums(u - 1, lw, lb, lc)
                    if m is not None:
                        table_angles(m, 1)
                    if wp is None and (cb, 0) in MOD_WORK:
                        finish_modulation(*MOD_WORK[cb, 0])
                    if cb == 1 and wp is not None:
                        read_heads(g - 1, bp, wp)
                    if cb == 2 and wp is not None:
                        ln_mean_var(mv2, g - 1, ln2_chain)
                    if cb == 0 and wn is not None:
                        ln_mean_var(mv1, g + 1, ln1_chain)
                    keep_assoc(u - 1, lw, lb, lc)
                    if cb == 2 and wp is not None:
                        ln_var_eps(mv2, ve2, nm2, g - 1, ln2_chain, var2_done)
                    if cb == 0 and wn is not None:
                        ln_var_eps(mv1, ve1, nm1, g + 1, ln1_chain, var1_done)
                    turns(u)
                    if m is not None:
                        table_angles(m, 2)
                    if wp is None and (cb, 1) in MOD_WORK:
                        finish_modulation(*MOD_WORK[cb, 1])
                        if cb == 7:
                            dve.wait_ge(modr_done, 9)
                    if cb == 1 and wp is not None:
                        add_heads(g - 1)
                    assoc_probe(u - 1, 1 - s, lw, lc)
                    add_positions(u - 1, 1 - s)

            bodies(dve, body)
            s = (CB - 1) % 2
            pos_sums(NU - 1, s, NW - 1, B - 1, CB - 1)
            assoc_products(NU - 1, s)
            assoc_sums(NU - 1, NW - 1, B - 1, CB - 1)
            assoc_probe(NU - 1, s, NW - 1, CB - 1)
            add_positions(NU - 1, s)
            read_heads(NG - 1, B - 1, NW - 1)
            add_heads(NG - 1)
            dve.wait_ge(x2_done, NG)
            ln_sums(xr, NG - 1, ln2_chain)
            ln_mean_var(mv2, NG - 1, ln2_chain)
            ln_var_eps(mv2, ve2, nm2, NG - 1, ln2_chain, var2_done)
            dve.wait_ge(rstd2_done, 2 * NG)
            for q in range(Q):
                last = v.tensor_scalar(h2[:, q, :], xr[:, q, :], rs2[:, q:q + 1], sh2[:, q:q + 1], ALU.mult, ALU.add)
            last.then_inc(h2n_done, 1)
            dve.wait_ge(h2n_done, NG)
            v.tensor_tensor(h2[:, :, :], h2[:, :, :], modr[:, B - 1:B, CB1, :].to_broadcast([P, Q, D]), ALU.mult).then_inc(h2c_done, 1)
            dve.wait_ge(h2c_done, NG)
            v.tensor_tensor(h2[:, :, :], h2[:, :, :], modr[:, B - 1:B, SB_, :].to_broadcast([P, Q, D]), ALU.add).then_inc(h2_done, 1)

            chain[0] = 0

            def step_(ins):
                link(ins, rt)

            def over_e(ap):
                return ap.unsqueeze(2).to_broadcast([P, NT, E])

            dve.wait_ge(rt_iota, 4)
            dve.wait_ge(lg_copied, NG)
            dve.wait_ge(parts_done, NU)
            dve.wait_ge(wo_done, NU)
            dve.wait_ge(trig_done, NU)
            e_row = e16.unsqueeze(1).to_broadcast([P, NT, E])
            src = logits[:, :, :]
            for k in range(2):
                step_(v.tensor_reduce(m1[:, k, :], src, AX.X, ALU.max))
                step_(v.tensor_tensor(eqt, src, over_e(m1[:, k, :]), ALU.is_equal))
                step_(v.tensor_scalar(eqt, eqt, -1.0, -float(E), ALU.add, ALU.mult))
                step_(v.tensor_tensor(eqt, eqt, e_row, ALU.add))
                step_(v.tensor_reduce(first[:, :], eqt, AX.X, ALU.min))
                step_(v.tensor_tensor(oh[:, k, :, :], e_row, over_e(first[:, :]), ALU.is_equal))
                if k == 0:
                    step_(v.scalar_tensor_tensor(lmask, oh[:, k, :, :], NEG, src, ALU.mult, ALU.add))
                    src = lmask
            v.tensor_copy(ohb.rearrange("p k (n e) -> p k n e", n=NT), oh).then_inc(rt_onehot, 1)
            step_(v.tensor_tensor(expo, logits[:, :, :], over_e(m1[:, 0, :]), ALU.subtract))
            step_(v.tensor_tensor(m1[:, 1, :], m1[:, 1, :], m1[:, 0, :], ALU.subtract))
            v.memset(segm, 1.0).then_inc(rt_exp_in, 1)
            dve.wait_ge(rt_exp_in, 1)
            step_(v.memset(segm[:, :, :, 0:1], 0.0))
            dve.wait_ge(rt_rank, 1)
            for k in range(2):
                step_(v.tensor_copy(tot[:, k, :, :], ps[:, 2 * k + 1, :].rearrange("p (n e) -> p e n", n=NT)))
            step_(v.tensor_tensor_scan(incl.rearrange("p k e n -> p (k e n)"), segm.rearrange("p k e n -> p (k e n)"),
                                       tot.rearrange("p k e n -> p (k e n)"), 0.0, ALU.mult, ALU.add))
            step_(v.tensor_tensor(tot, incl, tot, ALU.subtract))
            for k in range(2):
                step_(v.tensor_tensor(rank[:, k, :, :], ps[:, 2 * k, :].rearrange("p (n e) -> p n e", n=NT),
                                      tot[:, k, :, :].rearrange("p e n -> p n e"), ALU.add))
            step_(v.tensor_scalar(kept[:, :, :], incl[:, :, :, NT - 1], float(CAP), None, ALU.min))
            step_(v.tensor_tensor(nexp[:, :], kept[:, 0, :], kept[:, 1, :], ALU.add))
            step_(v.tensor_scalar(nexpi[:, :], nexp[:, :], float(P - 1), None, ALU.add))
            step_(v.tensor_scalar(nexpi[:, :], nexpi[:, :], 7, None, ALU.logical_shift_right))
            step_(v.tensor_copy(nblkf[:, :], nexpi[:, :]))
            step_(v.tensor_tensor_scan(bend[:, :], one[:, 0:1].to_broadcast([P, E]), nblkf[:, :], 0.0, ALU.mult, ALU.add))
            step_(v.tensor_tensor(nexp[:, :], bend[:, :], nblkf[:, :], ALU.subtract))
            step_(v.tensor_scalar(aoff[:, 0, :], nexp[:, :], float(P), None, ALU.mult))
            step_(v.tensor_tensor(aoff[:, 1, :], aoff[:, 0, :], kept[:, 0, :], ALU.add))
            for k in range(2):
                step_(v.tensor_tensor(eqt, oh[:, k, :, :], rank[:, k, :, :], ALU.mult))
                step_(v.tensor_reduce(rsel[:, k, :], eqt, AX.X, ALU.add))
                step_(v.tensor_tensor(eqt, oh[:, k, :, :], aoff[:, k:k + 1, :].to_broadcast([P, NT, E]), ALU.mult))
                step_(v.tensor_reduce(slot[:, k, :], eqt, AX.X, ALU.add))
            step_(v.tensor_scalar(keep[:, :, :], rsel[:, :, :], float(CAP), None, ALU.is_lt))
            step_(v.tensor_tensor(slot[:, :, :], slot[:, :, :], rsel[:, :, :], ALU.add))
            step_(v.tensor_tensor(slot[:, :, :], slot[:, :, :], keep[:, :, :], ALU.mult))
            step_(v.tensor_copy(gsi[:, :, :].rearrange("p n k -> p k n"), slot[:, :, :]))
            step_(v.tensor_scalar(smap[:, :, :], keep[:, :, :], -float(P * (P - 1)), float(P * (P - 1)), ALU.mult, ALU.add))
            step_(v.tensor_tensor(sloti[:, :, :], smap[:, :, :], slot[:, :, :], ALU.add))
            step_(v.tensor_scalar(posi[:, :, :], sloti[:, :, :], P - 1, None, ALU.bitwise_and))
            step_(v.tensor_copy(posf[:, :, :], posi[:, :, :]))
            step_(v.tensor_scalar(posi[:, :, :], sloti[:, :, :], 7, None, ALU.logical_shift_right))
            step_(v.tensor_copy(blkf[:, :, :], posi[:, :, :]))
            def hot_four(i, first):
                for s in range(4):
                    n, k = i * 2 + s // 2, s % 2
                    if not first:
                        dve.wait_ge(map_mm, i * 4 + s - 3)
                    v.tensor_scalar(pos_hot[:, s, :], iota_p, posf[:, k, ds(n, 1)], None, ALU.is_equal)
                    v.tensor_scalar(blk_hot[:, s, :], iota_p, blkf[:, k, ds(n, 1)], tokf[:, ds(n, 1)],
                                    ALU.is_equal, ALU.mult).then_inc(hot_done, 1)

            hot_four(0, True)
            with dve.Fori(1, NT // 2) as i:
                hot_four(i, False)
            step_(v.memset(eblk[:, :], 0.0))
            for e in range(E - 1):
                step_(v.scalar_tensor_tensor(eblk[:, :], iota_p, bend[:, e:e + 1], eblk[:, :], ALU.is_ge, ALU.add))
            v.tensor_copy(eblki[:, :], eblk[:, :]).then_inc(exps_done, 1)
            dve.wait_ge(map_mm, 2 * NT)
            v.tensor_copy(mapi[:, :], ps[:, MISC, 0:P]).then_inc(map_done, 1)
            dve.wait_ge(rt_exp, 2)
            step_(v.tensor_reduce(zsum[:, :], expo, AX.X, ALU.add))
            step_(v.reciprocal(wgt[:, 0, :], zsum[:, :]))
            step_(v.tensor_tensor(wgt[:, 1, :], wgt[:, 1, :], wgt[:, 0, :], ALU.mult))
            step_(v.tensor_tensor(wgt[:, :, :], wgt[:, :, :], keep[:, :, :], ALU.mult))

            def step(j, s, lo=0, hi=3):
                if lo <= 0 <= hi:
                    wait(dve, bt_done, j + 1)
                    wait(dve, bgu_done, j - 3)
                    v.tensor_copy(xgT[:, :, s % 4, :], ps[:, 0 + s % 2, 0:2 * P].rearrange("p (k m) -> p k m", k=KT)).then_inc(bxT_done, 1)
                if lo <= 1 <= hi:
                    wait(dve, bsilu_done, j)
                    wait(dve, bht_done, j - 2)
                    v.tensor_tensor(hid[:, (s - 1) % 2, :], sg[:, (s - 1) % 2, :], ps[:, 2 + (s - 1) % 2, EH:2 * EH],
                                    ALU.mult).then_inc(bhid_done, 1)

            for j in range(8):
                step(j, j % 4, 0, j)
            with dve.Fori(2, NBLK // 4) as i:
                for s in range(4):
                    step(i * 4 + s, s)
            step(NBLK, 0, 1, 3)

            with dve.Fori(0, B) as b:
                for nn in range(TB):
                    n = b * TB + nn
                    s = nn % 4
                    dve.wait_ge(yg[s], (b * (TB // 4) + nn // 4) * 32 + 32)
                    v.tensor_scalar(y0[:, s, :], y0[:, s, :], wgt[:, 0, ds(n, 1)], None, ALU.mult).then_inc(cw0_done, 1)
                    dve.wait_ge(cw0_done, n + 1)
                    v.scalar_tensor_tensor(y0[:, s, :], y1[:, s, :], wgt[:, 1, ds(n, 1)], y0[:, s, :], ALU.mult,
                                           ALU.add).then_inc(cw1_done, 1)
                    dve.wait_ge(cw1_done, n + 1)
                    v.tensor_tensor(y0[:, s, :], y0[:, s, :], modr[:, ds(b, 1), GB, :], ALU.mult).then_inc(cgb_done, 1)
                    dve.wait_ge(cgb_done, n + 1)
                    dve.wait_ge(xf_in[s], (b * (TB // 4) + nn // 4) * 16 + 16)
                    v.tensor_tensor(xf[:, s, :], xf[:, s, :], y0[:, s, :], ALU.add).then_inc(csum_done, 1)

        @block.gpsimd
        def _(pool):
            gp = nc.gpsimd
            gp.memset(ident[:, :], 0.0).then_inc(ident_done, 1)
            gp.iota(trow[:, :], [[1, T]], base=0, channel_multiplier=0, allow_small_or_imprecise_dtypes=True).then_inc(iota_done, 1)
            gp.iota(tcol[:, :], [[P, TB]], base=1, channel_multiplier=1, allow_small_or_imprecise_dtypes=True).then_inc(isq_done, 1)
            gp.iota(tokf[:, :], [[P, NT]], base=0, channel_multiplier=1, allow_small_or_imprecise_dtypes=True)
            pool.wait_ge(ident_done, 1)
            gp.affine_select(out=ident[:, :], in_=ident[:, :], compare_op=ALU.not_equal, fill=1.0, base=0,
                             pattern=[[-1, P]], channel_multiplier=1).then_inc(ident_done, 1)
            pool.wait_ge(pc_chain, 1)
            pool.wait_ge(isq_done, 1)
            gp.tensor_tensor(isq[:, :], tcol[:, :], mhalf[:, :], ALU.pow).then_inc(isq_done, 1)

            def rstd(var, rs, sh, ve, nm, n, done):
                wait(pool, var, n)
                gp.tensor_tensor(rs[:, :], ve[:, :], mhalf[:, 0:Q], ALU.pow).then_inc(done, 1)
                wait(pool, done, 2 * n - 1)
                gp.tensor_tensor(sh[:, :], nm[:, :], rs[:, :], ALU.mult).then_inc(done, 1)

            def modulate_cb(g, b):
                wait(pool, h2n_done, g + 1)
                apart(gp, g)
                gp.tensor_tensor(h2[:, :, :], h2[:, :, :], modr[:, ds(b, 1), CB1, :].to_broadcast([P, Q, D]),
                                 ALU.mult).then_inc(h2c_done, 1)

            def modulate_sb(g, b):
                wait(pool, h2c_done, g + 1)
                apart(gp, g)
                gp.tensor_tensor(h2[:, :, :], h2[:, :, :], modr[:, ds(b, 1), SB_, :].to_broadcast([P, Q, D]),
                                 ALU.add).then_inc(h2_done, 1)

            def pos_products(u, s, cb, w):
                wait(pool, vcopy_done, u + 1)
                wait(pool, tab_done, w * CB + cb + 1)
                wait(pool, parts_done, u - 1)
                gp.tensor_tensor(prod[:, s, :, :], vg[:, s:s + 1, :].to_broadcast([P, 2, WIN]), tab[:, cb, :, :],
                                 ALU.mult).then_inc(dpos_done, 1)

            def pos_probe(u, s, cb):
                wait(pool, carry_done, u + 1)
                gp.tensor_tensor(prod[:, s, :, :], prod[:, s, :, :], tab[:, cb, :, :], ALU.mult).then_inc(fpos_done, 1)

            rstd(var1_done, rs1, sh1, ve1, nm1, 1, rstd1_done)

            def body(w, b, wp, bp, wn, bn):
                g = w * B + b
                u0 = g * CB
                for cb in range(CB):
                    u = u0 + cb
                    s = cb % 2
                    lw, lc = (w, cb - 1) if cb else (wp, CB - 1)
                    pos_products(u, s, cb, w)
                    if lw is not None:
                        pos_probe(u - 1, 1 - s, lc)
                    if cb == 0 and wn is not None:
                        rstd(var1_done, rs1, sh1, ve1, nm1, g + 2, rstd1_done)
                    if cb == 2 and wp is not None:
                        rstd(var2_done, rs2, sh2, ve2, nm2, g, rstd2_done)
                    if cb == 3 and wp is not None:
                        modulate_cb(g - 1, bp)
                    if cb == 4 and wp is not None:
                        modulate_sb(g - 1, bp)

            bodies(pool, body)
            pos_probe(NU - 1, (CB - 1) % 2, CB - 1)
            rstd(var2_done, rs2, sh2, ve2, nm2, NG, rstd2_done)

            pool.wait_ge(trig_done, NU)
            gp.iota(iota_p, [[1, P]], base=0, channel_multiplier=0, allow_small_or_imprecise_dtypes=True).then_inc(rt_iota, 1)
            gp.iota(e16, [[1, E]], base=-E, channel_multiplier=0, allow_small_or_imprecise_dtypes=True).then_inc(rt_iota, 1)
            gp.memset(onesb, 1.0).then_inc(rt_iota, 1)
            pool.wait_ge(rt_iota, 3)
            gp.affine_select(out=triu, in_=onesb, compare_op=ALU.is_gt, fill=0.0, base=0,
                             pattern=[[1, P]], channel_multiplier=-1).then_inc(rt_iota, 1)

            pool.wait_ge(map_done, 1)
            pool.wait_ge(h2_out, 16 * NG)

            def gather(j, s, first_round):
                if not first_round:
                    pool.wait_ge(gath[s], 4 * (j - s))
                    pool.wait_ge(bt_done, j - 3)
                wait(pool, carried, j)
                gp.tensor_copy(idxc[:, s, 0:1], mapi[:, ds(j, 1)]).then_inc(idx_done, 1)
                pool.wait_ge(idx_done, j + 1)
                gp.tensor_tensor(spare[:, 4:5], one[:, 0:1], one[:, 0:1], ALU.mult).then_inc(carried, 1)
                gp.indirect_dma_start(out=xg[:, s, :], out_offset=None, in_=h2_d,
                                      in_offset=bass.IndirectOffsetOnAxis(ap=idxc[:, s, 0:1], axis=0)).then_inc(gath[s], 16)

            for j in range(4):
                gather(j, j, True)
            with pool.Fori(1, NBLK // 4) as i:
                for s in range(4):
                    gather(i * 4 + s, s, False)

            for s in range(4):
                pool.wait_ge(ystor[s], 16 * (NBLK // 4))
            pool.wait_ge(gath[3], 16 * (NBLK // 4))

            def gather_y(n, s, first_round):
                if not first_round:
                    pool.wait_ge(csum_done, n - 3)
                wait(pool, carried, NBLK + n)
                gp.tensor_copy(idxc[:, s, :], gsi[:, ds(n, 1), :].rearrange("p a k -> p (a k)")).then_inc(cidx_done, 1)
                pool.wait_ge(cidx_done, n + 1)
                gp.tensor_tensor(spare[:, 4:5], one[:, 0:1], one[:, 0:1], ALU.mult).then_inc(carried, 1)
                gp.indirect_dma_start(out=y0[:, s, :], out_offset=None, in_=y_d,
                                      in_offset=bass.IndirectOffsetOnAxis(ap=idxc[:, s, 0:1], axis=0)).then_inc(yg[s], 16)
                gp.indirect_dma_start(out=y1[:, s, :], out_offset=None, in_=y_d,
                                      in_offset=bass.IndirectOffsetOnAxis(ap=idxc[:, s, 1:2], axis=0)).then_inc(yg[s], 16)

            for n in range(4):
                gather_y(n, n, True)
            with pool.Fori(1, NT // 4) as i:
                for s in range(4):
                    gather_y(i * 4 + s, s, False)


_INS = ['L0_attn_x', 'L0_attn_Wk', 'L0_attn_Wv', 'L0_attn_Wo', 'L0_attn_gate', 'L0_attn_freqs', 'L0_ffn_router_w',
        'L0_ffn_gate_w', 'L0_ffn_up_w', 'L0_ffn_down_w', 'L0_c', 'L0_wmod']
_OUTS = [((4, 1024, 256), 'float32')]


def kernel(**inputs):
    import numpy as _np
    import concourse.bacc as _bacc
    from concourse import mybir as _mybir
    from concourse.bass_utils import run_bass_kernel_spmd as _run

    nc = _bacc.Bacc("TRN2", target_bir_lowering=False, num_devices=1)
    arrays, args = {}, []
    for name in _INS:
        a = _np.ascontiguousarray(inputs[name])
        arrays[f"in_{name}_dram"] = a
        args.append(nc.dram_tensor(f"in_{name}_dram", a.shape, _mybir.dt.from_np(a.dtype), kind="ExternalInput").ap())
    for i, (shape, dtype) in enumerate(_OUTS):
        dt = _mybir.dt.from_np(_np.dtype(dtype))
        args.append(nc.dram_tensor(f"out_{i}_dram", shape, dt, kind="ExternalOutput").ap())
    adaln_block(nc, *args)
    r = _run(nc, [arrays], core_ids=[0])
    return r.results[0]["out_0_dram"]
```

```python
import concourse.bass as bass
from concourse import mybir
from contextlib import ExitStack
import math
import numpy as np


def adaln_block(nc, x, wk_d, wv_d, wo_d, gate_d, freqs_d, router_d, egate_d, eup_d, edown_d, c_d, wmod_d, out):
    fp32, i32, bf16 = mybir.dt.float32, mybir.dt.int32, mybir.dt.bfloat16
    ALU, ACT, AX = mybir.AluOpType, mybir.ActivationFunctionType, mybir.AxisListType
    ds = bass.ds

    B, T, D = x.shape
    P = 128
    H, HD = freqs_d.shape
    CH = H * HD
    CB = CH // P
    WIN = 512
    NW = T // WIN
    Q = WIN // P
    KT = D // P
    NG = NW * B
    NU = NG * CB
    N = B * T
    NT = N // P
    TB = T // P
    E = router_d.shape[1]
    EH = egate_d.shape[2]
    TOPK = 2
    CAP = max(1, math.ceil(N * TOPK / E * 1.25))
    NBLK = (N * TOPK + E * (P - 1)) // P
    R = 8
    assert KT == 2 and EH == 2 * P and NBLK <= P and NG == 8 and CB % 2 == 0 and NBLK % R
    PHASE = 10.0
    TWO_PI = 2.0 * math.pi
    TURN = float(np.nextafter(np.float32(TWO_PI), np.float32(0)))
    HALF_PI = float(np.float32(math.pi / 2))
    PI = float(np.nextafter(np.float32(math.pi), np.float32(0)))
    MAGIC = 12582912.0
    C1 = 6.28125
    C2 = float(np.float32(TWO_PI - C1))
    EPS = 1e-5
    NEG = -3.0e38

    x_v = x.rearrange("b (n p) d -> p (b n) d", p=P)
    out_v = out.rearrange("b (n p) d -> p (b n) d", p=P)
    x2_d = nc.dram_tensor("x2_scratch", (N, D), fp32, kind="Internal").ap()
    h2_d = nc.dram_tensor("h2_scratch", (N, D), fp32, kind="Internal").ap()
    y_d = nc.dram_tensor("y_scratch", (TOPK * N + NBLK * P, D), fp32, kind="Internal").ap()
    x2_v = x2_d.rearrange("(n p) d -> p n d", p=P)
    h2_v = h2_d.rearrange("(n p) d -> p n d", p=P)
    y_v = y_d[0:TOPK * N, :].rearrange("(n p k) d -> p n (k d)", p=P, k=TOPK)
    ZR = 4
    yz_v = y_d[0:TOPK * N, :].rearrange("(n p r) d -> p n (r d)", p=P, r=ZR)
    NZ = TOPK * N // (P * ZR)

    ctx = ExitStack()
    with ctx:
        def sb(name, shape, dt=fp32):
            return ctx.enter_context(nc.sbuf_tensor(name, shape, dt))

        def sem(name):
            return ctx.enter_context(nc.semaphore(name))

        egu = sb("egu", [P, E * KT * 2 * EH])
        egu_v = egu[:, :].rearrange("p (e k n) -> p e k n", e=E, k=KT)
        LATE = 4
        pr_flat = egu[:, (E - LATE) * KT * 2 * EH:]
        prod = pr_flat[:, 0:4 * WIN].rearrange("p (s r t) -> p s r t", s=2, r=2)
        hT = pr_flat[:, 4 * WIN:(4 + 2 * KT) * WIN].rearrange("p (s k t) -> p s k t", s=2, k=KT)
        MODE = E - 2 * LATE
        assert 6 * D + B * P <= LATE * 2 * EH
        mo_flat = egu[:, MODE * KT * 2 * EH:(E - LATE) * KT * 2 * EH]
        wmod = mo_flat[:, 0:KT * 6 * D].rearrange("p (k n) -> p k n", k=KT)
        csb = mo_flat[:, KT * 6 * D:KT * 6 * D + KT * B * P].rearrange("p (k b m) -> p k b m", k=KT, b=B)
        tab_flat = sb("rotor_tables", [P, CB * 2 * WIN])
        tab = tab_flat[:, :].rearrange("p (c r t) -> p c r t", c=CB, r=2)
        edn_v = tab_flat[:, :].rearrange("p (e k n) -> p e k n", e=E, k=KT)
        assert 2 * KT * CH + CB * D + 4 * WIN == NT * D
        w_flat = sb("attention_weights", [P, NT * D])
        wk = w_flat[:, 0:KT * CH].rearrange("p (k n) -> p k n", k=KT)
        wv = w_flat[:, KT * CH:2 * KT * CH].rearrange("p (k n) -> p k n", k=KT)
        wo = w_flat[:, 2 * KT * CH:2 * KT * CH + CB * D].rearrange("p (c n) -> p c n", c=CB)
        x2all = w_flat[:, :].rearrange("p (n d) -> p n d", n=NT)
        modr = sb("mod_rows", [P, B, 4, D])
        GA, SB_, CB1, GB = range(4)
        modc = sb("mod_cols", [P, 2 * KT, B])
        trow = sb("t_row", [P, T])
        trig = sb("trig", [P, 2, 2, WIN + 1])
        v_flat = w_flat[:, NT * D - 4 * WIN:NT * D]
        vg = v_flat[:, 0:2 * WIN].rearrange("p (s t) -> p s t", s=2)
        parts = sb("head_parts", [P, 2, 2, WIN])
        t_t = sb("rounded_turns", [P, WIN])
        r_t = sb("turns", [P, WIN])
        a_t = sb("abs_turns", [P, WIN])
        phi = sb("phi", [P, WIN])
        nphi = sb("nphi", [P, WIN])
        xa = sb("xa", [P, Q, D])
        rows_flat = sb("xr_and_h2", [P, 2, Q, D])
        xr = rows_flat[:, 0, :, :]
        h2 = rows_flat[:, 1, :, :]
        xgT_flat = sb("xgT", [P, KT * WIN])
        h2T = sb("h2T", [P, KT, WIN])
        rw = sb("router_w", [P, KT, E])
        gcol = sb("gate_cols", [P, CB, 2])
        fcol = sb("freq_cols", [P, CB])
        cT = sb("cT", [P, KT, B])
        csT = sb("csT", [P, KT, B])
        ident = sb("ident", [P, P])
        tcarry = sb("trig_carry", [P, B, CB, 2])
        scarry = sb("scan_carry", [P, B, CB, 4])
        one = sb("one", [P, 1])
        spare = sb("spare", [P, 8 + NT // 4])
        mhalf = sb("minus_half", [P, TB])
        bnst = sb("bn_stats", [P, Q, 6])
        mv1 = sb("mean_var1", [P, Q, 2])
        mv2 = sb("mean_var2", [P, Q, 2])
        ve1 = sb("var_eps1", [P, Q])
        ve2 = sb("var_eps2", [P, Q])
        nm1 = sb("neg_mean1", [P, Q])
        nm2 = sb("neg_mean2", [P, Q])
        sh1 = sb("shift1", [P, Q])
        sh2 = sb("shift2", [P, Q])
        rs1 = sb("rstd1", [P, Q])
        rs2 = sb("rstd2", [P, Q])
        isq = sb("inv_sqrt_t", [P, TB])
        tcol = sb("t_col", [P, TB])
        logits = sb("logits", [P, NT, E])
        NE = NT * E
        vf = v_flat
        eqt = vf[:, 0:2 * NE].rearrange("p (k n e) -> p k n e", k=2, n=NT)
        lmask = vf[:, 2 * NE:3 * NE].rearrange("p (n e) -> p n e", n=NT)
        oh_flat = sb("choices", [P, 2 + 2 * NE], bf16)
        ohe = oh_flat[:, 2:2 + 2 * NE].rearrange("p (k e n) -> p k e n", k=2, e=E)
        oh = ohe.rearrange("p k e n -> p k n e")
        cum = t_t[:, :].bitcast(bf16).rearrange("p (k e n) -> p k e n", k=2, e=E)
        segm = xa[:, :, :].rearrange("p q d -> p (q d)")
        expo = r_t[:, :].rearrange("p (n e) -> p n e", n=NT)
        iota_p = a_t[:, 0:P]
        triu = a_t[:, P:P + P // 2].bitcast(bf16)
        onesb = a_t[:, P + P // 2:2 * P].bitcast(bf16)
        e16 = a_t[:, 2 * P:2 * P + E]
        iota_b = a_t[:, 2 * P + E:2 * P + E + P // 2].bitcast(bf16)
        tf = trig[:, :, :, :].rearrange("p a b t -> p (a b t)")
        pos_hot = tf[:, 0:8 * P].bitcast(bf16).rearrange("p (c s m) -> p c s m", c=2, s=8)
        pf = parts[:, :, :, :].rearrange("p a b t -> p (a b t)")
        CH8 = 8 * NBLK
        dist = pf[:, 0:2 * CH8].rearrange("p (c k n m) -> p c k n m", c=2, k=2, n=4)
        adist = pf[:, 2 * CH8:3 * CH8].bitcast(bf16).rearrange("p (c k n m) -> p c k n m", c=2, k=2, n=4)
        hot = rows_flat[:, :, :, :].rearrange("p a q d -> p (a q d)")[:, 0:2 * CH8].bitcast(bf16).rearrange(
            "p (c k n h m) -> p c k n h m", c=2, k=2, n=4, h=2)
        m1 = sb("top_logit", [P, 2, NT])
        first = sb("first_index", [P, NT])
        zsum = sb("z_sum", [P, NT])
        wgt = sb("weights", [P, 2, NT])
        rsel = sb("ranks", [P, 2, NT])
        keep = sb("keep", [P, 2, NT])
        slot = sb("slots", [P, 2, NT])
        far = sb("far_if_dropped", [P, 2, NT])
        sloti = sb("slots_int", [P, 2, NT], i32)
        posi = sb("pos_int", [P, 2, NT], i32)
        posf = sb("pos_f", [P, 2, NT])
        blkf = sb("blk_f", [P, 2, NT])
        row_hi = sb("row_ids_of_tiles", [P, NT])
        row_lo = sb("row_ids_in_tile", [P, 2])
        row_neg = sb("minus_row_ids_in_tile", [P, 2])
        rowf = sb("slot_rows_f", [P, NBLK])
        idle_row = sb("idle_rows", [P, NBLK])
        kept = sb("kept", [P, 2, E])
        nexp = sb("n_expert", [P, E])
        nexpi = sb("n_expert_int", [P, E], i32)
        nblkf = sb("n_blocks", [P, E])
        bend = sb("block_end", [P, E])
        aoff = sb("slot_offsets", [P, 2, E])
        ended = vf[:, 0:NBLK * (E - 1)].rearrange("p (j e) -> p j e", j=NBLK)
        eblk = sb("expert_of_block", [P, NBLK])
        eblki = sb("expert_of_block_int", [P, NBLK], i32)
        SLAG = 6
        idle = sb("idle_slots", [P, NBLK])
        rowi = sb("slot_rows", [P, NBLK], i32)
        pair_idx = sb("slot_indices", [P, NBLK + SLAG, 2], i32)
        idxc = sb("row_indices", [P, 4, 2], i32)
        xg = xa
        xgT = xgT_flat[:, :].rearrange("p (k s m) -> p k s m", k=KT, s=4)
        hidT = h2T[:, :, :].rearrange("p k (s m) -> p k s m", s=4)
        sg = parts[:, 0, :, 0:EH]
        hid = parts[:, 1, :, 0:EH]
        ysb = rows_flat[:, :, :, :].rearrange("p a q d -> p (a q) d")
        yl = egu[:, 0:NT * 2 * D].rearrange("p (i n k d) -> p i n k d", i=NT // 2, n=2, k=2)
        LH = NT // 4
        assert B % 2 == 0

        ps = ctx.enter_context(nc.psum_tensor("ps", [P, 8, 512], fp32))
        U, V, A, WO, TP = 0, 1, 3, 5, 7
        MISC = TP
        MOD_STEP = {0: (0, 1), 1: (2, 3, 4), 2: (5,), 3: (6,), 4: (7,)}
        MOD_BANK = (WO, WO + 1, WO, WO + 1, TP, TP, TP, TP)
        POOL_ADDS = (5, 6)
        LAG = 2

        def S(names):
            return [sem(n) for n in names.split()]

        (c_in, wmod_in, wmodr_in, wk_in, wv_in, wo_in, small_in, xa_in, xr_in, egu_in, elate_in, x2_out, h2_out) = S(
            "c_in wmod_in wmodr_in wk_in wv_in wo_in small_in xa_in xr_in egu_in elate_in x2_out h2_out")
        (ident_done, iota_done, pc_chain, silu_done, csb_done, modc_mm, modr_mm, modc_done, modr_copied, modr_done,
         wk_scaled, isq_done) = S(
            "ident_done iota_done pc_chain silu_done csb_done modc_mm modr_mm modc_done modr_copied modr_done wk_scaled isq_done")
        (var1_done, rstd1_done, xn_done, tp1_done, hT_done, k_done, v_done, t_done, r_done, abs_done, trig_done,
         vcopy_done) = S(
            "var1_done rstd1_done xn_done tp1_done hT_done k_done v_done t_done r_done abs_done trig_done vcopy_done")
        (phi_done, nphi_mid, nphi_done, phir_mid, phir_done, phia_done, tab_done) = S(
            "phi_done nphi_mid nphi_done phir_mid phir_done phia_done tab_done")
        (dassoc_done, sassoc_done, dpos_done, spos_done, carry_done, kept_done, fassoc_done, fpos_done, parts_done, wo_done) = S(
            "dassoc_done sassoc_done dpos_done spos_done carry_done kept_done fassoc_done fpos_done parts_done wo_done")
        (wo_read, gated_done, x2_done, var2_done, rstd2_done, h2n_done, h2c_done, h2_done) = S(
            "wo_read gated_done x2_done var2_done rstd2_done h2n_done h2c_done h2_done")
        (tp2_done, h2T_done, lg_done, lg_copied, ln1_chain, ln2_chain) = S(
            "tp2_done h2T_done lg_done lg_copied ln1_chain ln2_chain")
        (rt, mixed_done, rt_iota, rt_count, rt_rank, rt_exp_in, rt_exp, rt_slot, wgt_done) = S(
            "rt mixed_done rt_iota rt_count rt_rank rt_exp_in rt_exp rt_slot wgt_done")
        (dist_done, babs_done, lo_done, hi_done, pos_done, map_mm, map_done, exps_done) = S(
            "dist_done babs_done lo_done hi_done pos_done map_mm map_done exps_done")
        gath = [sem(f"rows_gathered{s}") for s in range(4)]
        ystor = [sem(f"y_scattered{s}") for s in range(R)]
        y_in = [sem(f"y_in{s}") for s in range(NT // 4)]
        (zero_set, zero_out, x2_in, out_stored, segm_set) = S("zero_set zero_out x2_in out_stored segm_set")
        (idx_done, bt_done, bxT_done, bgu_done, bsilu_done, bhid_done, bht_done, bhT_done, by_done, by_copied) = S(
            "idx_done bt_done bxT_done bgu_done bsilu_done bhid_done bht_done bhT_done by_done by_copied")
        carried = sem("carried")
        (cw0_done, cw1_done, cgb_done, csum_done, h2q_mid, h2q_done) = S("cw0_done cw1_done cgb_done csum_done h2q_mid h2q_done")

        block = ctx.enter_context(nc.Block())

        def wait(eng, s, n):
            if not (isinstance(n, int) and n <= 0):
                eng.wait_ge(s, n)

        def apart(eng, n):
            if not isinstance(n, int):
                if eng is nc.vector:
                    nc.vector.memset(spare[:, 0:1], 0.0)
                elif eng is nc.gpsimd:
                    nc.gpsimd.tensor_tensor(spare[:, 6:7], one[:, 0:1], one[:, 0:1], ALU.mult)
                else:
                    nc.scalar.activation(spare[:, 2:3], one[:, 0:1], ACT.Copy)

        def table_of(w, b, cb):
            if isinstance(b, int):
                if w == 0 and b == 0:
                    return cb + 1 if cb < CB - 1 else None
                if b == B - 1 and w == 0 and cb >= 2:
                    return CB + cb - 2
                if b == 0 and w == 1 and cb < 2:
                    return 2 * CB - 2 + cb
            return None

        def bodies(eng, body):
            for w in range(NW):
                body(w, 0, w - 1 if w else None, B - 1, w, 1)
                with eng.Fori(1, B - 1) as b:
                    body(w, b, w, b - 1, w, b + 1)
                body(w, B - 1, w, B - 2, w + 1 if w + 1 < NW else None, 0)

        def pipeline(eng, step, lag):
            for j in range(R):
                step(j, j)
            with eng.Fori(1, NBLK // R) as i:
                for s in range(R):
                    step(i * R + s, s)
            for j in range(NBLK // R * R, NBLK + lag):
                step(j, j % R)

        def there(j):
            return not isinstance(j, int) or 0 <= j < NBLK

        @block.sync
        def _(sp):
            sp.dma_start(cT[:, 0, :], c_d[:, 0:P].rearrange("b p -> p b"), allow_slow_non_contiguous=True).then_inc(c_in, 16)
            sp.dma_start(cT[:, 1, :], c_d[:, P:2 * P].rearrange("b p -> p b"), allow_slow_non_contiguous=True).then_inc(c_in, 16)
            sp.dma_start(xa[:, :, :], x_v[:, 0:Q, :]).then_inc(xa_in, 16)
            wmod_dv = wmod_d.rearrange("(k p) n -> p k n", p=P)
            sp.dma_start(wmod[:, :, 0:2 * D], wmod_dv[:, :, 0:2 * D]).then_inc(wmod_in, 16)
            for hh in range(P // HD):
                sp.dma_start(fcol[hh * HD:(hh + 1) * HD, :],
                             freqs_d.rearrange("(c h) d -> h d c", h=P // HD)[hh, :, :],
                             allow_slow_non_contiguous=True).then_inc(small_in, 16)
                sp.dma_start(gcol[hh * HD:(hh + 1) * HD, :, :],
                             gate_d.rearrange("(c h) g -> h c g", h=P // HD)[hh, :, :].partition_broadcast(HD)
                             ).then_inc(small_in, 16)
            sp.dma_start(wk[:, :, :], wk_d.rearrange("(k p) n -> p k n", p=P)).then_inc(wk_in, 16)
            sp.dma_start(wv[:, :, :], wv_d.rearrange("(k p) n -> p k n", p=P)).then_inc(wv_in, 16)
            sp.dma_start(wmod[:, :, 2 * D:6 * D], wmod_dv[:, :, 2 * D:6 * D]).then_inc(wmodr_in, 16)
            sp.dma_start(rw[:, :, :], router_d.rearrange("(k p) n -> p k n", p=P)).then_inc(wo_in, 16)
            sp.dma_start(wo[:, :, :], wo_d.rearrange("(c p) n -> p c n", p=P)).then_inc(wo_in, 16)

            def body(w, b, wp, bp, wn, bn):
                g = w * B + b
                if wn is not None:
                    wait(sp, tp1_done, KT * (g + 1))
                    sp.dma_start(xa[:, :, :], x_v[:, ds(bn * TB + wn * Q, Q), :]).then_inc(xa_in, 16)
                if wp is not None:
                    wait(sp, x2_done, g)
                    sp.dma_start(x2_v[:, ds(bp * TB + wp * Q, Q), :], xr[:, :, :]).then_inc(x2_out, 16)
                    wait(sp, x2_out, 16 * g)
                    wait(sp, h2n_done, g)
                sp.dma_start(xr[:, :, :], x_v[:, ds(b * TB + w * Q, Q), :]).then_inc(xr_in, 16)
                if wp is None:
                    sp.wait_ge(zero_set, 1)
                sp.dma_start(yz_v[:, ds(g * (NZ // NG), NZ // NG), :],
                             xgT_flat[:, :].unsqueeze(1).to_broadcast([P, NZ // NG, ZR * D])).then_inc(zero_out, 16)
                if wp is not None:
                    wait(sp, h2_done, g)
                    sp.dma_start(h2_v[:, ds(bp * TB + wp * Q, Q), :], h2[:, :, :]).then_inc(h2_out, 16)
                else:
                    for e in range(E - LATE):
                        if e == MODE:
                            sp.wait_ge(modr_mm, 2 * B)
                        for half, src in enumerate((egate_d, eup_d)):
                            sp.dma_start(egu_v[:, e, :, half * EH:(half + 1) * EH],
                                         src[e, :, :].rearrange("(k p) n -> p k n", p=P)).then_inc(egu_in, 16)

            bodies(sp, body)
            sp.wait_ge(x2_done, NG)
            sp.dma_start(x2_v[:, ds((B - 1) * TB + (NW - 1) * Q, Q), :], xr[:, :, :]).then_inc(x2_out, 16)
            sp.wait_ge(h2q_done, Q)
            sp.dma_start(h2_v[:, ds((B - 1) * TB + (NW - 1) * Q, Q), :], h2[:, :, :]).then_inc(h2_out, 16)
            sp.wait_ge(parts_done, NU)
            sp.wait_ge(v_done, NU)
            for e in range(E - LATE, E):
                for half, src in enumerate((egate_d, eup_d)):
                    sp.dma_start(egu_v[:, e, :, half * EH:(half + 1) * EH],
                                 src[e, :, :].rearrange("(k p) n -> p k n", p=P)).then_inc(elate_in, 16)
            for e in range(0, E, 4):
                sp.dma_start(edn_v[:, e:e + 4, :, :],
                             edown_d[e:e + 4, :, :].rearrange("e (k p) n -> p e k n", p=P)).then_inc(elate_in, 16)
            sp.wait_ge(x2_out, 16 * NG)
            sp.wait_ge(k_done, NU)
            sp.wait_ge(wo_done, NU)
            for b in range(B):
                if b == B - 1:
                    sp.wait_ge(exps_done, 1)
                sp.dma_start(x2all[:, b * TB:(b + 1) * TB, :], x2_v[:, b * TB:(b + 1) * TB, :]).then_inc(x2_in, 16)
            for s in range(R):
                sp.wait_ge(ystor[s], 16 * len(range(s, NBLK, R)))
            sp.wait_ge(by_done, NBLK)

            def load_y(i, s):
                sp.dma_start(yl[:, i, :, :, :].rearrange("p n k d -> p n (k d)"), y_v[:, i * 2:i * 2 + 2, :]).then_inc(y_in[s], 16)

            def store_sum(i):
                sp.wait_ge(csum_done, i + 1)
                sp.dma_start(out_v[:, ds(i * 2, 2), :], x2all[:, ds(i * 2, 2), :]).then_inc(out_stored, 16)

            for s in range(LH):
                load_y(s, s)
            for s in range(LH):
                sp.wait_ge(y_in[s], 16)
                load_y(LH + s, s)
                store_sum(s)
            with sp.Fori(LH, 2 * LH) as i:
                store_sum(i)
            sp.wait_ge(out_stored, 16 * (NT // 2))

        @block.tensor
        def _(pe):
            pe.wait_ge(silu_done, 1)
            pe.wait_ge(wmod_in, 16)
            for j in range(2 * KT):
                for k in range(KT):
                    last = nc.tensor.matmul(ps[:, MISC, j * B:(j + 1) * B], wmod[:, k, j * P:(j + 1) * P], csT[:, k, :],
                                            start=(k == 0), stop=(k == KT - 1))
            last.then_inc(modc_mm, 1)
            pe.wait_ge(ident_done, 2)

            def modulation_rows(i):
                b, n = i % B, i // B
                wait(pe, modr_copied, {2: 1, 3: 2, 5: 5, 6: 6, 7: 7}.get(i, 0))
                for k in range(KT):
                    last = nc.tensor.matmul(ps[:, MOD_BANK[i], :], csb[:, k, b, :],
                                            wmod[:, k, 2 * D + n * 512:2 * D + (n + 1) * 512],
                                            start=(k == 0), stop=(k == KT - 1))
                last.then_inc(modr_mm, 1)

            def group_of(u, cb):
                return (u - cb) // CB

            def project_out(u, cb):
                one_part = cb in POOL_ADDS
                if one_part:
                    wait(pe, mixed_done, group_of(u, cb) * len(POOL_ADDS) + POOL_ADDS.index(cb) + 1)
                else:
                    wait(pe, parts_done, u + 1)
                for q in range(Q):
                    for r in range(1 if one_part else 2):
                        last = nc.tensor.matmul(ps[:, WO + q // 2, (q % 2) * D:(q % 2 + 1) * D],
                                                parts[:, cb % 2, r, q * P:(q + 1) * P], wo[:, cb, :],
                                                start=(cb == 0 and q % 2 == 0 and r == 0),
                                                stop=(cb == CB - 1 and q % 2 == 1), skip_group_check=True)
                last.then_inc(wo_done, 1)

            def transposes(src, k, done):
                for q in range(Q):
                    last = nc.tensor.transpose(ps[:, TP, q * P:(q + 1) * P], src[:, q, k * P:(k + 1) * P], ident[:, :])
                last.then_inc(done, 1)

            def router_transposes(g, k):
                if k == 0:
                    wait(pe, h2_done, g + 1)
                    wait(pe, hT_done, KT * (g + 3) if not isinstance(g, int) or g < NG - 2 else KT * NG)
                    if isinstance(g, int) and g == NG - 1:
                        wait(pe, lg_copied, g)
                else:
                    wait(pe, h2T_done, KT * g + 1)
                transposes(h2, k, tp2_done)

            def router(g):
                wait(pe, h2T_done, KT * (g + 1))
                for q in range(Q):
                    for k in range(KT):
                        last = nc.tensor.matmul(ps[:, MISC, q * E:(q + 1) * E], h2T[:, k, q * P:(q + 1) * P], rw[:, k, :],
                                                start=(k == 0), stop=(k == KT - 1))
                last.then_inc(lg_done, 1)

            def ln1_transposes(g, k, first_loop=False):
                if k == 0:
                    wait(pe, xn_done, g + 1)
                    if isinstance(g, int) or not first_loop:
                        wait(pe, lg_copied, g - 2)
                else:
                    wait(pe, hT_done, KT * g + k)
                transposes(xa, k, tp1_done)

            pe.wait_ge(modc_done, 1)
            for k in range(KT):
                ln1_transposes(0, k)
            pe.wait_ge(wk_scaled, 1)
            pe.wait_ge(wv_in, 16)

            def body(w, b, wp, bp, wn, bn):
                g = w * B + b
                u0 = g * CB
                wait(pe, hT_done, KT * (g + 1))
                hTg = hT[:, ds(b % 2, 1), :, :].rearrange("p s k t -> p (s k) t")
                for cb in range(CB):
                    u = u0 + cb
                    wait(pe, vcopy_done, u - 1)
                    wait(pe, dassoc_done, u - 1)
                    for k in range(KT):
                        last = nc.tensor.matmul(ps[:, V + cb % 2, :], wv[:, k, cb * P:(cb + 1) * P], hTg[:, k, :],
                                                start=(k == 0), stop=(k == KT - 1))
                    last.then_inc(v_done, 1)
                    wait(pe, r_done, u)
                    for k in range(KT):
                        last = nc.tensor.matmul(ps[:, U, :], wk[:, k, cb * P:(cb + 1) * P], hTg[:, k, :],
                                                start=(k == 0), stop=(k == KT - 1))
                    last.then_inc(k_done, 1)
                    if wp is None and cb in MOD_STEP:
                        if cb == 0:
                            pe.wait_ge(wmodr_in, 16)
                            pe.wait_ge(csb_done, 1)
                        for i in MOD_STEP[cb]:
                            modulation_rows(i)
                        if cb == LAG:
                            pe.wait_ge(modr_copied, 4)
                            pe.wait_ge(wo_in, 32)
                        if cb == 4:
                            pe.wait_ge(modr_copied, 8)
                    if cb in (6, 7) and wp is not None:
                        router_transposes(g - 1, cb - 6)
                    if cb in (4, 5) and wn is not None:
                        ln1_transposes(g + 1, cb - 4, w == 0)
                    if wp is not None or cb >= LAG:
                        if cb == LAG:
                            wait(pe, wo_read, g)
                        project_out(u - LAG, (cb - LAG) % CB)
                    if cb == 7 and wp is not None:
                        router(g - 1)

            bodies(pe, body)
            for cb in range(CB - LAG, CB):
                project_out(NU - CB + cb, cb)
            pe.wait_ge(lg_copied, NG - 1)
            pe.wait_ge(r_done, NU)
            for q in range(Q):
                pe.wait_ge(h2q_done, q + 1)
                for k, bank in enumerate((TP, U)):
                    last = nc.tensor.transpose(ps[:, bank, q * P:(q + 1) * P], h2[:, q, k * P:(k + 1) * P], ident[:, :])
            last.then_inc(tp2_done, KT)
            pe.wait_ge(h2T_done, KT * NG)
            pe.wait_ge(dassoc_done, NU)
            for q in range(Q):
                for k in range(KT):
                    last = nc.tensor.matmul(ps[:, V, q * E:(q + 1) * E], h2T[:, k, q * P:(q + 1) * P], rw[:, k, :],
                                            start=(k == 0), stop=(k == KT - 1))
            last.then_inc(lg_done, 1)

            pe.wait_ge(rt_iota, 5)
            pe.wait_ge(rt_count, 1)
            for k in range(2):
                nc.tensor.matmul(ps[:, A + k, :], triu, ohe[:, k, :, :], start=True, stop=False)
                nc.tensor.matmul(ps[:, A + k, :], onesb, cum[:, k, :, :], start=False, stop=True)
            nc.tensor.matmul(ps[:, WO, 0:2 * E], onesb, ohe[:, :, :, NT - 1], start=True, stop=False)
            nc.tensor.matmul(ps[:, WO, 0:2 * E], onesb, cum[:, :, :, NT - 1], start=False, stop=True).then_inc(rt_rank, 1)

            def map_chunk(c, i):
                wait(pe, lo_done, i + 1)
                wait(pe, hi_done, i + 1)
                for s in range(8):
                    wait(pe, pos_done, i * 8 + s + 1)
                    last = nc.tensor.matmul(ps[:, MISC, 0:2 * NBLK], pos_hot[:, c, s, :], hot[:, c, s // 4, s % 4, :, :],
                                            start=(isinstance(i, int) and i == 0 and s == 0), stop=True, skip_group_check=True)
                last.then_inc(map_mm, 1)

            map_chunk(0, 0)
            map_chunk(1, 1)
            with pe.Fori(1, NT // 8) as i:
                for c in range(2):
                    map_chunk(c, i * 2 + c)

            pe.wait_ge(map_done, 1)
            pe.wait_ge(exps_done, 1)
            pe.wait_ge(egu_in, 16 * 2 * (E - LATE))
            pe.wait_ge(elate_in, 16 * (2 * LATE + 4))

            def step(j, s):
                if there(j):
                    pe.wait_ge(gath[s % 4], 16 * (j // 4 + 1) if isinstance(j, int) else 4 * (j - s % 4) + 16)
                    wait(pe, bxT_done, j - 1)
                    for k in range(KT):
                        last = nc.tensor.transpose(ps[:, 0 + s % 2, k * P:(k + 1) * P], xg[:, s % 4, k * P:(k + 1) * P], ident[:, :])
                    last.then_inc(bt_done, 1)
                if there(j - 1):
                    e = pe.value_load(eblki[0:1, ds(j - 1, 1)], min_val=0, max_val=E - 1)
                    wait(pe, bxT_done, j)
                    wait(pe, bhid_done, j - 2)
                    for k in range(KT):
                        last = nc.tensor.matmul(ps[:, 2 + (s - 1) % 2, :], xgT[:, k, (s - 1) % 4, :], egu_v[:, ds(e, 1), k, :],
                                                start=(k == 0), stop=(k == KT - 1))
                    last.then_inc(bgu_done, 1)
                if there(j - 2):
                    wait(pe, bhid_done, j - 1)
                    wait(pe, bhT_done, j - 3)
                    for k in range(KT):
                        last = nc.tensor.transpose(ps[:, 4 + s % 2, k * P:(k + 1) * P], hid[:, s % 2, k * P:(k + 1) * P], ident[:, :])
                    last.then_inc(bht_done, 1)
                if there(j - 3):
                    e = pe.value_load(eblki[0:1, ds(j - 3, 1)], min_val=0, max_val=E - 1)
                    wait(pe, bhT_done, j - 2)
                    wait(pe, by_copied, j - 4)
                    for k in range(KT):
                        last = nc.tensor.matmul(ps[:, 6 + (s - 3) % 2, 0:D], hidT[:, k, (s - 3) % 4, :], edn_v[:, ds(e, 1), k, :],
                                                start=(k == 0), stop=(k == KT - 1))
                    last.then_inc(by_done, 1)

            pipeline(pe, step, 3)

        @block.scalar
        def _(act):
            act.wait_ge(c_in, 32)
            act.activation(csT[:, :, :], cT[:, :, :], ACT.Silu).then_inc(silu_done, 1)
            act.wait_ge(small_in, 64)
            act.wait_ge(iota_done, 1)

            def copy_modulation(i):
                b, n = i % B, i // B
                act.wait_ge(modr_mm, i + 1)
                act.activation(modr[:, b, 2 * n:2 * n + 2, :].rearrange("p s d -> p (s d)"), ps[:, MOD_BANK[i], :],
                               ACT.Copy).then_inc(modr_copied, 1)

            def copy_h2T(g, k):
                wait(act, tp2_done, KT * g + k + 1)
                act.activation(h2T[:, k, :], ps[:, TP, :], ACT.Copy).then_inc(h2T_done, 1)

            def table_phases(m):
                w, cb = m // CB, m % CB
                wait(act, tab_done, m)
                act.activation(phi[:, :], trow[:, w * WIN:(w + 1) * WIN], ACT.Copy,
                               scale=fcol[:, cb:cb + 1]).then_inc(phi_done, 1)
                act.wait_ge(phi_done, m + 1)
                act.activation(nphi[:, :], phi[:, :], ACT.Copy, scale=1.0 / TWO_PI, bias=MAGIC).then_inc(nphi_mid, 1)
                act.wait_ge(nphi_mid, m + 1)
                act.activation(nphi[:, :], nphi[:, :], ACT.Copy, bias=-MAGIC).then_inc(nphi_done, 1)

            def table(m):
                wait(act, phir_done, m + 1)
                act.activation(nphi[:, :], phi[:, :], ACT.Abs).then_inc(phia_done, 1)
                if m >= CB:
                    wait(act, fpos_done, (B - 1) * CB + m % CB + 1)
                act.activation(tab[:, m % CB, 1, :], phi[:, :], ACT.Sin)
                act.wait_ge(phia_done, m + 1)
                act.activation(tab[:, m % CB, 0, :], nphi[:, :], ACT.Sin, scale=-1.0, bias=HALF_PI).then_inc(tab_done, 1)
                if m + 1 < NW * CB:
                    table_phases(m + 1)

            def copy_hT(g, b, k):
                wait(act, tp1_done, KT * g + k + 1)
                apart(act, b)
                act.activation(hT[:, ds(b % 2, 1), k, :].rearrange("p s t -> p (s t)"), ps[:, TP, :], ACT.Identity,
                               scale=modc[:, KT + k, ds(b, 1)], bias=modc[:, k, ds(b, 1)]).then_inc(hT_done, 1)

            def ln_apply(dst, src, rs, sh, shifted, n, done):
                wait(act, shifted, n)
                for q in range(Q):
                    last = act.activation(dst[:, q, :], src[:, q, :], ACT.Identity, scale=rs[:, q:q + 1], bias=sh[:, q:q + 1])
                last.then_inc(done, 1)

            def read_heads(g, w):
                wait(act, wo_done, CB * (g + 1))
                wait(act, h2_out, 16 * g)
                apart(act, g)
                for q in range(Q):
                    last = act.activation(h2[:, q, :], ps[:, WO + q // 2, (q % 2) * D:(q % 2 + 1) * D], ACT.Copy,
                                          scale=isq[:, w * Q + q:w * Q + q + 1])
                last.then_inc(wo_read, 1)

            def copy_logits(g, b, w):
                wait(act, lg_done, g + 1)
                apart(act, g)
                act.activation(logits[:, ds(b * TB + w * Q, Q), :],
                               ps[:, MISC, 0:Q * E].rearrange("p (q e) -> p q e", q=Q), ACT.Copy).then_inc(lg_copied, 1)

            table_phases(0)
            ln_apply(xa, xa, rs1, sh1, rstd1_done, 2, xn_done)
            act.wait_ge(modc_done, 1)
            for k in range(KT):
                copy_hT(0, 0, k)
            table(0)

            def body(w, b, wp, bp, wn, bn):
                g = w * B + b
                u0 = g * CB
                for cb in range(CB):
                    u = u0 + cb
                    s = cb % 2
                    wait(act, v_done, u + 1)
                    wait(act, dpos_done, u - 1)
                    act.activation(vg[:, s, :], ps[:, V + s, :], ACT.Copy, scale=gcol[:, cb, 0:1]).then_inc(vcopy_done, 1)
                    wait(act, k_done, u + 1)
                    wait(act, r_done, u)
                    wait(act, trig_done, u)
                    act.activation(t_t[:, :], ps[:, U, :], ACT.Copy, bias=MAGIC).then_inc(t_done, 1)
                    lb, lc = (b, cb - 1) if cb else (bp, CB - 1)
                    if w == 0 and (cb or wp is not None):
                        act.activation(tcarry[:, ds(lb, 1), lc, :].rearrange("p a r -> p r a"),
                                       trig[:, 1 - s, :, WIN:WIN + 1], ACT.Copy)
                    if w == 1 and isinstance(b, int) and b == 0 and cb == 0:
                        act.activation(tcarry[:, B - 1:B, CB - 1, :].rearrange("p a r -> p r a"),
                                       trig[:, 1 - s, :, WIN:WIN + 1], ACT.Copy)
                    m = table_of(w, b, cb)
                    if wp is None and cb in MOD_STEP:
                        for i in MOD_STEP[cb]:
                            copy_modulation(i)
                    if cb == 1 and wn is not None:
                        ln_apply(xa, xa, rs1, sh1, rstd1_done, 2 * (g + 2), xn_done)
                    if cb in (4, 5) and wn is not None:
                        copy_hT(g + 1, bn, cb - 4)
                    if cb == 4 and wp is not None:
                        ln_apply(h2, xr, rs2, sh2, rstd2_done, 2 * g, h2n_done)
                    if cb in (6, 7) and wp is not None:
                        copy_h2T(g - 1, cb - 6)
                    wait(act, r_done, u + 1)
                    wait(act, fassoc_done, 2 * (u - 1))
                    act.activation(a_t[:, :], r_t[:, :], ACT.Abs).then_inc(abs_done, 1)
                    act.activation(trig[:, s, 1, 1:WIN + 1], r_t[:, :], ACT.Sin, scale=-TURN)
                    act.activation(trig[:, s, :, 0:1], tcarry[:, ds(b, 1), cb, :].rearrange("p a r -> p r a"),
                                   ACT.Copy)
                    act.wait_ge(abs_done, u + 1)
                    act.activation(trig[:, s, 0, 1:WIN + 1], a_t[:, :], ACT.Sin, scale=-TURN, bias=HALF_PI).then_inc(trig_done, 1)
                    if m is not None:
                        table(m)
                    if cb == 1 and wp is not None:
                        read_heads(g - 1, wp)
                    if cb == 7 and wp is not None:
                        copy_logits(g - 1, bp, wp)

            bodies(act, body)
            act.wait_ge(tp2_done, KT * NG)
            for k, bank in enumerate((TP, U)):
                act.activation(h2T[:, k, :], ps[:, bank, :], ACT.Copy).then_inc(h2T_done, 1)
            act.wait_ge(lg_done, NG)
            act.activation(logits[:, NT - Q:NT, :], ps[:, V, 0:Q * E].rearrange("p (q e) -> p q e", q=Q),
                           ACT.Copy).then_inc(lg_copied, 1)
            act.wait_ge(rt_exp_in, 1)
            act.activation(expo, expo, ACT.Exp).then_inc(rt_exp, 1)
            act.activation(wgt[:, 1, :], m1[:, 1, :], ACT.Exp).then_inc(rt_exp, 1)

            def step(j, s):
                if there(j - 1):
                    wait(act, bgu_done, j)
                    wait(act, bhid_done, j - 2)
                    act.activation(sg[:, (s - 1) % 2, :], ps[:, 2 + (s - 1) % 2, 0:EH], ACT.Silu).then_inc(bsilu_done, 1)
                if there(j - 2):
                    wait(act, bht_done, j - 1)
                    wait(act, by_done, j - 4)
                    act.activation(hidT[:, :, (s - 2) % 4, :], ps[:, 4 + s % 2, 0:2 * P].rearrange("p (k m) -> p k m", k=KT),
                                   ACT.Copy).then_inc(bhT_done, 1)
                if there(j - 3):
                    wait(act, by_done, j - 2)
                    slot8 = (s - 3) % R
                    if isinstance(j, int):
                        wait(act, ystor[slot8], 16 * ((j - 3) // R))
                    else:
                        act.wait_ge(ystor[slot8], 2 * (j - 3 - slot8))
                    act.activation(ysb[:, slot8, :], ps[:, 6 + (s - 3) % 2, 0:D], ACT.Copy).then_inc(by_copied, 1)

            act.wait_ge(x2_out, 16 * NG)
            act.wait_ge(h2_out, 16 * NG)

            def lo_chunk(c, i):
                act.wait_ge(dist_done, i + 1)
                act.activation(adist[:, c, :, :, :], dist[:, c, :, :, :], ACT.Abs).then_inc(babs_done, 1)
                act.wait_ge(babs_done, i + 1)
                if not isinstance(i, int):
                    act.wait_ge(map_mm, i - 1)
                for k in range(2):
                    last = act.activation(hot[:, c, k, :, 1, :], adist[:, c, k, :, :], ACT.Relu,
                                          scale=row_neg[:, k:k + 1], bias=row_lo[:, k:k + 1])
                last.then_inc(lo_done, 1)

            lo_chunk(0, 0)
            lo_chunk(1, 1)
            with act.Fori(1, NT // 8) as i:
                for c in range(2):
                    lo_chunk(c, i * 2 + c)

            pipeline(act, step, 3)

            act.wait_ge(wgt_done, 1)
            with act.Fori(0, 2) as h:
                for s in range(LH):
                    i = h * LH + s
                    act.wait_ge(y_in[s], h * 16 + 16)
                    act.wait_ge(cw0_done, i)
                    act.activation(spare[:, 8 + s:9 + s], one[:, 0:1], ACT.Copy)
                    for n in range(2):
                        last = act.activation(yl[:, ds(i, 1), n, 0, :], yl[:, ds(i, 1), n, 0, :], ACT.Copy,
                                              scale=wgt[:, 0, ds(i * 2 + n, 1)])
                    last.then_inc(cw0_done, 1)

        @block.vector
        def _(dve):
            v = nc.vector
            chain = [0]

            def link(ins, s=pc_chain):
                chain[0] += 1
                ins.then_inc(s, 1)
                dve.wait_ge(s, chain[0])

            v.memset(one[:, :], 1.0)
            v.memset(mhalf[:, :], -0.5)
            link(v.memset(tcarry[:, :, :, :], 0.0))
            def ln_sums(src, g, chain_):
                for q in range(Q):
                    last = v.bn_stats(bnst[:, q, :], src[:, q, :])
                last.then_inc(chain_, 1)

            def ln_mean_var(mv, g, chain_):
                wait(dve, chain_, 2 * g + 1)
                apart(dve, g)
                for q in range(Q):
                    last = v.bn_aggr(mv[:, q, :], bnst[:, q, :])
                last.then_inc(chain_, 1)

            def ln_var_eps(mv, ve, nm, g, chain_, done):
                wait(dve, chain_, 2 * g + 2)
                v.tensor_scalar(ve[:, :], mv[:, :, 1], EPS, None, ALU.add)
                v.tensor_scalar(nm[:, :], mv[:, :, 0], -1.0, None, ALU.mult).then_inc(done, 1)

            def read_heads(g, b, w):
                wait(dve, wo_done, CB * (g + 1))
                wait(dve, h2_out, 16 * g)
                for q in range(Q):
                    last = v.scalar_tensor_tensor(h2[:, q, :], ps[:, WO + q // 2, (q % 2) * D:(q % 2 + 1) * D],
                                                  isq[:, w * Q + q:w * Q + q + 1], modr[:, ds(b, 1), GA, :], ALU.mult, ALU.mult)
                last.then_inc(wo_read, 1)

            def turns(u):
                wait(dve, t_done, u + 1)
                wait(dve, trig_done, u)
                v.scalar_tensor_tensor(r_t[:, :], t_t[:, :], MAGIC, ps[:, U, :], ALU.subtract, ALU.subtract).then_inc(r_done, 1)

            def assoc_products(u, s):
                wait(dve, trig_done, u + 1)
                wait(dve, vcopy_done, u + 1)
                wait(dve, parts_done, u)
                v.tensor_tensor(ps[:, A:A + 2, :], ps[:, V + s:V + s + 1, :].to_broadcast([P, 2, WIN]), trig[:, s, :, 0:WIN],
                                ALU.mult).then_inc(dassoc_done, 1)

            def total(row, w, b, cb, r):
                return v.tensor_tensor_scan(row, one[:, 0:1].to_broadcast([P, WIN]), row,
                                            scarry[:, ds(b, 1), cb, r] if w else 0.0, ALU.mult, ALU.add)

            def keep_sums(rows, b, cb, r0):
                return v.tensor_scalar(scarry[:, ds(b, 1), cb, r0:r0 + 2].rearrange("p a r -> p r a"),
                                       rows[:, :, WIN - 1:WIN], 1.0, None, ALU.mult)

            def pos_sums(u, s, w, b, cb):
                wait(dve, dpos_done, u + 1)
                for r in range(2):
                    last = total(prod[:, s, r, :], w, b, cb, r)
                last.then_inc(carry_done if w == NW - 1 else spos_done, 1)

            def keep_pos(u, s, w, b, cb):
                if w < NW - 1:
                    wait(dve, spos_done, u + 1)
                    keep_sums(prod[:, s, :, :], b, cb, 0).then_inc(carry_done, 1)

            def assoc_sums(u, w, b, cb):
                wait(dve, dassoc_done, u + 1)
                for r in range(2):
                    total(ps[:, A + r, :], w, b, cb, 2 + r).then_inc(sassoc_done, 1)

            def keep_assoc(u, w, b, cb):
                if w < NW - 1:
                    wait(dve, sassoc_done, 2 * u + 2)
                    keep_sums(ps[:, A:A + 2, :], b, cb, 2).then_inc(kept_done, 1)

            def assoc_probe(u, s, w, cb):
                for r in range(2):
                    if w < NW - 1:
                        if r == 0:
                            wait(dve, kept_done, u + 1)
                    else:
                        wait(dve, sassoc_done, 2 * u + 1 + r)
                    v.scalar_tensor_tensor(ps[:, A + r, :], ps[:, A + r, :], gcol[:, cb, 1:2], trig[:, s, r, 1:WIN + 1],
                                           ALU.mult, ALU.mult).then_inc(fassoc_done, 1)

            def add_positions(u, s):
                for r in range(2):
                    if r == 0:
                        wait(dve, fpos_done, u + 1)
                        wait(dve, wo_done, u - 1)
                    wait(dve, fassoc_done, 2 * u + 1 + r)
                    last = v.tensor_tensor(parts[:, s, r, :], ps[:, A + r, :], prod[:, s, r, :], ALU.add)
                last.then_inc(parts_done, 1)

            def table_angles(m, part):
                if part == 0:
                    wait(dve, nphi_done, m + 1)
                    v.scalar_tensor_tensor(phi[:, :], nphi[:, :], -C1, phi[:, :], ALU.mult, ALU.add).then_inc(phir_mid, 1)
                elif part == 1:
                    wait(dve, phir_mid, 2 * m + 1)
                    v.scalar_tensor_tensor(phi[:, :], nphi[:, :], -C2, phi[:, :], ALU.mult, ALU.add).then_inc(phir_mid, 1)
                else:
                    wait(dve, phir_mid, 2 * m + 2)
                    v.tensor_scalar(phi[:, :], phi[:, :], PI, -PI, ALU.min, ALU.max).then_inc(phir_done, 1)

            dve.wait_ge(xa_in, 16)
            ln_sums(xa, 0, ln1_chain)
            ln_mean_var(mv1, 0, ln1_chain)
            ln_var_eps(mv1, ve1, nm1, 0, ln1_chain, var1_done)
            for part in range(3):
                table_angles(0, part)
            dve.wait_ge(modc_mm, 1)
            link(v.tensor_copy(modc[:, :, :], ps[:, MISC, 0:2 * KT * B].rearrange("p (j b) -> p j b", b=B)))
            v.tensor_scalar(modc[:, KT:2 * KT, :], modc[:, KT:2 * KT, :], 1.0, None, ALU.add).then_inc(modc_done, 1)
            dve.wait_ge(wk_in, 16)
            v.tensor_scalar(wk[:, :, :], wk[:, :, :], PHASE / TWO_PI, None, ALU.mult).then_inc(wk_scaled, 1)
            dve.wait_ge(silu_done, 1)
            v.tensor_copy(csb, csT[:, :, :].unsqueeze(3).to_broadcast([P, KT, B, P])).then_inc(csb_done, 1)

            sgn = v_flat[:, 2 * WIN:4 * WIN].rearrange("p (b d) -> p b d", b=B)
            mod_chain = [0]

            def finish_modulation(which, part):
                m = modr[:, :, which, :]
                dve.wait_ge(modr_copied, 4 if which == GA else 8)
                wait(dve, modr_done, mod_chain[0])
                if which == CB1:
                    ins = v.tensor_scalar(m, m, 1.0, None, ALU.add)
                elif part == 0:
                    ins = v.tensor_scalar(sgn, m, 0.0, 2.0, ALU.is_ge, ALU.mult)
                elif part == 1:
                    ins = v.scalar_tensor_tensor(m, m, -1.0, m, ALU.mult, ALU.max)
                elif part == 2:
                    ins = v.tensor_scalar(m, m, 0.25, None, ALU.max)
                else:
                    ins = v.scalar_tensor_tensor(m, sgn, 1.0, m, ALU.subtract, ALU.mult)
                ins.then_inc(modr_done, 1)
                mod_chain[0] += 1

            MOD_WORK = {(2, 1): (GA, 0), (3, 1): (GA, 1), (4, 1): (GA, 2), (5, 0): (GA, 3), (5, 1): (CB1, 0),
                        (6, 0): (GB, 0), (6, 1): (GB, 1), (7, 0): (GB, 2), (7, 1): (GB, 3)}

            def body(w, b, wp, bp, wn, bn):
                g = w * B + b
                u0 = g * CB
                for cb in range(CB):
                    u = u0 + cb
                    s = cb % 2
                    lw, lb, lc = (w, b, cb - 1) if cb else (wp, bp, CB - 1)
                    if lw is None:
                        turns(u)
                        for part in range(3):
                            table_angles(1, part)
                        wait(dve, xa_in, 16 * (g + 2))
                        ln_sums(xa, g + 1, ln1_chain)
                        ln_mean_var(mv1, g + 1, ln1_chain)
                        ln_var_eps(mv1, ve1, nm1, g + 1, ln1_chain, var1_done)
                        continue
                    m = table_of(w, b, cb)
                    pos_sums(u - 1, 1 - s, lw, lb, lc)
                    assoc_products(u - 1, 1 - s)
                    if m is not None:
                        table_angles(m, 0)
                    keep_pos(u - 1, 1 - s, lw, lb, lc)
                    if lw == NW - 1:
                        turns(u)
                    if cb == 3 and wp is not None:
                        wait(dve, x2_done, g)
                        ln_sums(xr, g - 1, ln2_chain)
                    if cb == 0 and wn is not None:
                        wait(dve, xa_in, 16 * (g + 2))
                        ln_sums(xa, g + 1, ln1_chain)
                    assoc_sums(u - 1, lw, lb, lc)
                    if m is not None:
                        table_angles(m, 1)
                    if wp is None and (cb, 0) in MOD_WORK:
                        finish_modulation(*MOD_WORK[cb, 0])
                    if cb == 3 and wp is not None:
                        ln_mean_var(mv2, g - 1, ln2_chain)
                    if cb == 0 and wn is not None:
                        ln_mean_var(mv1, g + 1, ln1_chain)
                    if cb == 3 and wp is not None:
                        ln_var_eps(mv2, ve2, nm2, g - 1, ln2_chain, var2_done)
                    if cb == 0 and wn is not None:
                        ln_var_eps(mv1, ve1, nm1, g + 1, ln1_chain, var1_done)
                    if lw < NW - 1:
                        turns(u)
                        keep_assoc(u - 1, lw, lb, lc)
                    if m is not None:
                        table_angles(m, 2)
                    if wp is None and (cb, 1) in MOD_WORK:
                        finish_modulation(*MOD_WORK[cb, 1])
                        if cb == 7:
                            dve.wait_ge(modr_done, 9)
                    assoc_probe(u - 1, 1 - s, lw, lc)
                    add_positions(u - 1, 1 - s)

            bodies(dve, body)
            s = (CB - 1) % 2
            pos_sums(NU - 1, s, NW - 1, B - 1, CB - 1)
            assoc_products(NU - 1, s)
            assoc_sums(NU - 1, NW - 1, B - 1, CB - 1)
            assoc_probe(NU - 1, s, NW - 1, CB - 1)
            add_positions(NU - 1, s)
            read_heads(NG - 1, B - 1, NW - 1)
            dve.wait_ge(wo_read, NG)
            dve.wait_ge(xr_in, 16 * NG)
            v.tensor_tensor(xr[:, :, :], xr[:, :, :], h2[:, :, :], ALU.add).then_inc(x2_done, 1)
            dve.wait_ge(x2_done, NG)
            ln_sums(xr, NG - 1, ln2_chain)
            ln_mean_var(mv2, NG - 1, ln2_chain)
            ln_var_eps(mv2, ve2, nm2, NG - 1, ln2_chain, var2_done)
            for q in range(Q):
                last = v.scalar_tensor_tensor(h2[:, q, :], xr[:, q, :], mv2[:, q, 0:1], modr[:, B - 1, CB1, :],
                                              ALU.subtract, ALU.mult).then_inc(h2q_mid, 1)
            dve.wait_ge(rstd2_done, 2 * NG)
            for q in range(Q):
                dve.wait_ge(h2q_mid, q + 1)
                v.scalar_tensor_tensor(h2[:, q, :], h2[:, q, :], rs2[:, q:q + 1], modr[:, B - 1, SB_, :],
                                       ALU.mult, ALU.add).then_inc(h2q_done, 1)

            chain[0] = 0

            def step_(ins):
                link(ins, rt)

            def over_e(ap):
                return ap.unsqueeze(2).to_broadcast([P, NT, E])

            dve.wait_ge(rt_iota, 5)
            dve.wait_ge(lg_copied, NG)
            dve.wait_ge(wo_done, NU)
            e_row = e16.unsqueeze(1).to_broadcast([P, NT, E])
            src = logits[:, :, :]
            for k in range(2):
                step_(v.tensor_reduce(m1[:, k, :], src, AX.X, ALU.max))
                step_(v.tensor_tensor(eqt[:, k, :, :], src, over_e(m1[:, k, :]), ALU.is_equal))
                step_(v.tensor_tensor(eqt[:, k, :, :], eqt[:, k, :, :], e_row, ALU.mult))
                step_(v.tensor_reduce(first[:, :], eqt[:, k, :, :], AX.X, ALU.max))
                step_(v.tensor_tensor(oh[:, k, :, :], eqt[:, k, :, :], over_e(first[:, :]), ALU.is_equal))
                if k == 0:
                    step_(v.scalar_tensor_tensor(lmask, oh[:, k, :, :], NEG, src, ALU.mult, ALU.add))
                    src = lmask
            v.tensor_tensor_scan(cum.rearrange("p k e n -> p (k e n)"), oh_flat[:, 1:1 + 2 * NE], segm, 0.0,
                                 ALU.add, ALU.mult).then_inc(rt_count, 1)
            step_(v.tensor_tensor(expo, logits[:, :, :], over_e(m1[:, 0, :]), ALU.subtract))
            v.tensor_tensor(m1[:, 1, :], m1[:, 1, :], m1[:, 0, :], ALU.subtract).then_inc(rt_exp_in, 1)
            dve.wait_ge(rt_rank, 1)
            step_(v.tensor_scalar(kept[:, :, :], ps[:, WO, 0:2 * E].rearrange("p (k e) -> p k e", k=2), float(CAP), None, ALU.min))
            v.tensor_tensor(nexp[:, :], kept[:, 0, :], kept[:, 1, :], ALU.add).then_inc(rt, 1)
            chain[0] += 1
            step_(v.tensor_tensor(eqt, oh, ps[:, A:A + 2, :].rearrange("p k (e n) -> p k n e", n=NT), ALU.mult))
            v.tensor_scalar(nexpi[:, :], nexp[:, :], float(P - 1), None, ALU.add).then_inc(rt, 1)
            chain[0] += 1
            step_(v.tensor_reduce(rsel[:, :, :], eqt, AX.X, ALU.add))
            step_(v.tensor_scalar(nexpi[:, :], nexpi[:, :], 7, None, ALU.logical_shift_right))
            step_(v.tensor_copy(nblkf[:, :], nexpi[:, :]))
            step_(v.tensor_tensor_scan(bend[:, :], one[:, 0:1].to_broadcast([P, E]), nblkf[:, :], 0.0, ALU.mult, ALU.add))
            step_(v.tensor_tensor(nexp[:, :], bend[:, :], nblkf[:, :], ALU.subtract))
            step_(v.tensor_scalar(aoff[:, 0, :], nexp[:, :], float(P), None, ALU.mult))
            step_(v.tensor_tensor(aoff[:, 1, :], aoff[:, 0, :], kept[:, 0, :], ALU.add))
            v.tensor_tensor(eqt, oh, aoff[:, :, :].unsqueeze(2).to_broadcast([P, 2, NT, E]), ALU.mult).then_inc(rt, 1)
            chain[0] += 1
            step_(v.tensor_scalar(far[:, :, :], rsel[:, :, :], float(CAP), float(P * P), ALU.is_ge, ALU.mult))
            v.tensor_reduce(slot[:, :, :], eqt, AX.X, ALU.add).then_inc(rt, 1)
            chain[0] += 1
            step_(v.tensor_tensor(far[:, :, :], far[:, :, :], rsel[:, :, :], ALU.add))
            step_(v.tensor_tensor(sloti[:, :, :], slot[:, :, :], far[:, :, :], ALU.add))
            step_(v.tensor_scalar(posi[:, :, :], sloti[:, :, :], 7, None, ALU.logical_shift_right))
            v.tensor_copy(blkf[:, :, :], posi[:, :, :]).then_inc(rt_slot, 1)
            dve.wait_ge(rt_slot, 1)
            step_(v.tensor_scalar(posi[:, :, :], sloti[:, :, :], P - 1, None, ALU.bitwise_and))
            step_(v.tensor_copy(posf[:, :, :], posi[:, :, :]))

            dve.wait_ge(x2_out, 16 * NG)
            dve.wait_ge(h2_out, 16 * NG)

            def hot_chunk(c, i):
                for s in range(8):
                    k, n = s // 4, s % 4
                    if s == 0 and not isinstance(i, int):
                        dve.wait_ge(map_mm, i - 1)
                    v.tensor_scalar(pos_hot[:, c, s, :], iota_b, posf[:, k, ds(i * 4 + n, 1)], None,
                                    ALU.is_equal).then_inc(pos_done, 1)
                dve.wait_ge(dist_done, i + 1)
                rows = row_hi[:, ds(i * 4, 4)].unsqueeze(2).to_broadcast([P, 4, NBLK])
                v.scalar_tensor_tensor(hot[:, c, 0, :, 0, :], dist[:, c, 0, :, :], 0.0, rows, ALU.is_equal, ALU.mult)
                v.scalar_tensor_tensor(hot[:, c, 1, :, 0, :], dist[:, c, 1, :, :], 0.0, rows,
                                       ALU.is_equal, ALU.mult).then_inc(hi_done, 1)

            hot_chunk(0, 0)
            hot_chunk(1, 1)
            with dve.Fori(1, NT // 8) as i:
                for c in range(2):
                    hot_chunk(c, i * 2 + c)
            v.tensor_tensor(ended, iota_p[:, 0:NBLK].unsqueeze(2).to_broadcast([P, NBLK, E - 1]),
                            bend[:, 0:E - 1].unsqueeze(1).to_broadcast([P, NBLK, E - 1]), ALU.is_ge).then_inc(rt, 1)
            chain[0] += 1
            dve.wait_ge(map_mm, NT // 4)
            step_(v.tensor_scalar(rowf[:, :], ps[:, MISC, 0:NBLK], 1.0, None, ALU.mult))
            step_(v.tensor_tensor(rowf[:, :], rowf[:, :], ps[:, MISC, NBLK:2 * NBLK], ALU.add))
            v.tensor_scalar(rowi[:, :], rowf[:, :], -1.0, 0.0, ALU.add, ALU.max).then_inc(rt, 1)
            step_(v.scalar_tensor_tensor(idle[:, :], rowf[:, :], 0.0, idle_row[:, :], ALU.is_equal, ALU.mult))
            chain[0] += 1
            dve.wait_ge(rt, chain[0])
            v.tensor_scalar(pair_idx[:, 0:NBLK, 0], rowi[:, :], 1, None, ALU.logical_shift_right)
            v.scalar_tensor_tensor(pair_idx[:, SLAG:NBLK + SLAG, 1], rowf[:, :], -1.0, idle[:, :], ALU.add,
                                   ALU.add).then_inc(map_done, 1)
            step_(v.tensor_reduce(eblk[:, :], ended, AX.X, ALU.add))
            v.tensor_copy(eblki[:, :], eblk[:, :]).then_inc(exps_done, 1)
            dve.wait_ge(rt_exp, 2)
            step_(v.tensor_scalar(keep[:, :, :], rsel[:, :, :], float(CAP), None, ALU.is_lt))
            step_(v.tensor_reduce(zsum[:, :], expo, AX.X, ALU.add))
            step_(v.reciprocal(wgt[:, 0, :], zsum[:, :]))
            step_(v.tensor_tensor(wgt[:, 1, :], wgt[:, 1, :], wgt[:, 0, :], ALU.mult))
            v.tensor_tensor(wgt[:, :, :], wgt[:, :, :], keep[:, :, :], ALU.mult).then_inc(wgt_done, 1)

            def step(j, s):
                if there(j):
                    wait(dve, bt_done, j + 1)
                    wait(dve, bgu_done, j - 3)
                    v.tensor_copy(xgT[:, :, s % 4, :], ps[:, 0 + s % 2, 0:2 * P].rearrange("p (k m) -> p k m", k=KT)).then_inc(bxT_done, 1)
                if there(j - 1):
                    wait(dve, bsilu_done, j)
                    wait(dve, bht_done, j - 2)
                    v.tensor_tensor(hid[:, (s - 1) % 2, :], sg[:, (s - 1) % 2, :], ps[:, 2 + (s - 1) % 2, EH:2 * EH],
                                    ALU.mult).then_inc(bhid_done, 1)

            dve.wait_ge(zero_out, 16 * NG)
            pipeline(dve, step, 1)

            dve.wait_ge(x2_in, 16 * B)
            with dve.Fori(0, 2) as h:
                for s in range(LH + 1):
                    i = h * LH + s
                    if s < LH:
                        dve.wait_ge(cw0_done, i + 1)
                        for n in range(2):
                            last = v.scalar_tensor_tensor(yl[:, ds(i, 1), n, 0, :], yl[:, ds(i, 1), n, 1, :],
                                                          wgt[:, 1, ds(i * 2 + n, 1)], yl[:, ds(i, 1), n, 0, :], ALU.mult, ALU.add)
                        last.then_inc(cw1_done, 1)
                    if s > 0:
                        dve.wait_ge(cgb_done, i)
                        x2i = x2all[:, ds(i * 2 - 2, 2), :]
                        v.tensor_tensor(x2i, x2i, yl[:, ds(i - 1, 1), :, 0, :].rearrange("p i n d -> p (i n) d"),
                                        ALU.add).then_inc(csum_done, 1)
                    if s < LH:
                        dve.wait_ge(cw1_done, i + 1)
                        y01 = yl[:, ds(i, 1), :, 0, :].rearrange("p i n d -> p (i n) d")
                        v.tensor_tensor(y01, y01, modr[:, ds(h * (B // 2) + s // 4, 1), GB, :].to_broadcast([P, 2, D]),
                                        ALU.mult).then_inc(cgb_done, 1)

        @block.gpsimd
        def _(pool):
            gp = nc.gpsimd
            gp.memset(ident[:, :], 0.0).then_inc(ident_done, 1)
            gp.iota(trow[:, :], [[1, T]], base=0, channel_multiplier=0, allow_small_or_imprecise_dtypes=True).then_inc(iota_done, 1)
            gp.iota(tcol[:, :], [[P, TB]], base=1, channel_multiplier=1, allow_small_or_imprecise_dtypes=True).then_inc(isq_done, 1)
            gp.memset(pair_idx[:, :, :], 0)
            gp.memset(xgT_flat[:, :], 0.0).then_inc(zero_set, 1)
            gp.iota(row_hi[:, :], [[2 * P, NT]], base=0, channel_multiplier=0, allow_small_or_imprecise_dtypes=True)
            gp.iota(row_lo[:, :], [[1, 2]], base=1, channel_multiplier=2, allow_small_or_imprecise_dtypes=True)
            gp.iota(row_neg[:, :], [[-1, 2]], base=-1, channel_multiplier=-2, allow_small_or_imprecise_dtypes=True)
            gp.iota(idle_row[:, :], [[P, NBLK]], base=TOPK * N + 1, channel_multiplier=1, allow_small_or_imprecise_dtypes=True)
            pool.wait_ge(ident_done, 1)
            gp.affine_select(out=ident[:, :], in_=ident[:, :], compare_op=ALU.not_equal, fill=1.0, base=0,
                             pattern=[[-1, P]], channel_multiplier=1).then_inc(ident_done, 1)
            pool.wait_ge(pc_chain, 1)
            pool.wait_ge(isq_done, 1)
            gp.tensor_tensor(isq[:, :], tcol[:, :], mhalf[:, :], ALU.pow).then_inc(isq_done, 1)

            def rstd(var, rs, sh, ve, nm, n, done):
                wait(pool, var, n)
                gp.tensor_tensor(rs[:, :], ve[:, :], mhalf[:, 0:Q], ALU.pow).then_inc(done, 1)
                wait(pool, done, 2 * n - 1)
                gp.tensor_tensor(sh[:, :], nm[:, :], rs[:, :], ALU.mult).then_inc(done, 1)

            def modulate_cb(g, b):
                wait(pool, h2n_done, g + 1)
                apart(gp, g)
                gp.tensor_tensor(h2[:, :, :], h2[:, :, :], modr[:, ds(b, 1), CB1, :].to_broadcast([P, Q, D]),
                                 ALU.mult).then_inc(h2c_done, 1)

            def modulate_sb(g, b):
                wait(pool, h2c_done, g + 1)
                apart(gp, g)
                gp.tensor_tensor(h2[:, :, :], h2[:, :, :], modr[:, ds(b, 1), SB_, :].to_broadcast([P, Q, D]),
                                 ALU.add).then_inc(h2_done, 1)

            def gate_heads(g, b):
                wait(pool, wo_read, g + 1)
                gp.tensor_tensor(h2[:, :, :], h2[:, :, :], modr[:, ds(b, 1), GA, :].to_broadcast([P, Q, D]),
                                 ALU.mult).then_inc(gated_done, 1)

            def add_heads(g):
                wait(pool, gated_done, g + 1)
                wait(pool, xr_in, 16 * (g + 1))
                gp.tensor_tensor(xr[:, :, :], xr[:, :, :], h2[:, :, :], ALU.add).then_inc(x2_done, 1)

            def pos_products(u, s, cb, w):
                wait(pool, vcopy_done, u + 1)
                wait(pool, tab_done, w * CB + cb + 1)
                wait(pool, parts_done, u - 1)
                gp.tensor_tensor(prod[:, s, :, :], vg[:, s:s + 1, :].to_broadcast([P, 2, WIN]), tab[:, cb, :, :],
                                 ALU.mult).then_inc(dpos_done, 1)

            def mix(u, s):
                wait(pool, parts_done, u + 1)
                gp.tensor_tensor(parts[:, s, 0, :], parts[:, s, 0, :], parts[:, s, 1, :], ALU.add).then_inc(mixed_done, 1)

            def pos_probe(u, s, cb):
                wait(pool, carry_done, u + 1)
                gp.tensor_tensor(prod[:, s, :, :], prod[:, s, :, :], tab[:, cb, :, :], ALU.mult).then_inc(fpos_done, 1)

            rstd(var1_done, rs1, sh1, ve1, nm1, 1, rstd1_done)

            def body(w, b, wp, bp, wn, bn):
                g = w * B + b
                u0 = g * CB
                for cb in range(CB):
                    u = u0 + cb
                    s = cb % 2
                    lw, lc = (w, cb - 1) if cb else (wp, CB - 1)
                    if (cb - LAG) % CB in POOL_ADDS and (wp is not None or cb >= LAG):
                        mix(u - LAG, s)
                    pos_products(u, s, cb, w)
                    if lw is not None:
                        pos_probe(u - 1, 1 - s, lc)
                    if cb == 1 and wp is not None:
                        gate_heads(g - 1, bp)
                    if cb == 2 and wp is not None:
                        add_heads(g - 1)
                    if cb == 0 and wn is not None:
                        rstd(var1_done, rs1, sh1, ve1, nm1, g + 2, rstd1_done)
                    if cb == 3 and wp is not None:
                        rstd(var2_done, rs2, sh2, ve2, nm2, g, rstd2_done)
                    if cb == 4 and wp is not None:
                        modulate_cb(g - 1, bp)
                    if cb == 5 and wp is not None:
                        modulate_sb(g - 1, bp)

            bodies(pool, body)
            mix(NU - 2, 0)
            pos_probe(NU - 1, (CB - 1) % 2, CB - 1)
            rstd(var2_done, rs2, sh2, ve2, nm2, NG, rstd2_done)

            pool.wait_ge(trig_done, NU)
            gp.iota(iota_p, [[1, P]], base=0, channel_multiplier=0, allow_small_or_imprecise_dtypes=True).then_inc(rt_iota, 1)
            gp.iota(iota_b, [[1, P]], base=0, channel_multiplier=0, allow_small_or_imprecise_dtypes=True)
            gp.iota(e16, [[-1, E]], base=E, channel_multiplier=0, allow_small_or_imprecise_dtypes=True).then_inc(rt_iota, 1)
            gp.memset(onesb, 1.0).then_inc(rt_iota, 1)
            gp.memset(oh_flat[:, 0:2], 0.0)
            pool.wait_ge(tp1_done, KT * NG)
            gp.memset(segm, 1.0).then_inc(segm_set, 1)
            pool.wait_ge(segm_set, 1)
            gp.memset(segm.rearrange("p (c n) -> p c n", n=NT)[:, :, 0:1], 0.0).then_inc(rt_iota, 1)
            pool.wait_ge(rt_iota, 3)
            gp.affine_select(out=triu, in_=onesb, compare_op=ALU.is_gt, fill=0.0, base=0,
                             pattern=[[1, P]], channel_multiplier=-1).then_inc(rt_iota, 1)

            pool.wait_ge(rt_slot, 1)

            def dist_chunk(c, i):
                if not isinstance(i, int):
                    pool.wait_ge(lo_done, i - 1)
                    pool.wait_ge(hi_done, i - 1)
                    gp.tensor_tensor(spare[:, 4 + c:5 + c], one[:, 0:1], one[:, 0:1], ALU.mult)
                gp.tensor_tensor(dist[:, c, :, :, :], iota_p[:, 0:NBLK].unsqueeze(1).unsqueeze(1).to_broadcast([P, 2, 4, NBLK]),
                                 blkf[:, :, ds(i * 4, 4)].unsqueeze(3).to_broadcast([P, 2, 4, NBLK]),
                                 ALU.subtract).then_inc(dist_done, 1)

            dist_chunk(0, 0)
            dist_chunk(1, 1)
            with pool.Fori(1, NT // 8) as i:
                for c in range(2):
                    dist_chunk(c, i * 2 + c)

            pool.wait_ge(map_done, 1)
            pool.wait_ge(h2_out, 16 * NG)
            pool.wait_ge(zero_out, 16 * NG)

            def step(j, s):
                s4 = s % 4
                if not isinstance(j, int) or j >= 4:
                    if there(j - 4):
                        wait(pool, gath[s4], 16 * ((j - 4) // 4) + 16 if isinstance(j, int) else 4 * (j - s4))
                    if there(j - 4 - SLAG):
                        s8 = (s - 4 - SLAG) % R
                        pool.wait_ge(ystor[s8], 16 * ((j - 4 - SLAG) // R) + 16 if isinstance(j, int) else 2 * (j - 4 - SLAG - s8) + 16)
                wait(pool, carried, j)
                gp.tensor_copy(idxc[:, s4, :], pair_idx[:, ds(j, 1), :].rearrange("p a k -> p (a k)")).then_inc(idx_done, 1)
                pool.wait_ge(idx_done, j + 1)
                if there(j):
                    wait(pool, bt_done, j - 3)
                if there(j - SLAG):
                    wait(pool, by_copied, j - SLAG + 1)
                gp.tensor_tensor(spare[:, 4:5], one[:, 0:1], one[:, 0:1], ALU.mult).then_inc(carried, 1)
                if there(j):
                    gp.indirect_dma_start(out=xg[:, s4, :], out_offset=None, in_=h2_d,
                                          in_offset=bass.IndirectOffsetOnAxis(ap=idxc[:, s4, 0:1], axis=0)).then_inc(gath[s4], 16)
                if there(j - SLAG):
                    s8 = (s - SLAG) % R
                    gp.indirect_dma_start(out=y_d, out_offset=bass.IndirectOffsetOnAxis(ap=idxc[:, s4, 1:2], axis=0),
                                          in_=ysb[:, s8, :], in_offset=None).then_inc(ystor[s8], 16)

            pipeline(pool, step, SLAG)


_INS = ['L0_attn_x', 'L0_attn_Wk', 'L0_attn_Wv', 'L0_attn_Wo', 'L0_attn_gate', 'L0_attn_freqs', 'L0_ffn_router_w',
        'L0_ffn_gate_w', 'L0_ffn_up_w', 'L0_ffn_down_w', 'L0_c', 'L0_wmod']
_OUTS = [((4, 1024, 256), 'float32')]


def kernel(**inputs):
    import numpy as _np
    import concourse.bacc as _bacc
    from concourse import mybir as _mybir
    from concourse.bass_utils import run_bass_kernel_spmd as _run

    nc = _bacc.Bacc("TRN2", target_bir_lowering=False, num_devices=1)
    arrays, args = {}, []
    for name in _INS:
        a = _np.ascontiguousarray(inputs[name])
        arrays[f"in_{name}_dram"] = a
        args.append(nc.dram_tensor(f"in_{name}_dram", a.shape, _mybir.dt.from_np(a.dtype), kind="ExternalInput").ap())
    for i, (shape, dtype) in enumerate(_OUTS):
        dt = _mybir.dt.from_np(_np.dtype(dtype))
        args.append(nc.dram_tensor(f"out_{i}_dram", shape, dt, kind="ExternalOutput").ap())
    adaln_block(nc, *args)
    r = _run(nc, [arrays], core_ids=[0])
    return r.results[0]["out_0_dram"]
```
